# Optimizing a Trainium2 kernel written in Bass

```python
import numpy as np
import jax
import jax.numpy as jnp

def _softmax(x, axis=-1):
    return jax.nn.softmax(x, axis=axis)

def _gelu(x):
    return jax.nn.gelu(x, approximate=True)

def _silu(x):
    return jax.nn.silu(x)

def _sigmoid(x):
    return jax.nn.sigmoid(x)

def _layernorm(x, axis=-1, eps=1e-05):
    m = jnp.mean(x, axis=axis, keepdims=True)
    v = jnp.var(x, axis=axis, keepdims=True)
    return (x - m) / jnp.sqrt(v + eps)

def _scatter_add(tgt, idx, src, axis=0):
    return tgt.at[idx].add(src)

def _segment_sum(src, seg, n):
    return jax.ops.segment_sum(src, seg, n)
kernel_name = 'mk_gnn_ffn_d2_gnn_r8_f2176d'

def setup_inputs(seed: int=0):
    np.random.seed(seed)
    _w = jnp.asarray

    def _rec_inputs():
        import jax
        import jax.numpy as jnp
        _gk = jax.random.key(seed)
        x = -0.0003713 + 1 * jax.random.normal(jax.random.fold_in(_gk, 1), (6250, 256), jnp.float32)
        src = jax.random.randint(jax.random.fold_in(_gk, 2), (100000,), 0, 6250, jnp.int32)
        dst = jax.random.randint(jax.random.fold_in(_gk, 3), (100000,), 0, 6250, jnp.int32)
        _o = jnp.argsort(dst, stable=True)
        src = src[_o]
        dst = dst[_o]
        edge_weight = jax.random.uniform(jax.random.fold_in(_gk, 12), (100000,), jnp.float32, 0.0, 0.999998)
        return (x, src, dst, edge_weight)
    x, src, dst, edge_weight = _rec_inputs()

    def _L0_gnn_setup():
        import jax, jax.numpy as jnp
        import numpy as np
        EPS = 1e-05

        def _ln(x, g, b):
            m = jnp.mean(x, axis=-1, keepdims=True)
            v = jnp.var(x, axis=-1, keepdims=True)
            return (x - m) * jax.lax.rsqrt(v + EPS) * g + b
        N, E, D, L = (6250, 100000, 256, 4)
        key = jax.random.key(seed)
        ks = jax.random.split(key, 10)
        node = jax.random.normal(ks[0], (N, D), jnp.float32)
        edge_index = jax.random.randint(ks[1], (2, E), 0, N, dtype=jnp.int32)
        edge_attr = jax.random.uniform(ks[2], (E,), jnp.float32)
        batch_ptr = jnp.array([0, N], dtype=jnp.int32)
        s = 1.0 / np.sqrt(D)
        W_rel = jax.random.uniform(ks[3], (L, D, D), jnp.float32, -s, s)
        b_rel = jnp.zeros((L, D), jnp.float32)
        W_root = jax.random.uniform(ks[4], (L, D, D), jnp.float32, -s, s)
        ln_g = jnp.ones((L, D), jnp.float32)
        ln_b = jnp.zeros((L, D), jnp.float32)
        W1 = jax.random.uniform(ks[5], (D, D), jnp.float32, -s, s)
        b1 = jnp.zeros((D,), jnp.float32)
        mg1 = jnp.ones((D,), jnp.float32)
        mb1 = jnp.zeros((D,), jnp.float32)
        W2 = jax.random.uniform(ks[6], (D, D), jnp.float32, -s, s)
        b2 = jnp.zeros((D,), jnp.float32)
        mg2 = jnp.ones((D,), jnp.float32)
        mb2 = jnp.zeros((D,), jnp.float32)
        return dict(node=node, edge_index=edge_index, edge_attr=edge_attr, batch_ptr=batch_ptr, W_rel=W_rel, b_rel=b_rel, W_root=W_root, ln_g=ln_g, ln_b=ln_b, W1=W1, b1=b1, mg1=mg1, mb1=mb1, W2=W2, b2=b2, mg2=mg2, mb2=mb2)
    _L0_gnn_all = _L0_gnn_setup()
    _L0_gnn_in = {k: v for k, v in _L0_gnn_all.items() if k in ('batch_ptr', 'W_rel', 'b_rel', 'W_root', 'ln_g', 'ln_b', 'W1', 'b1', 'mg1', 'mb1', 'W2', 'b2', 'mg2', 'mb2')}
    del _L0_gnn_all

    def _L0_ffn_setup():
        import jax, jax.numpy as jnp
        import numpy as np
        E, D, H, TOP_K = (6, 256, 256, 2)
        ROUTER_H = D // 2
        key = jax.random.key(seed)
        ks = jax.random.split(key, 12)
        s = 1.0 / np.sqrt(D)
        sh = 1.0 / np.sqrt(H)
        sr = 1.0 / np.sqrt(ROUTER_H)
        return {'features': jax.random.normal(ks[0], (8, 512, D), dtype=jnp.float32), 'router_w1': jax.random.uniform(ks[1], (D, ROUTER_H), jnp.float32, -s, s), 'router_b1': jnp.zeros((ROUTER_H,), jnp.float32), 'router_w2': jax.random.uniform(ks[2], (ROUTER_H, E), jnp.float32, -sr, sr), 'router_b2': jnp.zeros((E,), jnp.float32), 'expert_w1': jax.random.uniform(ks[3], (E, D, H), jnp.float32, -s, s), 'expert_b1': jnp.zeros((E, H), jnp.float32), 'expert_w2': jax.random.uniform(ks[4], (E, H, H), jnp.float32, -sh, sh), 'expert_b2': jnp.zeros((E, H), jnp.float32), 'expert_w3': jax.random.uniform(ks[5], (E, H, D), jnp.float32, -sh, sh), 'expert_b3': jnp.zeros((E, D), jnp.float32)}
    _L0_ffn_all = _L0_ffn_setup()
    _L0_ffn_in = {k: v for k, v in _L0_ffn_all.items() if k in ('router_w1', 'router_b1', 'router_w2', 'router_b2', 'expert_w1', 'expert_b1', 'expert_w2', 'expert_b2', 'expert_w3', 'expert_b3')}
    del _L0_ffn_all

    def _L1_gnn_setup():
        import jax, jax.numpy as jnp
        import numpy as np
        N_NODES = 6250
        N_EDGES = 100000
        IN_DIM = 256
        OUT_DIM = 64
        HEADS = 4
        NEG_SLOPE = 0.2
        key = jax.random.key(seed)
        k1, k2, k3, k4, k5, k6 = jax.random.split(key, 6)
        x = jax.random.normal(k1, (N_NODES, IN_DIM), dtype=jnp.float32)
        edge_index = jax.random.randint(k2, (2, N_EDGES), 0, N_NODES, dtype=jnp.int64)
        scale = 1.0 / np.sqrt(IN_DIM)
        W = jax.random.normal(k3, (IN_DIM, HEADS * OUT_DIM), dtype=jnp.float32) * scale
        att_src = jax.random.normal(k4, (HEADS, OUT_DIM), dtype=jnp.float32) * scale
        att_dst = jax.random.normal(k5, (HEADS, OUT_DIM), dtype=jnp.float32) * scale
        bias = jnp.zeros((HEADS * OUT_DIM,), dtype=jnp.float32)
        return {'x': x, 'edge_index': edge_index, 'W': W, 'att_src': att_src, 'att_dst': att_dst, 'bias': bias}
    _L1_gnn_all = _L1_gnn_setup()
    _L1_gnn_in = {k: v for k, v in _L1_gnn_all.items() if k in ('W', 'att_src', 'att_dst', 'bias')}
    del _L1_gnn_all

    def _L1_ffn_setup():
        import jax, jax.numpy as jnp
        import numpy as np
        NUM_EXPERTS = 8
        TOP_K = 2
        B, S, D = (8, 1024, 256)

        def _moe(tokens, router_w, w1, b1, w2, b2):
            N = tokens.shape[0]
            E = router_w.shape[0]
            logits = tokens.astype(jnp.float32) @ router_w.astype(jnp.float32).T
            probs = jax.nn.softmax(logits, axis=-1)
            rw, re = jax.lax.top_k(probs, TOP_K)
            if TOP_K > 1:
                rw = rw / jnp.maximum(rw.sum(-1, keepdims=True), 1e-12)
            rw = rw.astype(tokens.dtype)
            combine = jnp.zeros((N, E), tokens.dtype).at[jnp.arange(N)[:, None], re].set(rw)
            out = tokens
            for e in range(E):
                h = jax.nn.gelu(tokens @ w1[e] + b1[e], approximate=False)
                y = h @ w2[e] + b2[e]
                out = out + combine[:, e:e + 1] * y
            return out
        key = jax.random.key(seed)
        ks = jax.random.split(key, 4)
        scale = 1.0 / np.sqrt(D).astype(np.float32)
        return {'input_embeddings': jax.random.normal(ks[0], (B, S, D), jnp.float32), 'router_w': jax.random.normal(ks[1], (NUM_EXPERTS, D), jnp.float32) * scale, 'w1': jax.random.normal(ks[2], (NUM_EXPERTS, D, D), jnp.float32) * scale, 'b1': jnp.zeros((NUM_EXPERTS, D), jnp.float32), 'w2': jax.random.normal(ks[3], (NUM_EXPERTS, D, D), jnp.float32) * scale, 'b2': jnp.zeros((NUM_EXPERTS, D), jnp.float32)}
    _L1_ffn_all = _L1_ffn_setup()
    _L1_ffn_in = {k: v for k, v in _L1_ffn_all.items() if k in ('router_w', 'w1', 'b1', 'w2', 'b2')}
    del _L1_ffn_all
    return {'x': x, 'src': src, 'dst': dst, 'edge_weight': edge_weight, 'L0_gnn_batch_ptr': _L0_gnn_in['batch_ptr'], 'L0_gnn_W_rel': _L0_gnn_in['W_rel'], 'L0_gnn_b_rel': _L0_gnn_in['b_rel'], 'L0_gnn_W_root': _L0_gnn_in['W_root'], 'L0_gnn_ln_g': _L0_gnn_in['ln_g'], 'L0_gnn_ln_b': _L0_gnn_in['ln_b'], 'L0_gnn_W1': _L0_gnn_in['W1'], 'L0_gnn_b1': _L0_gnn_in['b1'], 'L0_gnn_mg1': _L0_gnn_in['mg1'], 'L0_gnn_mb1': _L0_gnn_in['mb1'], 'L0_gnn_W2': _L0_gnn_in['W2'], 'L0_gnn_b2': _L0_gnn_in['b2'], 'L0_gnn_mg2': _L0_gnn_in['mg2'], 'L0_gnn_mb2': _L0_gnn_in['mb2'], 'L0_ffn_router_w1': _L0_ffn_in['router_w1'], 'L0_ffn_router_b1': _L0_ffn_in['router_b1'], 'L0_ffn_router_w2': _L0_ffn_in['router_w2'], 'L0_ffn_router_b2': _L0_ffn_in['router_b2'], 'L0_ffn_expert_w1': _L0_ffn_in['expert_w1'], 'L0_ffn_expert_b1': _L0_ffn_in['expert_b1'], 'L0_ffn_expert_w2': _L0_ffn_in['expert_w2'], 'L0_ffn_expert_b2': _L0_ffn_in['expert_b2'], 'L0_ffn_expert_w3': _L0_ffn_in['expert_w3'], 'L0_ffn_expert_b3': _L0_ffn_in['expert_b3'], 'L1_gnn_W': _L1_gnn_in['W'], 'L1_gnn_att_src': _L1_gnn_in['att_src'], 'L1_gnn_att_dst': _L1_gnn_in['att_dst'], 'L1_gnn_bias': _L1_gnn_in['bias'], 'L1_ffn_router_w': _L1_ffn_in['router_w'], 'L1_ffn_w1': _L1_ffn_in['w1'], 'L1_ffn_b1': _L1_ffn_in['b1'], 'L1_ffn_w2': _L1_ffn_in['w2'], 'L1_ffn_b2': _L1_ffn_in['b2']}

def reference(x, src, dst, edge_weight, L0_gnn_batch_ptr, L0_gnn_W_rel, L0_gnn_b_rel, L0_gnn_W_root, L0_gnn_ln_g, L0_gnn_ln_b, L0_gnn_W1, L0_gnn_b1, L0_gnn_mg1, L0_gnn_mb1, L0_gnn_W2, L0_gnn_b2, L0_gnn_mg2, L0_gnn_mb2, L0_ffn_router_w1, L0_ffn_router_b1, L0_ffn_router_w2, L0_ffn_router_b2, L0_ffn_expert_w1, L0_ffn_expert_b1, L0_ffn_expert_w2, L0_ffn_expert_b2, L0_ffn_expert_w3, L0_ffn_expert_b3, L1_gnn_W, L1_gnn_att_src, L1_gnn_att_dst, L1_gnn_bias, L1_ffn_router_w, L1_ffn_w1, L1_ffn_b1, L1_ffn_w2, L1_ffn_b2):
    import jax
    import jax.numpy as jnp

    def _L0_gnn_ref(node, edge_index, edge_attr, batch_ptr, W_rel, b_rel, W_root, ln_g, ln_b, W1, b1, mg1, mb1, W2, b2, mg2, mb2):
        import jax, jax.numpy as jnp
        import numpy as np
        EPS = 1e-05

        def _ln(x, g, b):
            m = jnp.mean(x, axis=-1, keepdims=True)
            v = jnp.var(x, axis=-1, keepdims=True)
            return (x - m) * jax.lax.rsqrt(v + EPS) * g + b
        N = node.shape[0]
        L = W_rel.shape[0]
        src, dst = (edge_index[0], edge_index[1])
        msg = node[src] * edge_attr[:, None]
        deg = jnp.clip(jax.ops.segment_sum(jnp.ones_like(edge_attr), dst, num_segments=N), 1.0)
        agg = jax.ops.segment_sum(msg, dst, num_segments=N) / deg[:, None]

        def conv_layer(i):
            h = agg @ W_rel[i].T + b_rel[i] + node @ W_root[i].T
            return jax.nn.relu(_ln(node + h, ln_g[i], ln_b[i]))
        out = conv_layer(0)
        for i in range(1, L):
            out = out + conv_layer(i)
        h = jax.nn.relu(_ln(out @ W1.T + b1, mg1, mb1))
        h = jax.nn.relu(_ln(h @ W2.T + b2, mg2, mb2))
        return h

    def _L0_ffn_ref(features, router_w1, router_b1, router_w2, router_b2, expert_w1, expert_b1, expert_w2, expert_b2, expert_w3, expert_b3):
        import jax, jax.numpy as jnp
        import numpy as np
        E, D, H, TOP_K = (6, 256, 256, 2)
        ROUTER_H = D // 2
        rh = jax.nn.relu(features @ router_w1 + router_b1)
        expert_logits = jax.nn.softmax(rh @ router_w2 + router_b2, axis=-1)
        top_w, top_i = jax.lax.top_k(expert_logits, TOP_K)
        routing_weights = jax.nn.softmax(top_w, axis=-1)
        h1 = jax.nn.relu(jnp.einsum('bsd,edh->bseh', features, expert_w1) + expert_b1)
        h2 = jax.nn.relu(jnp.einsum('bseh,ehf->bsef', h1, expert_w2) + expert_b2)
        expert_out = jnp.einsum('bsef,efo->bseo', h2, expert_w3) + expert_b3
        sel = jnp.take_along_axis(expert_out, top_i[:, :, :, None], axis=2)
        combined = jnp.sum(sel * routing_weights[..., None], axis=2)
        return combined

    def _L1_gnn_ref(x, edge_index, W, att_src, att_dst, bias):
        import jax, jax.numpy as jnp
        import numpy as np
        N_NODES = 6250
        N_EDGES = 100000
        IN_DIM = 256
        OUT_DIM = 64
        HEADS = 4
        NEG_SLOPE = 0.2
        N = x.shape[0]
        H, C = att_src.shape
        loop = jnp.arange(N, dtype=edge_index.dtype)
        src = jnp.concatenate([edge_index[0], loop])
        dst = jnp.concatenate([edge_index[1], loop])
        h = (x @ W).reshape(N, H, C)
        a_src = jnp.einsum('nhc,hc->nh', h, att_src)
        a_dst = jnp.einsum('nhc,hc->nh', h, att_dst)
        e = jax.nn.leaky_relu(a_src[src] + a_dst[dst], negative_slope=NEG_SLOPE)
        m = jax.ops.segment_max(e, dst, num_segments=N)
        p = jnp.exp(e - m[dst])
        denom = jax.ops.segment_sum(p, dst, num_segments=N)
        alpha = p / (denom[dst] + 1e-16)
        out = jax.ops.segment_sum(alpha[:, :, None] * h[src], dst, num_segments=N)
        out = out.reshape(N, H * C) + bias
        return jax.nn.relu(out)

    def _L1_ffn_ref(input_embeddings, router_w, w1, b1, w2, b2):
        import jax, jax.numpy as jnp
        import numpy as np
        NUM_EXPERTS = 8
        TOP_K = 2
        B, S, D = (8, 1024, 256)

        def _moe(tokens, router_w, w1, b1, w2, b2):
            N = tokens.shape[0]
            E = router_w.shape[0]
            logits = tokens.astype(jnp.float32) @ router_w.astype(jnp.float32).T
            probs = jax.nn.softmax(logits, axis=-1)
            rw, re = jax.lax.top_k(probs, TOP_K)
            if TOP_K > 1:
                rw = rw / jnp.maximum(rw.sum(-1, keepdims=True), 1e-12)
            rw = rw.astype(tokens.dtype)
            combine = jnp.zeros((N, E), tokens.dtype).at[jnp.arange(N)[:, None], re].set(rw)
            out = tokens
            for e in range(E):
                h = jax.nn.gelu(tokens @ w1[e] + b1[e], approximate=False)
                y = h @ w2[e] + b2[e]
                out = out + combine[:, e:e + 1] * y
            return out
        b, s, d = input_embeddings.shape
        tokens = input_embeddings.reshape(b * s, d)
        return _moe(tokens, router_w, w1, b1, w2, b2).reshape(b, s, d)
    edge_index = jnp.stack([src, dst])
    x = x + _L0_gnn_ref(_layernorm(x, axis=-1), edge_index, edge_weight, L0_gnn_batch_ptr, L0_gnn_W_rel, L0_gnn_b_rel, L0_gnn_W_root, L0_gnn_ln_g, L0_gnn_ln_b, L0_gnn_W1, L0_gnn_b1, L0_gnn_mg1, L0_gnn_mb1, L0_gnn_W2, L0_gnn_b2, L0_gnn_mg2, L0_gnn_mb2)
    x = x + _L0_ffn_ref(_layernorm(x, axis=-1)[None], L0_ffn_router_w1, L0_ffn_router_b1, L0_ffn_router_w2, L0_ffn_router_b2, L0_ffn_expert_w1, L0_ffn_expert_b1, L0_ffn_expert_w2, L0_ffn_expert_b2, L0_ffn_expert_w3, L0_ffn_expert_b3)[0]
    x = x + _L1_gnn_ref(_layernorm(x, axis=-1), edge_index, L1_gnn_W, L1_gnn_att_src, L1_gnn_att_dst, L1_gnn_bias)
    x = x + _L1_ffn_ref(_layernorm(x, axis=-1)[None], L1_ffn_router_w, L1_ffn_w1, L1_ffn_b1, L1_ffn_w2, L1_ffn_b2)[0]
    return x

_drawn_inputs = setup_inputs


def setup_inputs(seed=0):
    import zlib

    import numpy as np

    out = dict(_drawn_inputs(seed))
    spreads = {'L0_gnn_b_rel': (0.0, 0.1),
     'L0_gnn_ln_g': (1.0, 0.2),
     'L0_gnn_ln_b': (0.0, 0.1),
     'L0_gnn_b1': (0.0, 0.1),
     'L0_gnn_mg1': (1.0, 0.2),
     'L0_gnn_mb1': (0.0, 0.1),
     'L0_gnn_b2': (0.0, 0.1),
     'L0_gnn_mg2': (1.0, 0.2),
     'L0_gnn_mb2': (0.0, 0.1),
     'L0_ffn_router_b1': (0.0, 0.1),
     'L0_ffn_router_b2': (0.0, 0.1),
     'L0_ffn_expert_b1': (0.0, 0.453),
     'L0_ffn_expert_b2': (0.0, 0.1),
     'L0_ffn_expert_b3': (0.0, 0.1),
     'L1_gnn_bias': (0.0, 0.1),
     'L1_ffn_b1': (0.0, 0.357),
     'L1_ffn_b2': (0.0, 0.1)}
    factors = {'edge_weight': 2.737}
    for name, (base, spread) in spreads.items():
        noise = np.random.default_rng([zlib.crc32(name.encode()), seed]).standard_normal(out[name].shape)
        drawn = base * np.exp(spread * noise) if base else spread * noise
        out[name] = jnp.asarray(drawn.astype(out[name].dtype))
    for name, factor in factors.items():
        out[name] = (out[name] * factor).astype(out[name].dtype)
    return out
```

```python
from contextlib import ExitStack, contextmanager

import concourse.bass as bass
from concourse import mybir

ALU = mybir.AluOpType
ACT = mybir.ActivationFunctionType
AX = mybir.AxisListType.X
F32 = mybir.dt.float32
I32 = mybir.dt.int32
U32 = mybir.dt.uint32

P = 128
N = 6250
E = 100000
D = 256
KD = D // P
NT = -(-N // P)
NP = NT * P
BT = 7
NB = NT // BT
BN = BT * P
HALF = BN // 2
EC = -(-E // P)
EP = EC * P
GE = 2
NG = EP // (GE * P)
U = 4
RING = 2 * U
SPARE = NT
STEPS = -(-(NG + NT - 1) // RING) * RING
SB = -(-STEPS // P)
SW = SB * P
PAD_DST = NP + 10 * P
LAYERS = 4
H, C = 4, 64
W1H = D + H
E0, R0 = 6, 128
E1 = 8
EPS = 1e-5
SLOPE = 0.2
LOW = -1e30
ds = bass.ds


class Arena:

    def __init__(self, nc, stack):
        self.nc, self.stack = nc, stack
        sb = self.sbuf
        self.nodes = sb("nodes", [P, NT, D], F32)
        self.degree = sb("degree", [P, NT])
        self.ident = sb("ident", [P, P], F32)
        self.columns = sb("columns", [P, P], F32)
        self.ones_row = sb("ones_row", [1, P], F32)
        self.ones_col = sb("ones_col", [P, 1], F32)
        self.step_src_dram = nc.dram_tensor("step_src", [P, SW, GE], I32)
        self.step_dst_dram = nc.dram_tensor("step_dst", [P, SW, GE], F32)
        self.step_weight_dram = nc.dram_tensor("step_weight", [P, SW, GE], F32)
        self.step_tile_dram = nc.dram_tensor("step_tile", [1, SW], I32)
        self.normed_dram = nc.dram_tensor("normed", [NP, D], F32)
        self.projected_dram = nc.dram_tensor("projected", [NP, W1H], F32)
        self.logit_dram = nc.dram_tensor("source_logit", [NP, H], F32)
        self.running_dram = nc.dram_tensor("running_max", [EP, H], F32)

    def sbuf(self, name, shape, dtype=F32):
        return self.stack.enter_context(self.nc.sbuf_tensor(name, shape, dtype))

    @contextmanager
    def edge_sums(self, name):
        with self.nc.sbuf_tensor(name, [P, NT + 1, W1H], F32) as self.sums:
            yield

    @contextmanager
    def attention_tables(self):
        sb = self.nc.sbuf_tensor
        with (
            sb("attention", [P, NT + 1, 2 * H], F32) as self.attention,
            sb("best", [P, NT, H], F32) as self.best,
        ):
            yield


class Stage:

    def __init__(self, nc, name):
        self.nc, self.name, self.stack, self.sems = nc, name, ExitStack(), []

    def __enter__(self):
        return self

    def __exit__(self, *error):
        self.stack.__exit__(*error)
        if error[0] is None:
            self.nc.clear_and_free_semaphores(self.sems)
            self.nc.all_engine_barrier()

    def sbuf(self, name, shape, dtype=F32):
        return self.stack.enter_context(self.nc.sbuf_tensor(f"{self.name}_{name}", shape, dtype))

    def psum(self, name, shape, dtype=F32):
        return self.stack.enter_context(self.nc.psum_tensor(f"{self.name}_{name}", shape, dtype))

    def sem(self, name):
        self.sems.append(self.nc.alloc_semaphore(f"{self.name}_{name}"))
        return self.sems[-1]


class Order:

    def __init__(self, eng, sem, base=0):
        self.eng, self.sem, self.base, self.n = eng, sem, base, 0

    def mark(self, ins):
        ins.then_inc(self.sem, 1)
        self.n += 1

    def wait(self):
        self.eng.wait_ge(self.sem, self.base + self.n)

    def wait_apart(self, settled):
        self.wait()
        self.eng.sem_inc(settled, 1)

    def link(self, ins):
        self.mark(ins)
        self.wait()


def make_constants(nc, a):
    with Stage(nc, "const") as st:
        index = st.sbuf("index", [P, P], I32)
        filled = st.sem("filled")
        block = st.stack.enter_context(nc.Block())

        @block.gpsimd
        def _(pool):
            o = Order(pool, filled)
            o.mark(pool.memset(a.ones_row[:, :], 1.0))
            o.mark(pool.memset(a.ones_col[:, :], 1.0))
            o.mark(pool.iota(index[:, :], [[1, P]], base=0, channel_multiplier=0))
            o.link(pool.memset(a.ident[:, :], 0.0))
            o.mark(pool.tensor_copy(a.columns[:, :], index[:, :]))
            o.link(pool.affine_select(out=a.ident[:, :], in_=a.ident[:, :], compare_op=ALU.not_equal, fill=1.0,
                                      base=0, pattern=[[-1, P]], channel_multiplier=1))


def plan_walk(nc, a, src, dst, weight):
    with Stage(nc, "plan") as st:
        last = st.sbuf("last", [1, NG], I32)
        last_tile = st.sbuf("last_tile", [1, NG], I32)
        ends = st.sbuf("ends", [1, NG])
        group_index = st.sbuf("group_index", [1, NG], I32)
        group_number = st.sbuf("group_number", [1, NG])
        ends_all = st.sbuf("ends_all", [P, NG])
        step_index = st.sbuf("step_index", [P, SB], I32)
        step_number = st.sbuf("step_number", [P, SB])
        ended = st.sbuf("ended", [P, SB, NG])
        group = st.sbuf("group", [P, SB])
        group_id = st.sbuf("group_id", [P, SB], I32)
        tile = st.sbuf("tile", [P, SB])
        tile_base = st.sbuf("tile_base", [P, SB])
        ints = st.sbuf("ints", [P, 2, SB, GE * P], I32)
        rows = st.sbuf("rows", [P, 3, SB, GE * P])
        step_src = st.sbuf("step_src", [P, SW, GE], I32)
        step_dst = st.sbuf("step_dst", [P, SW, GE])
        step_weight = st.sbuf("step_weight", [P, SW, GE])
        step_tile = st.sbuf("step_tile", [1, SW], I32)
        tables_ready, tables_stored = st.sem("tables_ready"), st.sem("tables_stored")
        spread = st.psum("spread", [P, NG])
        turned = [st.psum(f"turned{k}", [P, 4, P]) for k in range(2)]
        tile_row = st.psum("tile_row", [1, SW])
        last_in, numbered, own = st.sem("last_in"), st.sem("numbered"), st.sem("own")
        ends_ready, spread_ready, group_ready = st.sem("ends_ready"), st.sem("spread_ready"), st.sem("group_ready")
        rows_in, rows_ready, turned_ready, turned_used = (
            st.sem("rows_in"), st.sem("rows_ready"), st.sem("turned_ready"), st.sem("turned_used"))
        tile_ready, tile_row_ready = st.sem("tile_ready"), st.sem("tile_row_ready")
        block = st.stack.enter_context(nc.Block())
        tables = [src, dst, weight]
        turns = [(t, g) for t in range(3) for g in range(GE)]

        @block.sync
        def _(sp):
            with nc.allow_non_contiguous_dma(reason="one element of each edge group"):
                sp.dma_start(last[:, :], dst[:, GE * P - 1:GE * P].rearrange("g o -> o g")).then_inc(last_in, 16)
            sp.wait_ge(tables_ready, 1)
            sp.wait_ge(turned_used, len(turns))
            for out, table in ((a.step_src_dram, step_src), (a.step_dst_dram, step_dst),
                               (a.step_weight_dram, step_weight), (a.step_tile_dram, step_tile)):
                sp.dma_start(out.ap(), table.ap()).then_inc(tables_stored, 16)
            sp.wait_ge(tables_stored, 16 * 4)

        @block.gpsimd
        def _(pool):
            o = Order(pool, numbered)
            o.mark(pool.iota(group_index[:, :], [[1, NG]], base=0, channel_multiplier=0))
            o.link(pool.iota(step_index[:, :], [[P, SB]], base=0, channel_multiplier=1))
            o.mark(pool.tensor_copy(group_number[:, :], group_index[:, :]))
            o.mark(pool.tensor_copy(step_number[:, :], step_index[:, :]))
            pool.wait_ge(group_ready, 1)
            for t, table in enumerate(tables):
                for k in range(SB):
                    out = ints[:, t, k, :] if t < 2 else rows[:, 2, k, :]
                    pool.indirect_dma_start(
                        out, None, table, bass.IndirectOffsetOnAxis(group_id[:, k:k + 1].bitcast(U32), 0)
                    ).then_inc(rows_in, 16)

        @block.vector
        def _(dve):
            o = Order(dve, own)
            dve.wait_ge(last_in, 16)
            o.link(dve.tensor_scalar(last_tile[:, :], last[:, :], 7, None, ALU.arith_shift_right))
            o.link(dve.tensor_scalar(ends[:, :], last_tile[:, :], float(NT - 1), None, ALU.min))
            dve.wait_ge(numbered, 4)
            dve.tensor_tensor(ends[:, :], ends[:, :], group_number[:, :], ALU.add).then_inc(ends_ready, 1)
            dve.wait_ge(spread_ready, 1)
            o.link(dve.tensor_copy(ends_all[:, :], spread[:, :]))
            for k in range(SB):
                o.mark(dve.tensor_scalar(ended[:, k, :], ends_all[:, :], step_number[:, k:k + 1], None, ALU.is_lt))
            o.wait()
            o.link(dve.tensor_reduce(group[:, :], ended[:, :, :], AX, ALU.add))
            o.link(dve.tensor_scalar(group[:, :], group[:, :], float(NG - 1), None, ALU.min))
            dve.tensor_copy(group_id[:, :], group[:, :]).then_inc(group_ready, 1)
            o.link(dve.tensor_tensor(tile[:, :], step_number[:, :], group[:, :], ALU.subtract))
            o.link(dve.tensor_scalar(tile[:, :], tile[:, :], float(SPARE), None, ALU.min))
            dve.tensor_scalar(tile_base[:, :], tile[:, :], float(P), None, ALU.mult).then_inc(tile_ready, 1)
            dve.wait_ge(tile_ready, 1)
            dve.wait_ge(rows_in, 16 * 3 * SB)
            o.link(dve.tensor_copy(rows[:, 0:2, :, :], ints[:, :, :, :]))
            for k in range(SB):
                dve.tensor_scalar(rows[:, 1, k, :], rows[:, 1, k, :], tile_base[:, k:k + 1], None,
                                  ALU.subtract).then_inc(rows_ready, 1)
            outs = [step_src, step_dst, step_weight]
            for n, (t, g) in enumerate(turns):
                dve.wait_ge(turned_ready, n + 1)
                dve.tensor_copy(outs[t][:, :, g].rearrange("p (k s) -> p k s", k=SB),
                                turned[n % 2][:, 0:SB, :]).then_inc(turned_used, 1)
            dve.wait_ge(tile_row_ready, 1)
            dve.tensor_copy(step_tile[:, :], tile_row[:, :]).then_inc(tables_ready, 1)

        @block.tensor
        def _(pe):
            pe.wait_ge(ends_ready, 1)
            pe.matmul(spread[:, :], a.ones_row[:, :], ends[:, :], start=True, stop=True).then_inc(spread_ready, 1)
            pe.wait_ge(tile_ready, 1)
            for k in range(SB):
                last_mm = pe.matmul(tile_row[:, k * P:(k + 1) * P], tile[:, k:k + 1], a.ident[:, :],
                                    start=True, stop=True)
            last_mm.then_inc(tile_row_ready, 1)
            pe.wait_ge(rows_ready, SB)
            for n, (t, g) in enumerate(turns):
                if n >= 2:
                    pe.wait_ge(turned_used, n - 1)
                for k in range(SB):
                    last_mm = pe.transpose(turned[n % 2][:, k, :], rows[:, t, k, g * P:(g + 1) * P], a.ident[:, :])
                last_mm.then_inc(turned_ready, 1)


def normalize(dve, o, x, stats, moments, scale_ready, var_ready, out, base, n):
    for k in range(n):
        o.mark(dve.bn_stats(stats[:, k, :], x(k)))
    o.wait()
    for k in range(n):
        o.mark(dve.bn_aggr(moments[:, k, 0:2], stats[:, k, :]))
    o.wait()
    o.link(dve.tensor_scalar(moments[:, 0:n, 2], moments[:, 0:n, 1], EPS, None, ALU.add))
    dve.reciprocal(moments[:, 0:n, 2], moments[:, 0:n, 2]).then_inc(var_ready, 1)
    dve.wait_ge(scale_ready, base + 1)
    for k in range(n):
        o.mark(dve.tensor_scalar(out(k), x(k), moments[:, k, 0:1], moments[:, k, 3:4], ALU.subtract, ALU.mult))


def normalize_input(nc, a, x):
    with Stage(nc, "norm") as st:
        raw = [st.sbuf(f"raw{i}", [P, BT, D]) for i in range(2)]
        stats = st.sbuf("stats", [P, BT, 6])
        moments = st.sbuf("moments", [P, BT, 4])
        raw_in = [st.sem(f"raw_in{i}") for i in range(2)]
        own, var_ready, scale_ready, normed, stored = (
            st.sem("own"), st.sem("var_ready"), st.sem("scale_ready"), st.sem("normed"), st.sem("stored"))
        block = st.stack.enter_context(nc.Block())
        rows = x.rearrange("(t p) d -> p t d", p=P)
        out = a.normed_dram.ap().rearrange("(t p) d -> p t d", p=P)

        @block.sync
        def _(sp):
            for b in range(NB):
                if b >= 2:
                    sp.wait_ge(normed, b - 1)
                sp.dma_start(raw[b % 2][:, :, :], rows[:, b * BT:(b + 1) * BT, :]).then_inc(raw_in[b % 2], 16)
            for b in range(NB):
                sp.wait_ge(normed, b + 1)
                sp.dma_start(out[:, b * BT:(b + 1) * BT, :], a.nodes[:, b * BT:(b + 1) * BT, :]).then_inc(stored, 16)
            sp.wait_ge(stored, 16 * NB)

        @block.vector
        def _(dve):
            o = Order(dve, own)
            for b in range(NB):
                dve.wait_ge(raw_in[b % 2], 16 * (b // 2 + 1))
                normalize(dve, o, lambda k: raw[b % 2][:, k, :], stats, moments, scale_ready, var_ready,
                          lambda k: a.nodes[:, b * BT + k, :], b, BT)
                o.wait()
                dve.sem_inc(normed, 1)

        @block.scalar
        def _(act):
            for b in range(NB):
                act.wait_ge(var_ready, b + 1)
                act.activation(moments[:, :, 3], moments[:, :, 2], ACT.Sqrt).then_inc(scale_ready, 1)


class WalkTables:

    def __init__(self, st, a, weights):
        self.a = a
        self.src = st.sbuf("step_src", [P, SW, GE], I32)
        self.dst = st.sbuf("step_dst", [P, SW, GE])
        self.weight = st.sbuf("step_weight", [P, SW, GE]) if weights else None
        self.tile = st.sbuf("step_tile", [1, SW], I32)
        self.loaded = st.sem("tables_loaded")
        self.count = 16 * (4 if weights else 3)

    def load(self, sp):
        pairs = [(self.src, self.a.step_src_dram), (self.dst, self.a.step_dst_dram), (self.tile, self.a.step_tile_dram)]
        if self.weight is not None:
            pairs.append((self.weight, self.a.step_weight_dram))
        for table, stored in pairs:
            sp.dma_start(table.ap(), stored.ap()).then_inc(self.loaded, 16)


def aggregate_messages(nc, a):
    with Stage(nc, "agg") as st:
        tables = WalkTables(st, a, weights=True)
        rows = st.sbuf("rows", [P, RING, GE, D])
        picked = st.sbuf("picked", [P, 2, U * GE], I32)
        hot = st.sbuf("hot", [P, 4, GE, P])
        weighted = st.sbuf("weighted", [P, 4, GE, P])
        part = [st.psum(f"part{i}", [P, D]) for i in range(2)]
        count = [st.psum(f"count{i}", [P, 1]) for i in range(2)]
        rows_in = [st.sem(f"rows_in{i}") for i in range(RING)]
        gathers_begun = st.sem("gathers_begun")
        cleared, picked_ready, hot_ready, weighted_ready, product_ready, sums_added = (
            st.sem("cleared"), st.sem("picked_ready"), st.sem("hot_ready"), st.sem("weighted_ready"),
            st.sem("product_ready"), st.sem("sums_added"))
        block = st.stack.enter_context(nc.Block())
        src_of = tables.src[:, :, :].rearrange("p s g -> p (s g)")

        @block.sync
        def _(sp):
            tables.load(sp)

        @block.gpsimd
        def _(pool):
            pool.memset(a.sums[:, :, :], 0.0).then_inc(cleared, 1)
            pool.wait_ge(tables.loaded, tables.count)

            def gather(half, t, first):
                if not first:
                    pool.wait_ge(product_ready, t * U - U)
                pool.tensor_copy(picked[:, half, :],
                                 src_of[:, ds(t * (U * GE), U * GE)]).then_inc(picked_ready, 1)
                pool.wait_ge(picked_ready, t + 1)
                pool.sem_inc(gathers_begun, 1)
                for u in range(U):
                    for g in range(GE):
                        pool.indirect_dma_start(
                            rows[:, half * U + u, g, :], None, a.normed_dram.ap(),
                            bass.IndirectOffsetOnAxis(picked[:, half, u * GE + g:u * GE + g + 1].bitcast(U32), 0)
                        ).then_inc(rows_in[half * U + u], 16)

            gather(0, 0, True)
            gather(1, 1, True)
            with pool.Fori(2, STEPS // U, 2) as t:
                gather(0, t, False)
                gather(1, t + 1, False)

        @block.vector
        def _(dve):
            dve.wait_ge(cleared, 1)
            dve.wait_ge(tables.loaded, tables.count)

            def one_hot(s, u):
                at = u % 4
                d = tables.dst[:, ds(s, 1), :].rearrange("p o g -> p (o g)")
                w = tables.weight[:, ds(s, 1), :].rearrange("p o g -> p (o g)")
                dve.tensor_tensor(hot[:, at, :, :], a.columns[:, None, :].to_broadcast([P, GE, P]),
                                  d[:, :, None].to_broadcast([P, GE, P]), ALU.is_equal).then_inc(hot_ready, 1)
                dve.wait_ge(hot_ready, s + 1)
                dve.tensor_tensor(weighted[:, at, :, :], hot[:, at, :, :],
                                  w[:, :, None].to_broadcast([P, GE, P]), ALU.mult).then_inc(weighted_ready, 1)

            def add(s, u):
                j = dve.value_load(tables.tile[0:1, ds(s, 1)], min_val=0, max_val=SPARE)
                dve.wait_ge(product_ready, s + 1)
                dve.wait_ge(sums_added, 2 * s)
                total = a.sums[:, ds(j, 1), 0:D].rearrange("p o d -> p (o d)")
                degree = a.sums[:, ds(j, 1), D:D + 1].rearrange("p o d -> p (o d)")
                dve.tensor_tensor(total, total, part[u % 2][:, :], ALU.add).then_inc(sums_added, 1)
                dve.tensor_tensor(degree, degree, count[u % 2][:, :], ALU.add).then_inc(sums_added, 1)

            def steps(t, first):
                for u in range(RING):
                    s = t * RING + u
                    if not (first and u < 4):
                        dve.wait_ge(product_ready, s - 3)
                    one_hot(s, u)
                    if not (first and u < 1):
                        add(s - 1, (u - 1) % RING)

            steps(0, True)
            with dve.Fori(1, STEPS // RING) as t:
                steps(t, False)
            add(STEPS - 1, RING - 1)

        @block.tensor
        def _(pe):
            def steps(t, first):
                for u in range(RING):
                    s = t * RING + u
                    pe.wait_ge(weighted_ready, s + 1)
                    pe.wait_ge(rows_in[u], t * (16 * GE) + 16 * GE)
                    if not (first and u < 2):
                        pe.wait_ge(sums_added, 2 * s - 2)
                    for g in range(GE):
                        pe.matmul(count[u % 2][:, :], hot[:, u % 4, g, :], a.ones_col[:, :],
                                  start=(g == 0), stop=(g == GE - 1))
                    for g in range(GE):
                        last_mm = pe.matmul(part[u % 2][:, :], weighted[:, u % 4, g, :], rows[:, u, g, :],
                                            start=(g == 0), stop=(g == GE - 1))
                    last_mm.then_inc(product_ready, 1)

            steps(0, True)
            with pe.Fori(1, STEPS // RING) as t:
                steps(t, False)


def after(eng, sem, value):
    if not isinstance(value, int) or value > 0:
        eng.wait_ge(sem, value)


def in_pairs(eng, head, first, last, tail, body):
    for j in range(head, first):
        body(j, j % 2)
    with eng.Fori(first, last, 2) as j:
        body(j, first % 2)
        body(j + 1, 1 - first % 2)
    for j in range(last, tail):
        body(j, j % 2)


def convolve(nc, a, x, w):
    FB, FC = 2, 3
    LD = LAYERS * D
    with Stage(nc, "conv") as st:
        w_conv = st.sbuf("w_conv", [P, 2 * KD, LD])
        w_mlp = st.sbuf("w_mlp", [P, 2, KD, D])
        b_conv = st.sbuf("b_conv", [1, LD])
        b_mlp = st.sbuf("b_mlp", [1, 2, D])
        gain = st.sbuf("gain", [P, LAYERS, D])
        shift = st.sbuf("shift", [P, LAYERS, D])
        gain_mlp = st.sbuf("gain_mlp", [P, 2, D])
        shift_mlp = st.sbuf("shift_mlp", [P, 2, D])
        per_degree = st.sbuf("per_degree", [P, NT])
        x_in = st.sbuf("x_in", [P, 2, D])
        staged = st.sbuf("staged", [P, 2, 2 * D])
        lhs = st.sbuf("lhs", [P, 2, 2 * KD, P])
        conv = st.sbuf("conv", [P, 2, LAYERS, D])
        summed = st.sbuf("summed", [P, 2, D])
        lhs_b = st.sbuf("lhs_b", [P, 2, KD, P])
        out_b = st.sbuf("out_b", [P, 2, D])
        act_b = st.sbuf("act_b", [P, 2, D])
        lhs_c = st.sbuf("lhs_c", [P, 2, KD, P])
        out_c = st.sbuf("out_c", [P, 2, D])
        stats = st.sbuf("stats", [P, 3, LAYERS, 6])
        moments = st.sbuf("moments", [P, 3, LAYERS, 4])
        turn = st.psum("turn", [P, 2 * KD, P])
        turn_b = st.psum("turn_b", [P, KD, P])
        turn_c = st.psum("turn_c", [P, KD, P])
        ps_conv = [st.psum(f"ps_conv{i}", [P, 2, D]) for i in range(2)]
        ps_b = st.psum("ps_b", [P, D])
        ps_c = st.psum("ps_c", [P, D])
        weights_in, degrees_ready = st.sem("weights_in"), st.sem("degrees_ready")
        settled, pool_begun = st.sem("settled"), st.sem("pool_begun")
        x_ready = [st.sem(f"x_ready{i}") for i in range(2)]
        staged_ready, turn_ready, lhs_ready, conv_ready, conv_read = (
            st.sem("staged_ready"), st.sem("turn_ready"), st.sem("lhs_ready"), st.sem("conv_ready"), st.sem("conv_read"))
        var, scale = [st.sem(f"var{i}") for i in range(3)], [st.sem(f"scale{i}") for i in range(3)]
        own = [st.sem(f"own{i}") for i in range(3)]
        affine_ready, pool_own, summed_ready = st.sem("affine_ready"), st.sem("pool_own"), st.sem("summed_ready")
        turn_b_ready, lhs_b_ready, b_ready, out_b_ready, act_b_ready = (
            st.sem("turn_b_ready"), st.sem("lhs_b_ready"), st.sem("b_ready"), st.sem("out_b_ready"), st.sem("act_b_ready"))
        turn_c_ready, lhs_c_ready, c_ready, tile_done = (
            st.sem("turn_c_ready"), st.sem("lhs_c_ready"), st.sem("c_ready"), st.sem("tile_done"))
        block = st.stack.enter_context(nc.Block())
        x_rows = x.rearrange("(t p) d -> p t d", p=P)
        PASSES = NT + FC
        NW = 11

        @block.sync
        def _(sp):
            k_rows = lambda t: t.rearrange("(k p) n -> p k n", p=P)
            sp.dma_start(w_conv[:, 0:KD, :], k_rows(w["L0_gnn_W_rel"])).then_inc(weights_in, 16)
            sp.dma_start(w_conv[:, KD:2 * KD, :], k_rows(w["L0_gnn_W_root"])).then_inc(weights_in, 16)
            sp.dma_start(w_mlp[:, 0, :, :], k_rows(w["L0_gnn_W1"])).then_inc(weights_in, 16)
            sp.dma_start(w_mlp[:, 1, :, :], k_rows(w["L0_gnn_W2"])).then_inc(weights_in, 16)
            sp.dma_start(b_conv[:, :], w["L0_gnn_b_rel"]).then_inc(weights_in, 16)
            for i, name in enumerate(("L0_gnn_b1", "L0_gnn_b2")):
                sp.dma_start(b_mlp[:, i, :], w[name]).then_inc(weights_in, 16)
            for out, name in ((gain[:, :, :], "L0_gnn_ln_g"), (shift[:, :, :], "L0_gnn_ln_b")):
                sp.dma_start(out.rearrange("p l d -> p (l d)"), w[name].to_broadcast([P, LD])).then_inc(weights_in, 16)
            for i, (g, b) in enumerate((("L0_gnn_mg1", "L0_gnn_mb1"), ("L0_gnn_mg2", "L0_gnn_mb2"))):
                sp.dma_start(gain_mlp[:, i, :], w[g].to_broadcast([P, D])).then_inc(weights_in, 16)
                sp.dma_start(shift_mlp[:, i, :], w[b].to_broadcast([P, D])).then_inc(weights_in, 16)

            def load(j, par):
                after(sp, tile_done, j - 1)
                sp.dma_start(x_in[:, par, :], x_rows[:, ds(j, 1), :].rearrange("p o d -> p (o d)")
                             ).then_inc(x_ready[par], 16)

            in_pairs(sp, 0, 5, 47, NT, load)

        @block.scalar
        def _(act):
            def stage(j, par):
                after(act, turn_ready, j - 1)
                act.activation(staged[:, par, 0:D], a.sums[:, ds(j, 1), 0:D].rearrange("p o d -> p (o d)"), ACT.Copy,
                               scale=per_degree[:, ds(j, 1)])
                act.activation(staged[:, par, D:2 * D], a.nodes[:, ds(j, 1), :].rearrange("p o d -> p (o d)"), ACT.Copy
                               ).then_inc(staged_ready, 1)

            def root(i, k, n):
                act.wait_ge(var[i], k + 1)
                act.activation(moments[:, i, 0:n, 3], moments[:, i, 0:n, 2], ACT.Sqrt).then_inc(scale[i], 1)

            def tile(j, par):
                runs = lambda back: not isinstance(j, int) or 0 <= j - back < NT
                if runs(0):
                    act.wait_ge(turn_ready, j + 1)
                    after(act, conv_ready, j - 1)
                    act.activation(lhs[:, par, :, :], turn[:, :, :], ACT.Copy).then_inc(lhs_ready, 1)
                if runs(FB):
                    act.wait_ge(turn_b_ready, j - FB + 1)
                    after(act, b_ready, j - FB - 1)
                    act.activation(lhs_b[:, par, :, :], turn_b[:, :, :], ACT.Copy).then_inc(lhs_b_ready, 1)
                if runs(FC):
                    act.wait_ge(turn_c_ready, j - FC + 1)
                    after(act, c_ready, j - FC - 1)
                    act.activation(lhs_c[:, 1 - par, :, :], turn_c[:, :, :], ACT.Copy).then_inc(lhs_c_ready, 1)
                if not isinstance(j, int) or j + 1 < NT:
                    stage(j + 1, 1 - par)
                if runs(FB):
                    root(1, j - FB, 1)
                    act.wait_ge(out_b_ready, j - FB + 1)
                    after(act, turn_c_ready, j - FB - 1)
                    act.activation(act_b[:, par, :], out_b[:, par, :], ACT.Relu).then_inc(act_b_ready, 1)
                if runs(FC):
                    root(2, j - FC, 1)
                if runs(0):
                    root(0, j, LAYERS)

            act.wait_ge(degrees_ready, 2)
            stage(0, 0)
            in_pairs(act, 0, 5, 47, PASSES, tile)

        @block.gpsimd
        def _(pool):
            def tile(j, par):
                pool.wait_ge(affine_ready, j + 1)
                after(pool, turn_b_ready, j - 1)
                pool.sem_inc(pool_begun, 1)
                o = Order(pool, pool_own, j * (2 * LAYERS - 2))
                for i in range(LAYERS):
                    o.mark(pool.tensor_scalar(conv[:, par, i, :], conv[:, par, i, :], 0.0, None, ALU.max))
                for i in range(1, LAYERS):
                    o.wait()
                    so_far = conv[:, par, 0, :] if i == 1 else summed[:, par, :]
                    add = pool.tensor_tensor(summed[:, par, :], so_far, conv[:, par, i, :], ALU.add)
                    if i < LAYERS - 1:
                        o.mark(add)
                add.then_inc(summed_ready, 1)

            in_pairs(pool, 0, 5, 47, NT, tile)

        @block.vector
        def _(dve):
            dve.tensor_scalar(per_degree[:, :], a.sums[:, 0:NT, D], 1.0, None, ALU.max).then_inc(degrees_ready, 1)
            dve.wait_ge(degrees_ready, 1)
            dve.reciprocal(per_degree[:, :], per_degree[:, :]).then_inc(degrees_ready, 1)
            dve.tensor_copy(a.degree[:, :], a.sums[:, 0:NT, D])

            def moments_of(o, i, sources, k):
                for n, s in enumerate(sources):
                    o.mark(dve.bn_stats(stats[:, i, n, :], s))
                o.wait_apart(settled)
                for n in range(len(sources)):
                    o.mark(dve.bn_aggr(moments[:, i, n, 0:2], stats[:, i, n, :]))
                o.wait()
                m = moments[:, i, 0:len(sources), :]
                o.link(dve.tensor_scalar(m[:, :, 2], m[:, :, 1], EPS, None, ALU.add))
                dve.reciprocal(m[:, :, 2], m[:, :, 2]).then_inc(var[i], 1)
                dve.wait_ge(scale[i], k + 1)

            def affine(o, i, n, out, x_, g, b):
                o.link(dve.scalar_tensor_tensor(out=out, in0=x_, scalar=moments[:, i, n, 0:1], in1=g,
                                                op0=ALU.subtract, op1=ALU.mult))
                return dve.scalar_tensor_tensor(out=out, in0=out, scalar=moments[:, i, n, 3:4], in1=b,
                                                op0=ALU.mult, op1=ALU.add)

            def tile(j, par):
                runs = lambda back: not isinstance(j, int) or 0 <= j - back < NT
                if runs(FB):
                    k = j - FB
                    o = Order(dve, own[1], k * 4)
                    dve.wait_ge(b_ready, k + 1)
                    moments_of(o, 1, [ps_b[:, :]], k)
                    after(dve, act_b_ready, k - 1)
                    affine(o, 1, 0, out_b[:, par, :], ps_b[:, :], gain_mlp[:, 0, :], shift_mlp[:, 0, :]
                           ).then_inc(out_b_ready, 1)
                    assert o.n == 4
                if runs(FC):
                    k = j - FC
                    o = Order(dve, own[2], k * 5)
                    dve.wait_ge(c_ready, k + 1)
                    moments_of(o, 2, [ps_c[:, :]], k)
                    o.link(affine(o, 2, 0, out_c[:, 1 - par, :], ps_c[:, :], gain_mlp[:, 1, :], shift_mlp[:, 1, :]))
                    if isinstance(k, int):
                        dve.wait_ge(x_ready[1 - par], 16 * (k // 2 + 1))
                    else:
                        dve.wait_ge(x_ready[1 - par], (k - (1 - par)) * 8 + 16)
                    dve.scalar_tensor_tensor(out=a.nodes[:, ds(k, 1), :].rearrange("p o d -> p (o d)"),
                                             in0=out_c[:, 1 - par, :], scalar=0.0, in1=x_in[:, 1 - par, :],
                                             op0=ALU.max, op1=ALU.add).then_inc(tile_done, 1)
                    assert o.n == 5
                if runs(0):
                    o = Order(dve, own[0], j * 15)
                    dve.wait_ge(conv_ready, j + 1)
                    after(dve, summed_ready, j - 1)
                    for h in range(2):
                        o.mark(dve.tensor_tensor(conv[:, par, 2 * h:2 * h + 2, :], ps_conv[h][:, :, :],
                                                 a.nodes[:, ds(j, 1), :].to_broadcast([P, 2, D]), ALU.add))
                    o.wait()
                    dve.sem_inc(conv_read, 1)
                    moments_of(o, 0, [conv[:, par, i, :] for i in range(LAYERS)], j)
                    for i in range(LAYERS):
                        o.mark(dve.scalar_tensor_tensor(out=conv[:, par, i, :], in0=conv[:, par, i, :],
                                                        scalar=moments[:, 0, i, 0:1], in1=gain[:, i, :],
                                                        op0=ALU.subtract, op1=ALU.mult))
                    o.wait()
                    for i in range(LAYERS):
                        last = dve.scalar_tensor_tensor(out=conv[:, par, i, :], in0=conv[:, par, i, :],
                                                        scalar=moments[:, 0, i, 3:4], in1=shift[:, i, :],
                                                        op0=ALU.mult, op1=ALU.add)
                    last.then_inc(affine_ready, 1)
                    assert o.n == 15, o.n

            dve.wait_ge(degrees_ready, 2)
            dve.wait_ge(weights_in, 16 * 13)
            in_pairs(dve, 0, 5, 47, PASSES, tile)

        @block.tensor
        def _(pe):
            def tile(j, par):
                runs = lambda back: not isinstance(j, int) or 0 <= j - back < NT
                if runs(0):
                    pe.wait_ge(staged_ready, j + 1)
                    after(pe, lhs_ready, j)
                    for k in range(2 * KD):
                        mm = pe.transpose(turn[:, k, :], staged[:, par, k * P:(k + 1) * P], a.ident[:, :])
                    mm.then_inc(turn_ready, 1)
                if runs(FB):
                    pe.wait_ge(summed_ready, j - FB + 1)
                    after(pe, lhs_b_ready, j - FB)
                    for k in range(KD):
                        mm = pe.transpose(turn_b[:, k, :], summed[:, par, k * P:(k + 1) * P], a.ident[:, :])
                    mm.then_inc(turn_b_ready, 1)
                if runs(FC):
                    pe.wait_ge(act_b_ready, j - FC + 1)
                    after(pe, lhs_c_ready, j - FC)
                    for k in range(KD):
                        mm = pe.transpose(turn_c[:, k, :], act_b[:, 1 - par, k * P:(k + 1) * P], a.ident[:, :])
                    mm.then_inc(turn_c_ready, 1)
                for back, i, ready, used, out, left, side, done in (
                        (FB, 0, lhs_b_ready, out_b_ready, ps_b, lhs_b, par, b_ready),
                        (FC, 1, lhs_c_ready, tile_done, ps_c, lhs_c, 1 - par, c_ready)):
                    if runs(back):
                        pe.wait_ge(ready, j - back + 1)
                        after(pe, used, j - back)
                        for k in range(KD):
                            pe.matmul(out[:, :], left[:, side, k, :], w_mlp[:, i, k, :], start=(k == 0), stop=False)
                        pe.matmul(out[:, :], a.ones_row[:, :], b_mlp[:, i, :], start=False, stop=True
                                  ).then_inc(done, 1)
                if runs(0):
                    pe.wait_ge(lhs_ready, j + 1)
                    after(pe, conv_read, j)
                    for h in range(2):
                        half = slice(h * 2 * D, (h + 1) * 2 * D)
                        out = ps_conv[h][:, :, :].rearrange("p l d -> p (l d)")
                        for k in range(2 * KD):
                            pe.matmul(out, lhs[:, par, k, :], w_conv[:, k, half], start=(k == 0), stop=False)
                        mm = pe.matmul(out, a.ones_row[:, :], b_conv[:, half], start=False, stop=True)
                    mm.then_inc(conv_ready, 1)

            pe.wait_ge(weights_in, 16 * 13)
            in_pairs(pe, 0, 5, 47, PASSES, tile)


class Mixture:

    def __init__(self, experts, hidden, func, router_hidden, adds_input, weights, biases, out_bias, router):
        self.experts, self.hidden, self.func, self.router_hidden = experts, hidden, func, router_hidden
        self.adds_input = adds_input
        self.weights, self.biases, self.out_bias, self.router = weights, biases, out_bias, router


HEADS = (4, BT - 4)
SLOTS = 8


def mix(nc, a, name, moe, w, out=None):
    NE, NH = moe.experts, moe.hidden
    NL = NH + 1
    UNITS = [(e, h) for e in range(NE) for h in range(2)]
    NU = len(UNITS)
    F32R = mybir.dt.float32r
    WIDE = HEADS[0] * P
    TILES = {1: (0, 1), 2: (2, 3), 3: (4, 5), 4: (6,)}
    PAIRS = list(TILES.values())
    PARTS = 8
    NEXP = 2 if moe.router_hidden else 1
    OWN_INPUT = BT if moe.adds_input else 0
    OWN_STATS, OWN_ROUTE = 2 * BT + 1, 2 * BT + (13 if moe.router_hidden else 14)
    with Stage(nc, name) as st:
        w_hi = st.sbuf("w_hi", [P, NE, NL, KD, D], F32R)
        w_lo = st.sbuf("w_lo", [P, NE, NL, KD, D], F32R)
        bias = st.sbuf("bias", [P, NH, NE, KD])
        out_bias = st.sbuf("out_bias", [NE, D])
        RW = R0 if moe.router_hidden else SLOTS
        r_raw = st.sbuf("r_raw", [P, KD, RW])
        r_hi = st.sbuf("r_hi", [P, KD, RW], F32R)
        r_lo = st.sbuf("r_lo", [P, KD, RW], F32R)
        f_hi = st.sbuf("f_hi", [P, 2, KD, BN], F32R)
        f_lo = st.sbuf("f_lo", [P, 2, KD, BN], F32R)
        normed = st.sbuf("normed", [P, 2, D])
        full = [st.sbuf(f"full{l}", [P, KD, WIDE]) for l in range(NH)]
        w_raw = full[0][:, :, :].rearrange("p i (k n) -> p i k n", k=KD)
        h_hi = [st.sbuf(f"h_hi{l}", [P, 2, KD, WIDE], F32R) for l in range(NH)]
        h_lo = [st.sbuf(f"h_lo{l}", [P, 2, KD, WIDE], F32R) for l in range(NH)]
        stats = st.sbuf("stats", [P, BT, 6])
        moments = st.sbuf("moments", [P, BT, 4])
        logits = st.sbuf("logits", [P, BT, SLOTS])
        probs = st.sbuf("probs", [P, BT, SLOTS])
        top = st.sbuf("top", [P, BT, SLOTS])
        top_index = st.sbuf("top_index", [P, BT, SLOTS], U32)
        chosen = st.sbuf("chosen", [P, BT, 2])
        share = st.sbuf("share", [P, BT, 2])
        row = st.sbuf("row", [P, BT, 2])
        picks = st.sbuf("picks", [P, BT, SLOTS])
        combine = st.sbuf("combine", [P, 2, BT, SLOTS])
        combine_turned = st.sbuf("combine_turned", [SLOTS, BT, P])
        if moe.router_hidden:
            rh_bias = st.sbuf("rh_bias", [P, 1])
            rh = st.sbuf("rh", [P, WIDE])
            r_out = st.sbuf("r_out", [P, NE])
            r_out_bias = st.sbuf("r_out_bias", [P, NE])
        ps_h = [[st.psum(f"ps_h{l}{m}", [P, WIDE]) for m in range(KD)] for l in range(NH)]
        ps_out = [st.psum(f"ps_out{i}", [P, 2, D]) for i in range(2)]
        ps_turn = st.psum("ps_turn", [P, 2, KD, P])
        turned_tiles = ps_turn[:, :, :, :].rearrange("p i k n -> p (i k) n")
        route_logits = ps_turn[:, 0, 0, 0:BT * SLOTS].rearrange("p (t e) -> p t e", t=BT)
        ps_route = st.psum("ps_route", [P, 512])
        names = ["raw_in", "small_in", "weight_used", "weights_ready", "cleared", "own", "var", "scale", "normed_ready",
                 "turned", "hi_ready", "features_ready", "rh_ready", "rh_read", "half_routed", "exp_in", "exp_out",
                 "combine_ready", "combine_turn", "combine_turned_ready", "bias_product", "bias_added", "pre_own",
                 "out_product", "out_added", "stored", "weight_hi", "settled"]
        s = {n: st.sem(n) for n in names}
        prod = [st.sem(f"prod{l}") for l in range(NH)]
        evac = [st.sem(f"evac{l}") for l in range(NH)]
        split = [st.sem(f"split{l}") for l in range(NH)]
        raw_in = [st.sem(f"raw_in{i}") for i in range(2)]
        block = st.stack.enter_context(nc.Block())
        MATS = [(e, l) for e in range(NE) for l in range(NL)]
        n_small = [0]

        def tiles_of(f, par, t0, n):
            return f[:, par, :, t0 * P:(t0 + n) * P].rearrange("p k (t n) -> p t k n", n=P)

        def out_count(b, u):
            return b * (2 * NU) + 2 * u

        def stream(b, hidden, output, bias_unit, other, before):
            more = not isinstance(b, int) or b + 1 < NB
            for v in range(NU + NH):
                for l in range(NH):
                    if 0 <= v - l < NU:
                        hidden(l, v - l)
                if v == 0:
                    bias_unit(b)
                if v >= NH:
                    output(v - NH)
                if more and v < PARTS:
                    before(b + 1, other, v)

        @block.sync
        def _(sp):
            def small(dst, src):
                sp.dma_start(dst, src).then_inc(s["small_in"], 16)
                n_small[0] += 16

            small(r_raw[:, :, :], moe.router[0].rearrange("(k p) n -> p k n", p=P))
            for l in range(NH):
                small(bias[:, l, :, :], moe.biases[l])
            small(out_bias[:, :], moe.out_bias)
            if moe.router_hidden:
                small(rh_bias[:, :], moe.router[1])
                small(r_out[:, :], moe.router[2])
                small(r_out_bias[:, :], moe.router[3].to_broadcast([P, NE]))
            for n, (e, l) in enumerate(MATS):
                if n >= 2:
                    sp.wait_ge(s["weight_used"], n - 1)
                sp.dma_start(w_raw[:, n % 2, :, :], moe.weights[l][e].rearrange("(k p) n -> p k n", p=P)
                             ).then_inc(raw_in[n % 2], 16)
            if out is not None:
                rows = out.rearrange("(t p) d -> p t d", p=P)

                def store(b, par):
                    sp.wait_ge(s["out_added"], b * (2 * NU) + 2 * NU)
                    sp.dma_start(rows[:, ds(b * BT, BT), :], a.nodes[:, ds(b * BT, BT), :]).then_inc(s["stored"], 16)

                in_pairs(sp, 0, 1, 5, NB, store)
                sp.wait_ge(s["stored"], 16 * NB)

        @block.gpsimd
        def _(pool):
            pool.memset(logits[:, :, :], LOW).then_inc(s["cleared"], 1)

        @block.scalar
        def _(act):
            act.wait_ge(s["small_in"], n_small[0])
            act.activation(r_hi[:, :, :], r_raw[:, :, :], ACT.Copy).then_inc(s["weight_hi"], 1)
            for n, (e, l) in enumerate(MATS):
                act.wait_ge(raw_in[n % 2], 16 * (n // 2 + 1))
                act.activation(w_hi[:, e, l, :, :], w_raw[:, n % 2, :, :], ACT.Copy).then_inc(s["weight_hi"], 1)

            def features(b, par, part):
                t0, n = TILES[part][0], len(TILES[part])
                act.wait_ge(s["turned"], b * len(TILES) + part)
                act.activation(tiles_of(f_hi, par, t0, n), ps_turn[:, 0:n, :, :], ACT.Copy).then_inc(s["hi_ready"], 1)

            def before(b, par, part):
                if part == 0:
                    act.wait_ge(s["var"], b + 1)
                    act.activation(moments[:, :, 3], moments[:, :, 2], ACT.Sqrt).then_inc(s["scale"], 1)
                if part in TILES:
                    features(b, par, part)
                if part == 5 and moe.router_hidden:
                    for h in range(2):
                        c0, n = h * WIDE, HEADS[h] * P
                        act.wait_ge(s["rh_ready"], b * 2 + (h + 1))
                        after(act, s["half_routed"], b * 2 + h)
                        act.activation(rh[:, 0:n], ps_route[:, 0:n], ACT.Relu, bias=rh_bias[:, 0:1]
                                       ).then_inc(s["rh_read"], 1)
                if part == 6:
                    act.wait_ge(s["exp_in"], b * NEXP + 1)
                    act.activation(probs[:, :, :], logits[:, :, :], ACT.Exp).then_inc(s["exp_out"], 1)
                    if NEXP == 2:
                        act.wait_ge(s["exp_in"], b * NEXP + 2)
                        act.activation(share[:, :, 1], row[:, :, 0], ACT.Exp).then_inc(s["exp_out"], 1)
                if part == 7:
                    for h in range(2):
                        act.wait_ge(s["combine_turn"], b * 2 + (h + 1))
                        t0 = h * HEADS[0]
                        act.activation(combine_turned[:, t0:t0 + HEADS[h], :],
                                       turned_tiles[0:SLOTS, 0:HEADS[h], :], ACT.Copy
                                       ).then_inc(s["combine_turned_ready"], 1)

            def hidden(b, l, u):
                e, h = UNITS[u]
                n = HEADS[h] * P
                for m in range(KD):
                    c = b * (2 * NU) + (2 * u + m)
                    act.wait_ge(prod[l], c + 1)
                    if l + 1 < NH:
                        after(act, prod[l + 1], c - m - 2)
                    else:
                        if not isinstance(b, int) or b > 0 or u >= 2:
                            act.wait_ge(s["out_product"], out_count(b, u - 1))
                    after(act, split[l], c - 1)
                    act.activation(h_hi[l][:, u % 2, m, 0:n], ps_h[l][m][:, 0:n], moe.func, bias=bias[:, l, e, m:m + 1])
                    act.activation(full[l][:, m, 0:n], ps_h[l][m][:, 0:n], moe.func, bias=bias[:, l, e, m:m + 1]
                                   ).then_inc(evac[l], 1)

            def body(b, par):
                stream(b, lambda l, u: hidden(b, l, u), lambda u: None, lambda u: None, 1 - par, before)

            for part in range(PARTS):
                before(0, 0, part)
            in_pairs(act, 0, 1, 5, NB, body)

        @block.vector
        def _(dve):
            dve.wait_ge(s["weight_hi"], 1)
            dve.wait_ge(s["small_in"], n_small[0])
            dve.tensor_tensor(r_lo[:, :, :], r_raw[:, :, :], r_hi[:, :, :].bitcast(F32), ALU.subtract
                              ).then_inc(s["weights_ready"], 1)
            for n, (e, l) in enumerate(MATS):
                dve.wait_ge(s["weight_hi"], n + 2)
                dve.wait_ge(raw_in[n % 2], 16 * (n // 2 + 1))
                dve.tensor_tensor(w_lo[:, e, l, :, :], w_raw[:, n % 2, :, :], w_hi[:, e, l, :, :].bitcast(F32),
                                  ALU.subtract).then_inc(s["weight_used"], 1)
            dve.wait_ge(s["cleared"], 1)

            def own_before(part):
                tiles = sum(len(ts) for p, ts in TILES.items() if p < part) if moe.adds_input else 0
                return tiles + (OWN_STATS if part else 0)

            def before(b, par, part):
                o = Order(dve, s["pre_own"], b * (OWN_STATS + OWN_INPUT + OWN_ROUTE) + own_before(part))
                node = lambda t: a.nodes[:, ds(b * BT + t, 1), :].rearrange("p o d -> p (o d)")
                if part == 0:
                    for t in range(BT):
                        o.mark(dve.bn_stats(stats[:, t, :], node(t)))
                    o.wait_apart(s["settled"])
                    for t in range(BT):
                        o.mark(dve.bn_aggr(moments[:, t, 0:2], stats[:, t, :]))
                    o.wait()
                    o.link(dve.tensor_scalar(moments[:, :, 2], moments[:, :, 1], EPS, None, ALU.add))
                    dve.reciprocal(moments[:, :, 2], moments[:, :, 2]).then_inc(s["var"], 1)
                if part in TILES:
                    if part == 1:
                        dve.wait_ge(s["scale"], b + 1)
                    after(dve, s["turned"], b * len(TILES) + part - 1)
                    for t in TILES[part]:
                        last = dve.tensor_scalar(normed[:, t % 2, :], node(t), moments[:, t, 0:1], moments[:, t, 3:4],
                                                 ALU.subtract, ALU.mult)
                    last.then_inc(s["normed_ready"], 1)
                    if moe.adds_input:
                        dve.wait_ge(s["normed_ready"], b * len(TILES) + part)
                        for t in TILES[part]:
                            o.mark(dve.tensor_tensor(node(t), node(t), normed[:, t % 2, :], ALU.add))
                        o.wait()
                if part - 1 in TILES:
                    t0, n = TILES[part - 1][0], len(TILES[part - 1])
                    dve.wait_ge(s["hi_ready"], b * len(TILES) + part - 1)
                    dve.tensor_tensor(tiles_of(f_lo, par, t0, n), ps_turn[:, 0:n, :, :],
                                      tiles_of(f_hi, par, t0, n).bitcast(F32), ALU.subtract
                                      ).then_inc(s["features_ready"], 1)
                if part == 6:
                    got = route_logits[:, :, 0:NE]
                    z = logits[:, :, 0:NE]
                    dve.wait_ge(s["half_routed"], b * 2 + 2)
                    if moe.router_hidden:
                        o.link(dve.tensor_tensor(z, got, r_out_bias[:, None, :].to_broadcast([P, BT, NE]), ALU.add))
                    else:
                        o.link(dve.tensor_copy(z, got))
                    o.link(dve.tensor_reduce(row[:, :, 1], z, AX, ALU.max))
                    dve.tensor_tensor(z, z, row[:, :, 1:2].to_broadcast([P, BT, NE]), ALU.subtract
                                      ).then_inc(s["exp_in"], 1)
                    dve.wait_ge(s["exp_out"], b * NEXP + 1)
                    o.link(dve.tensor_reduce(row[:, :, 1], probs[:, :, :], AX, ALU.add))
                    o.link(dve.reciprocal(row[:, :, 1], row[:, :, 1]))
                    o.mark(dve.tensor_tensor(probs[:, :, :], probs[:, :, :],
                                             row[:, :, 1:2].to_broadcast([P, BT, SLOTS]), ALU.mult))
                    o.wait_apart(s["settled"])
                    for t in range(BT):
                        o.mark(dve.max(top[:, t, :], probs[:, t, :]))
                    o.wait_apart(s["settled"])
                    for t in range(BT):
                        o.mark(dve.max_index(top_index[:, t, :], top[:, t, :], probs[:, t, :]))
                    o.wait()
                    o.mark(dve.tensor_copy(chosen[:, :, :], top_index[:, :, 0:2]))
                    if NEXP == 2:
                        dve.tensor_tensor(row[:, :, 0], top[:, :, 1], top[:, :, 0], ALU.subtract
                                          ).then_inc(s["exp_in"], 1)
                        dve.wait_ge(s["exp_out"], b * NEXP + 2)
                        o.link(dve.tensor_scalar(row[:, :, 1], share[:, :, 1], 1.0, None, ALU.add))
                        o.link(dve.reciprocal(share[:, :, 0], row[:, :, 1]))
                        o.link(dve.tensor_tensor(share[:, :, 1], share[:, :, 1], share[:, :, 0], ALU.mult))
                    else:
                        o.link(dve.tensor_tensor(row[:, :, 0], top[:, :, 0], top[:, :, 1], ALU.add))
                        o.link(dve.tensor_scalar(row[:, :, 0], row[:, :, 0], 1e-12, None, ALU.max))
                        o.link(dve.reciprocal(row[:, :, 1], row[:, :, 0]))
                        o.link(dve.tensor_tensor(share[:, :, :], top[:, :, 0:2],
                                                 row[:, :, 1:2].to_broadcast([P, BT, 2]), ALU.mult))
                    index = a.columns[:, None, 0:SLOTS].to_broadcast([P, BT, SLOTS])
                    wide = lambda x: x.to_broadcast([P, BT, SLOTS])
                    o.mark(dve.tensor_tensor(combine[:, par, :, :], index, wide(chosen[:, :, 0:1]), ALU.is_equal))
                    o.link(dve.tensor_tensor(picks[:, :, :], index, wide(chosen[:, :, 1:2]), ALU.is_equal))
                    o.mark(dve.tensor_tensor(combine[:, par, :, :], combine[:, par, :, :], wide(share[:, :, 0:1]),
                                             ALU.mult))
                    o.link(dve.tensor_tensor(picks[:, :, :], picks[:, :, :], wide(share[:, :, 1:2]), ALU.mult))
                    dve.tensor_tensor(combine[:, par, :, :], combine[:, par, :, :], picks[:, :, :], ALU.add
                                      ).then_inc(s["combine_ready"], 1)
                assert part in TILES or o.n == {0: OWN_STATS, 6: OWN_ROUTE}.get(part, 0), o.n

            def hidden(b, l, u):
                e, h = UNITS[u]
                n = HEADS[h] * P
                for m in range(KD):
                    c = b * (2 * NU) + (2 * u + m)
                    dve.wait_ge(evac[l], c + 1)
                    dve.tensor_tensor(h_lo[l][:, u % 2, m, 0:n], full[l][:, m, 0:n],
                                      h_hi[l][:, u % 2, m, 0:n].bitcast(F32), ALU.subtract).then_inc(split[l], 1)

            def add_bias(b, par):
                for j, tiles in enumerate(PAIRS):
                    dve.wait_ge(s["bias_product"], b * len(PAIRS) + (j + 1))
                    for i, t in enumerate(tiles):
                        x = a.nodes[:, ds(b * BT + t, 1), :].rearrange("p o d -> p (o d)")
                        last = dve.tensor_tensor(x, x, ps_out[j % 2][:, i, :], ALU.add)
                    last.then_inc(s["bias_added"], 1)

            def output(b, par, u):
                e, h = UNITS[u]
                for j in range(2):
                    q = out_count(b, u) + j
                    dve.wait_ge(s["out_product"], q + 1)
                    if u < 2:
                        dve.wait_ge(s["bias_added"], b * len(PAIRS) + (2 * h + j + 1))
                    else:
                        dve.wait_ge(s["out_added"], q - len(PAIRS) + 1)
                    for i, t in enumerate(PAIRS[2 * h + j]):
                        x = a.nodes[:, ds(b * BT + t, 1), :].rearrange("p o d -> p (o d)")
                        last = dve.scalar_tensor_tensor(out=x, in0=ps_out[j][:, i, :],
                                                        scalar=combine[:, par, t, e:e + 1], in1=x,
                                                        op0=ALU.mult, op1=ALU.add)
                    last.then_inc(s["out_added"], 1)

            def body(b, par):
                stream(b, lambda l, u: hidden(b, l, u), lambda u: output(b, par, u),
                       lambda b_: add_bias(b, par), 1 - par, before)

            for part in range(PARTS):
                before(0, 0, part)
            in_pairs(dve, 0, 1, 5, NB, body)

        @block.tensor
        def _(pe):
            pe.wait_ge(s["weights_ready"], 1)

            def triple(out_, pairs, first=True, last=True):
                terms = [(lh, rh_) for lh, ll, rh_, rl in pairs] + [(lh, rl) for lh, ll, rh_, rl in pairs] + [
                    (ll, rh_) for lh, ll, rh_, rl in pairs]
                for i, (x, y) in enumerate(terms):
                    mm = pe.matmul(out_, x, y, start=first and i == 0, stop=last and i == len(terms) - 1)
                return mm

            def before(b, par, part):
                if part in TILES:
                    pe.wait_ge(s["normed_ready"], b * len(TILES) + part)
                    after(pe, s["features_ready"], b * len(TILES) + part - 1)
                    after(pe, s["combine_turned_ready"], b * 2)
                    for i, t in enumerate(TILES[part]):
                        for k in range(KD):
                            mm = pe.transpose(ps_turn[:, i, k, :], normed[:, t % 2, k * P:(k + 1) * P], a.ident[:, :])
                    mm.then_inc(s["turned"], 1)
                if part == 5:
                    pe.wait_ge(s["features_ready"], b * len(TILES) + len(TILES))
                    after(pe, s["combine_ready"], b)
                    if moe.router_hidden:
                        for h in range(2):
                            c0, n = h * WIDE, HEADS[h] * P
                            after(pe, s["rh_read"], b * 2 + h)
                            triple(ps_route[:, 0:n],
                                   [(r_hi[:, k, :], r_lo[:, k, :], f_hi[:, par, k, c0:c0 + n], f_lo[:, par, k, c0:c0 + n])
                                    for k in range(KD)]).then_inc(s["rh_ready"], 1)
                            pe.wait_ge(s["rh_read"], b * 2 + (h + 1))
                            for i in range(HEADS[h]):
                                t = h * HEADS[0] + i
                                mm = pe.matmul(route_logits[:, t, 0:NE], rh[:, i * P:(i + 1) * P], r_out[:, :],
                                               start=True, stop=True)
                            mm.then_inc(s["half_routed"], 1)
                    else:
                        for t in range(BT):
                            c = slice(t * P, (t + 1) * P)
                            mm = triple(route_logits[:, t, :],
                                        [(f_hi[:, par, k, c], f_lo[:, par, k, c], r_hi[:, k, :], r_lo[:, k, :])
                                         for k in range(KD)])
                        mm.then_inc(s["half_routed"], 2)
                if part == 7:
                    pe.wait_ge(s["combine_ready"], b + 1)
                    for h in range(2):
                        after(pe, s["combine_turned_ready"], b * 2 + h)
                        for i in range(HEADS[h]):
                            t = h * HEADS[0] + i
                            mm = pe.transpose(turned_tiles[0:SLOTS, i, :], combine[:, par, t, :], a.ident[:, :])
                        mm.then_inc(s["combine_turn"], 1)

            def hidden(b, par, l, u):
                e, h = UNITS[u]
                c0, n = h * WIDE, HEADS[h] * P
                if l > 0:
                    pe.wait_ge(split[l - 1], b * (2 * NU) + 2 * (u + 1))
                for m in range(KD):
                    c = b * (2 * NU) + (2 * u + m)
                    after(pe, evac[l], c - 1)
                    cols = slice(m * P, (m + 1) * P)
                    x = [(f_hi[:, par, k, c0:c0 + n], f_lo[:, par, k, c0:c0 + n]) if l == 0 else
                         (h_hi[l - 1][:, u % 2, k, 0:n], h_lo[l - 1][:, u % 2, k, 0:n]) for k in range(KD)]
                    triple(ps_h[l][m][:, 0:n],
                           [(w_hi[:, e, l, k, cols], w_lo[:, e, l, k, cols], *x[k]) for k in range(KD)]
                           ).then_inc(prod[l], 1)

            def bias_products(b, par):
                pe.wait_ge(s["combine_turned_ready"], b * 2 + 2)
                for j, tiles in enumerate(PAIRS):
                    if j < 2:
                        after(pe, s["out_added"], b * (2 * NU))
                    else:
                        pe.wait_ge(s["bias_added"], b * len(PAIRS) + j - 1)
                    for i, t in enumerate(tiles):
                        mm = pe.matmul(ps_out[j % 2][:, i, :], combine_turned[0:NE, t, :], out_bias[:, :],
                                       start=True, stop=True)
                    mm.then_inc(s["bias_product"], 1)

            def output(b, par, u):
                e, h = UNITS[u]
                pe.wait_ge(split[NH - 1], b * (2 * NU) + 2 * (u + 1))
                if u == 0:
                    pe.wait_ge(s["bias_added"], b * len(PAIRS) + len(PAIRS))
                for j in range(2):
                    q = out_count(b, u) + j
                    if u > 0:
                        pe.wait_ge(s["out_added"], q - 1)
                    for i, t in enumerate(PAIRS[2 * h + j]):
                        c = slice((2 * j + i) * P, (2 * j + i + 1) * P)
                        mm = triple(ps_out[j][:, i, :],
                                    [(h_hi[NH - 1][:, u % 2, k, c], h_lo[NH - 1][:, u % 2, k, c],
                                      w_hi[:, e, NL - 1, k, :], w_lo[:, e, NL - 1, k, :]) for k in range(KD)])
                    mm.then_inc(s["out_product"], 1)

            def body(b, par):
                stream(b, lambda l, u: hidden(b, par, l, u), lambda u: output(b, par, u),
                       lambda b_: bias_products(b, par), 1 - par, before)

            for part in range(PARTS):
                before(0, 0, part)
            pe.wait_ge(s["weight_used"], len(MATS))
            in_pairs(pe, 0, 1, 5, NB, body)


def project(nc, a, w):
    F32R = mybir.dt.float32r
    PAIRS = [(0, 1), (2, 3), (4, 5), (6,)]
    NPAIR = len(PAIRS)
    with Stage(nc, "proj") as st:
        w_raw = st.sbuf("w_raw", [P, KD, D])
        w_hi = st.sbuf("w_hi", [P, KD, D], F32R)
        w_lo = st.sbuf("w_lo", [P, KD, D], F32R)
        att = st.sbuf("att", [P, 2, D])
        stats = st.sbuf("stats", [P, BT, 6])
        moments = st.sbuf("moments", [P, BT, 4])
        normed = st.sbuf("normed", [P, 2, 2, D])
        f_hi = st.sbuf("f_hi", [P, 2, 2, KD, P], F32R)
        f_lo = st.sbuf("f_lo", [P, 2, 2, KD, P], F32R)
        terms = st.sbuf("terms", [P, 2, 2, 2, D])
        logit = st.sbuf("logit", [P, 2, 2, 2 * H])
        turn = [st.psum(f"turn{i}", [P, 2, KD, P]) for i in range(2)]
        ps_h = [st.psum(f"ps_h{i}", [P, 2, D]) for i in range(2)]
        weights_in, w_hi_ready, w_ready, own, settled = (
            st.sem("weights_in"), st.sem("w_hi_ready"), st.sem("w_ready"), st.sem("own"), st.sem("settled"))
        var, scale, normed_ready, turned, hi_ready, f_ready, h_ready, h_copied, terms_ready, logit_ready, pair_done = (
            st.sem(n) for n in ("var", "scale", "normed_ready", "turned", "hi_ready", "f_ready", "h_ready", "h_copied",
                                "terms_ready", "logit_ready", "pair_done"))
        spare_cleared, stored, pool_begun = st.sem("spare_cleared"), st.sem("stored"), st.sem("pool_begun")
        block = st.stack.enter_context(nc.Block())
        node = lambda b, t: a.nodes[:, ds(b * BT + t, 1), :].rearrange("p o d -> p (o d)")

        def blocks(eng, body):
            with eng.Fori(0, NB) as b:
                body(b)

        @block.sync
        def _(sp):
            sp.dma_start(w_raw[:, :, :], w["L1_gnn_W"].rearrange("(k p) n -> p k n", p=P)).then_inc(weights_in, 16)
            for i, name in enumerate(("L1_gnn_att_src", "L1_gnn_att_dst")):
                sp.dma_start(att[:, i, :], w[name].to_broadcast([P, D])).then_inc(weights_in, 16)
            rows = a.projected_dram.ap().rearrange("(t p) d -> p t d", p=P)
            logits = a.logit_dram.ap().rearrange("(t p) d -> p t d", p=P)

            def store(b):
                sp.wait_ge(pair_done, b * NPAIR + NPAIR)
                sp.dma_start(rows[:, ds(b * BT, BT), :], a.sums[:, ds(b * BT, BT), :]).then_inc(stored, 16)
                with nc.allow_non_contiguous_dma(reason="the heads' logits of each node"):
                    sp.dma_start(logits[:, ds(b * BT, BT), :], a.sums[:, ds(b * BT, BT), D:W1H]).then_inc(stored, 16)

            blocks(sp, store)
            sp.wait_ge(stored, 16 * 2 * NB)

        @block.gpsimd
        def _(pool):
            pool.memset(a.sums[:, SPARE, :], 0.0).then_inc(spare_cleared, 1)
            pool.memset(a.attention[:, :, :], 0.0).then_inc(spare_cleared, 1)

            def tiles(b):
                for j, ts in enumerate(PAIRS):
                    i, n = j % 2, len(ts)
                    pool.wait_ge(h_copied, b * NPAIR + j + 1)
                    if j >= 2:
                        pool.wait_ge(logit_ready, b * NPAIR + j - 1)
                    for k, t in enumerate(ts):
                        h = a.sums[:, ds(b * BT + t, 1), 0:D]
                        last = pool.tensor_tensor(terms[:, i, k, :, :], h.to_broadcast([P, 2, D]), att[:, :, :], ALU.mult)
                    last.then_inc(terms_ready, 1)

            pool.wait_ge(weights_in, 16 * 3)
            blocks(pool, tiles)

        @block.scalar
        def _(act):
            act.wait_ge(weights_in, 16 * 3)
            act.activation(w_hi[:, :, :], w_raw[:, :, :], ACT.Copy).then_inc(w_hi_ready, 1)

            def tiles(b):
                act.wait_ge(var, b + 1)
                act.activation(moments[:, :, 3], moments[:, :, 2], ACT.Sqrt).then_inc(scale, 1)

                def copy_h(j):
                    ts = PAIRS[j]
                    act.wait_ge(h_ready, b * NPAIR + j + 1)
                    act.activation(a.sums[:, ds(b * BT + ts[0], len(ts)), 0:D], ps_h[j % 2][:, 0:len(ts), :], ACT.Copy
                                   ).then_inc(h_copied, 1)

                for j, ts in enumerate(PAIRS):
                    i, n = j % 2, len(ts)
                    act.wait_ge(turned, b * NPAIR + j + 1)
                    if j >= 2:
                        act.wait_ge(h_ready, b * NPAIR + j - 1)
                    act.activation(f_hi[:, i, 0:n, :, :], turn[i][:, 0:n, :, :], ACT.Copy).then_inc(hi_ready, 1)
                    if j:
                        copy_h(j - 1)
                copy_h(NPAIR - 1)

            blocks(act, tiles)

        @block.vector
        def _(dve):
            dve.wait_ge(w_hi_ready, 1)
            dve.tensor_tensor(w_lo[:, :, :], w_raw[:, :, :], w_hi[:, :, :].bitcast(F32), ALU.subtract).then_inc(w_ready, 1)
            dve.wait_ge(spare_cleared, 2)

            def tiles(b):
                o = Order(dve, own, b * (2 * BT + 1 + NPAIR))
                for t in range(BT):
                    o.mark(dve.bn_stats(stats[:, t, :], node(b, t)))
                o.wait_apart(settled)
                for t in range(BT):
                    o.mark(dve.bn_aggr(moments[:, t, 0:2], stats[:, t, :]))
                o.wait()
                o.link(dve.tensor_scalar(moments[:, :, 2], moments[:, :, 1], EPS, None, ALU.add))
                dve.reciprocal(moments[:, :, 2], moments[:, :, 2]).then_inc(var, 1)
                dve.wait_ge(scale, b + 1)

                def norm(j):
                    if j >= 2:
                        dve.wait_ge(turned, b * NPAIR + j - 1)
                    for k, t in enumerate(PAIRS[j]):
                        last = dve.tensor_scalar(normed[:, j % 2, k, :], node(b, t), moments[:, t, 0:1],
                                                 moments[:, t, 3:4], ALU.subtract, ALU.mult)
                    last.then_inc(normed_ready, 1)

                def sum_terms(j):
                    ts = PAIRS[j]
                    i, n = j % 2, len(ts)
                    dve.wait_ge(terms_ready, b * NPAIR + j + 1)
                    o.mark(dve.tensor_reduce(logit[:, i, 0:n, :],
                                             terms[:, i, 0:n, :, :].rearrange("p t a (h c) -> p t (a h) c", c=C), AX,
                                             ALU.add))
                    o.wait()
                    dve.sem_inc(logit_ready, 1)
                    rows = ds(b * BT + ts[0], n)
                    dve.tensor_copy(a.attention[:, rows, 0:H], logit[:, i, 0:n, H:2 * H])
                    dve.tensor_copy(a.sums[:, rows, D:W1H], logit[:, i, 0:n, 0:H]).then_inc(pair_done, 1)

                norm(0)
                norm(1)
                for j, ts in enumerate(PAIRS):
                    i, n = j % 2, len(ts)
                    dve.wait_ge(hi_ready, b * NPAIR + j + 1)
                    dve.tensor_tensor(f_lo[:, i, 0:n, :, :], turn[i][:, 0:n, :, :], f_hi[:, i, 0:n, :, :].bitcast(F32),
                                      ALU.subtract).then_inc(f_ready, 1)
                    if j + 2 < NPAIR:
                        norm(j + 2)
                    if j:
                        sum_terms(j - 1)
                sum_terms(NPAIR - 1)

            blocks(dve, tiles)

        @block.tensor
        def _(pe):
            pe.wait_ge(w_ready, 1)

            def tiles(b):
                def turn_pair(j):
                    pe.wait_ge(normed_ready, b * NPAIR + j + 1)
                    if j >= 2:
                        pe.wait_ge(f_ready, b * NPAIR + j - 1)
                    for k in range(len(PAIRS[j])):
                        for c in range(KD):
                            mm = pe.transpose(turn[j % 2][:, k, c, :], normed[:, j % 2, k, c * P:(c + 1) * P],
                                              a.ident[:, :])
                    mm.then_inc(turned, 1)

                turn_pair(0)
                for j, ts in enumerate(PAIRS):
                    if j + 1 < NPAIR:
                        turn_pair(j + 1)
                    i = j % 2
                    pe.wait_ge(f_ready, b * NPAIR + j + 1)
                    if j >= 2:
                        pe.wait_ge(h_copied, b * NPAIR + j - 1)
                    for k in range(len(ts)):
                        pairs = [(f_hi, w_hi), (f_hi, w_lo), (f_lo, w_hi)]
                        for q, (f, ww) in enumerate(pairs):
                            for c in range(KD):
                                mm = pe.matmul(ps_h[i][:, k, :], f[:, i, k, c, :], ww[:, c, :],
                                               start=(q == 0 and c == 0), stop=(q == 2 and c == KD - 1))
                    mm.then_inc(h_ready, 1)

            blocks(pe, tiles)


def find_maxima(nc, a, src_of_edge, dst_of_edge):
    CH = 23
    NCH = EC // CH
    assert NCH * CH == EC and NCH % 2 == 0
    with Stage(nc, "maxima") as st:
        src = st.sbuf("src", [P, EC + CH], I32)
        dst = st.sbuf("dst", [P, EC], I32)
        before = st.sbuf("before", [P, 1], I32)
        picked = st.sbuf("picked", [P, 2, CH], I32)
        got = st.sbuf("got", [P, 2, CH, H])
        logit = st.sbuf("logit", [P, EC + CH, H])
        running = st.sbuf("running", [P, EC, H])
        dest = st.sbuf("dest", [P, EC])
        dest_before = st.sbuf("dest_before", [P, 1])
        reset = st.sbuf("reset", [P, EC])
        in_first = st.sbuf("in_first", [P, EC])
        flags = st.sbuf("flags", [P, 4])
        tail = st.sbuf("tail", [P, 2, H])
        tail_rows = st.sbuf("tail_rows", [H, 2, P])
        carried = st.sbuf("carried", [H, P + 1])
        carry = st.sbuf("carry", [P, H])
        upto = st.sbuf("upto", [P, P])
        ones = st.sbuf("ones", [P, P])
        ones_nt = st.sbuf("ones_nt", [P, NT])
        before_tile = st.sbuf("before_tile", [P, NT])
        last_edge = st.sbuf("last_edge", [P, NT])
        last_edge_id = st.sbuf("last_edge_id", [P, NT], I32)
        edgeless = st.sbuf("edgeless", [P, NT])
        ps_tail = [st.psum(f"ps_tail{i}", [H, P]) for i in range(2)]
        ps_carry = st.psum("ps_carry", [P, H])
        ps_count = [st.psum(f"ps_count{i}", [P, NT]) for i in range(2)]
        edges_in, own, pool_own, picked_ready, gathers_begun, copied = (
            st.sem(n) for n in ("edges_in", "own", "pool_own", "picked_ready", "gathers_begun", "copied"))
        before_in = st.sem("before_in")
        got_in = [st.sem(f"got_in{i}") for i in range(2)]
        counts_ready, tails_ready, tail_turned, carried_ready, carry_turned, running_ready, running_stored, best_in, \
            last_ready = (st.sem(n) for n in ("counts_ready", "tails_ready", "tail_turned", "carried_ready",
                                              "carry_turned", "running_ready", "running_stored", "best_in", "last_ready"))
        block = st.stack.enter_context(nc.Block())

        @block.sync
        def _(sp):
            sp.dma_start(src[:, 0:EC], src_of_edge).then_inc(edges_in, 16)
            sp.dma_start(dst[:, :], dst_of_edge).then_inc(edges_in, 16)
            sp.wait_ge(pool_own, 1)
            with nc.allow_non_contiguous_dma(reason="the last edge of each partition but one"):
                sp.dma_start(before[1:P, :], dst_of_edge[0:P - 1, EC - 1:EC]).then_inc(before_in, 16)
            sp.wait_ge(running_ready, H)
            sp.dma_start(a.running_dram.ap().rearrange("(p e) h -> p (e h)", p=P),
                         running[:, :, :].rearrange("p e h -> p (e h)")).then_inc(running_stored, 16)

        @block.gpsimd
        def _(pool):
            pool.memset(before[:, :], -1).then_inc(pool_own, 1)
            pool.memset(ones[:, :], 1.0).then_inc(pool_own, 1)
            pool.memset(ones_nt[:, :], 1.0).then_inc(pool_own, 1)
            pool.memset(carried[:, :], LOW).then_inc(pool_own, 1)
            pool.wait_ge(pool_own, 4)
            pool.affine_select(out=upto[:, :], in_=ones[:, :], compare_op=ALU.is_ge, fill=0.0, base=0,
                               pattern=[[1, P]], channel_multiplier=-1).then_inc(pool_own, 1)
            pool.wait_ge(edges_in, 32)

            def gather(half, t, first):
                if not first:
                    pool.wait_ge(copied, t - 1)
                pool.tensor_copy(picked[:, half, :], src[:, ds(t * CH, CH)]).then_inc(picked_ready, 1)
                pool.wait_ge(picked_ready, t + 1)
                pool.sem_inc(gathers_begun, 1)
                for c in range(CH):
                    pool.indirect_dma_start(got[:, half, c, :], None, a.logit_dram.ap(),
                                            bass.IndirectOffsetOnAxis(picked[:, half, c:c + 1].bitcast(U32), 0)
                                            ).then_inc(got_in[half], 16)

            gather(0, 0, True)
            gather(1, 1, True)
            with pool.Fori(2, NCH, 2) as t:
                gather(0, t, False)
                gather(1, t + 1, False)
            pool.wait_ge(last_ready, 1)
            pool.wait_ge(running_stored, 16)
            for t in range(NT):
                pool.indirect_dma_start(a.best[:, t, :], None, a.running_dram.ap(),
                                        bass.IndirectOffsetOnAxis(last_edge_id[:, t:t + 1].bitcast(U32), 0)
                                        ).then_inc(best_in, 16)

        @block.scalar
        def _(act):
            with act.Fori(0, NCH, 2) as t:
                for half in range(2):
                    act.wait_ge(got_in[half], t * (CH * 8) + CH * 16)
                    act.activation(logit[:, ds((t + half) * CH, CH), :], got[:, half, :, :], ACT.Copy).then_inc(copied, 1)

        @block.tensor
        def _(pe):
            pe.wait_ge(pool_own, 5)
            pe.matmul(ps_count[0][:, :], upto[:, :], a.degree[:, :], start=True, stop=True).then_inc(counts_ready, 1)
            pe.matmul(ps_count[1][:, :], ones[:, :], a.degree[:, :], start=True, stop=True).then_inc(counts_ready, 1)
            pe.wait_ge(tails_ready, 1)
            for i in range(2):
                mm = pe.transpose(ps_tail[i][:, :], tail[:, i, :], a.ident[:, :])
            mm.then_inc(tail_turned, 1)
            pe.wait_ge(carried_ready, 1)
            pe.transpose(ps_carry[:, :], carried[:, 0:P], a.ident[0:H, 0:H]).then_inc(carry_turned, 1)

        @block.vector
        def _(dve):
            o = Order(dve, own)
            dve.wait_ge(counts_ready, 2)
            o.link(dve.tensor_copy(last_edge[:, :], ps_count[1][:, :]))
            dve.wait_ge(pool_own, 5)
            o.link(dve.tensor_tensor_scan(before_tile[:, :], ones_nt[:, :], last_edge[:, :], 0.0, ALU.mult, ALU.add))
            o.link(dve.tensor_tensor(before_tile[:, :], before_tile[:, :], last_edge[:, :], ALU.subtract))
            o.link(dve.tensor_tensor(last_edge[:, :], before_tile[:, :], ps_count[0][:, :], ALU.add))
            o.link(dve.tensor_scalar(last_edge[:, :], last_edge[:, :], -1.0, 0.0, ALU.add, ALU.max))
            dve.tensor_copy(last_edge_id[:, :], last_edge[:, :]).then_inc(last_ready, 1)
            o.mark(dve.tensor_scalar(edgeless[:, :], a.degree[:, :], 0.0, LOW, ALU.is_equal, ALU.mult))

            dve.wait_ge(edges_in, 32)
            dve.wait_ge(before_in, 16)
            o.mark(dve.tensor_copy(dest[:, :], dst[:, :]))
            o.link(dve.tensor_copy(dest_before[:, :], before[:, :]))
            o.mark(dve.memset(reset[:, 0:1], LOW))
            o.mark(dve.tensor_tensor(reset[:, 1:EC], dest[:, 1:EC], dest[:, 0:EC - 1], ALU.not_equal))
            o.mark(dve.tensor_scalar(in_first[:, :], dest[:, :], dest[:, 0:1], LOW, ALU.not_equal, ALU.mult))
            o.mark(dve.tensor_tensor(flags[:, 0:1], dest[:, 0:1], dest_before[:, :], ALU.not_equal))
            o.link(dve.tensor_tensor(flags[:, 1:2], dest[:, 0:1], dest[:, EC - 1:EC], ALU.not_equal))
            o.mark(dve.tensor_scalar(reset[:, 1:EC], reset[:, 1:EC], LOW, None, ALU.mult))
            o.mark(dve.tensor_scalar(flags[:, 2:3], flags[:, 0:1], LOW, None, ALU.mult))
            o.link(dve.tensor_tensor(flags[:, 3:4], flags[:, 0:1], flags[:, 1:2], ALU.max))
            o.link(dve.tensor_scalar(tail[:, 1, :], flags[:, 3:4].to_broadcast([P, H]), LOW, None, ALU.mult))

            dve.wait_ge(copied, NCH)
            for h in range(H):
                o.mark(dve.tensor_tensor_scan(running[:, :, h], reset[:, :], logit[:, 0:EC, h], LOW, ALU.add, ALU.max))
            o.wait()
            dve.tensor_copy(tail[:, 0, :], running[:, EC - 1, :]).then_inc(tails_ready, 1)
            dve.wait_ge(tail_turned, 1)
            for i in range(2):
                o.link(dve.tensor_copy(tail_rows[:, i, :], ps_tail[i][:, :]))
            dve.tensor_tensor_scan(carried[:, 1:P + 1], tail_rows[:, 1, :], tail_rows[:, 0, :], LOW, ALU.add, ALU.max
                                   ).then_inc(carried_ready, 1)
            dve.wait_ge(carry_turned, 1)
            o.link(dve.tensor_scalar(carry[:, :], ps_carry[:, :], flags[:, 2:3], None, ALU.add))
            for h in range(H):
                dve.scalar_tensor_tensor(out=running[:, :, h], in0=in_first[:, :], scalar=carry[:, h:h + 1],
                                         in1=running[:, :, h], op0=ALU.add, op1=ALU.max).then_inc(running_ready, 1)
            dve.wait_ge(best_in, 16 * NT)
            o.link(dve.tensor_tensor(a.best[:, :, :], a.best[:, :, :],
                                     edgeless[:, :, None].to_broadcast([P, NT, H]), ALU.add))


def start_softmax(nc, a):
    with Stage(nc, "start") as st:
        z = st.sbuf("z", [P, NT, H])
        own = st.sem("own")
        z_ready, p_ready = st.sem("z_ready"), st.sem("p_ready")
        block = st.stack.enter_context(nc.Block())

        @block.scalar
        def _(act):
            act.wait_ge(z_ready, 1)
            act.activation(a.sums[:, 0:NT, D:W1H], z[:, :, :], ACT.Exp).then_inc(p_ready, 1)

        @block.vector
        def _(dve):
            o = Order(dve, own)
            source = a.sums[:, 0:NT, D:W1H]
            ad, top = a.attention[:, 0:NT, 0:H], a.attention[:, 0:NT, H:2 * H]
            o.link(dve.tensor_tensor(top, a.best[:, :, :], source, ALU.max))
            o.mark(dve.tensor_tensor(top, top, ad, ALU.add))
            o.link(dve.tensor_tensor(z[:, :, :], source, ad, ALU.add))
            o.mark(dve.scalar_tensor_tensor(out=top, in0=top, scalar=SLOPE, in1=top, op0=ALU.mult, op1=ALU.max))
            o.link(dve.scalar_tensor_tensor(out=z[:, :, :], in0=z[:, :, :], scalar=SLOPE, in1=z[:, :, :],
                                            op0=ALU.mult, op1=ALU.max))
            dve.tensor_tensor(z[:, :, :], z[:, :, :], top, ALU.subtract).then_inc(z_ready, 1)
            dve.wait_ge(p_ready, 1)
            for h in range(H):
                x = a.sums[:, 0:NT, h * C:(h + 1) * C]
                o.mark(dve.tensor_tensor(x, x, a.sums[:, 0:NT, D + h:D + h + 1].to_broadcast([P, NT, C]), ALU.mult))
            o.wait()


def attend(nc, a):
    with Stage(nc, "att") as st:
        tables = WalkTables(st, a, weights=False)
        rows = st.sbuf("rows", [P, RING, GE, W1H])
        picked = st.sbuf("picked", [P, 2, U * GE], I32)
        hot = st.sbuf("hot", [P, 4, GE, P])
        hot_turned = st.sbuf("hot_turned", [P, 2, GE, P])
        z = st.sbuf("z", [P, 2, GE, H])
        ps_hot = [st.psum(f"ps_hot{i}", [P, GE, P]) for i in range(2)]
        ps_logit = [st.psum(f"ps_logit{i}", [P, GE, 2 * H]) for i in range(2)]
        part = [st.psum(f"part{i}", [P, W1H]) for i in range(2)]
        rows_in = [st.sem(f"rows_in{i}") for i in range(RING)]
        picked_ready, gathers_begun, hot_ready, turned, turned_copied, logit_ready, own, z_ready, p_ready, weighted, \
            product_ready, added = (st.sem(n) for n in (
                "picked_ready", "gathers_begun", "hot_ready", "turned", "turned_copied", "logit_ready", "own",
                "z_ready", "p_ready", "weighted", "product_ready", "added"))
        block = st.stack.enter_context(nc.Block())
        src_of = tables.src[:, :, :].rearrange("p s g -> p (s g)")

        def steps(eng, lags, after_last):
            end = max(lags)

            def run(i, u, stages):
                for lag, stage in zip(lags, stages):
                    if isinstance(i, int) and not 0 <= i - lag < STEPS:
                        continue
                    stage(i - lag, (u - lag) % RING)

            for u in range(RING):
                run(u, u, after_last)
            with eng.Fori(1, STEPS // RING) as t:
                for u in range(RING):
                    run(t * RING + u, u, after_last)
            for u in range(end):
                run(STEPS + u, u, after_last)

        def landed(eng, s, u):
            if isinstance(s, int):
                eng.wait_ge(rows_in[u], 16 * GE * (s // RING + 1))
            else:
                eng.wait_ge(rows_in[u], (s - u) * (16 * GE // RING) + 16 * GE)

        @block.sync
        def _(sp):
            tables.load(sp)

        @block.gpsimd
        def _(pool):
            pool.wait_ge(tables.loaded, tables.count)

            def gather(half, t, first):
                if not first:
                    pool.wait_ge(product_ready, t * U - U)
                pool.tensor_copy(picked[:, half, :],
                                 src_of[:, ds(t * (U * GE), U * GE)]).then_inc(picked_ready, 1)
                pool.wait_ge(picked_ready, t + 1)
                pool.sem_inc(gathers_begun, 1)
                for u in range(U):
                    for g in range(GE):
                        pool.indirect_dma_start(
                            rows[:, half * U + u, g, :], None, a.projected_dram.ap(),
                            bass.IndirectOffsetOnAxis(picked[:, half, u * GE + g:u * GE + g + 1].bitcast(U32), 0)
                        ).then_inc(rows_in[half * U + u], 16)

            gather(0, 0, True)
            gather(1, 1, True)
            with pool.Fori(2, STEPS // U, 2) as t:
                gather(0, t, False)
                gather(1, t + 1, False)

        @block.scalar
        def _(act):
            def copy_turned(s, u):
                act.wait_ge(turned, s + 1)
                after(act, logit_ready, s - 1)
                act.activation(hot_turned[:, u % 2, :, :], ps_hot[u % 2][:, :, :], ACT.Copy).then_inc(turned_copied, 1)

            def exponent(s, u):
                act.wait_ge(z_ready, s + 1)
                act.activation(rows[:, u, :, D:W1H], z[:, u % 2, :, :], ACT.Exp).then_inc(p_ready, 1)

            steps(act, (0, 1), (copy_turned, exponent))

        @block.vector
        def _(dve):
            def one_hot(s, u):
                after(dve, product_ready, s - 3)
                d = tables.dst[:, ds(s, 1), :].rearrange("p o g -> p (o g)")
                dve.tensor_tensor(hot[:, u % 4, :, :], a.columns[:, None, :].to_broadcast([P, GE, P]),
                                  d[:, :, None].to_broadcast([P, GE, P]), ALU.is_equal).then_inc(hot_ready, 1)

            def logits(s, u):
                o = Order(dve, own, s * 2)
                dve.wait_ge(logit_ready, s + 1)
                landed(dve, s, u)
                zz = z[:, u % 2, :, :]
                got = ps_logit[u % 2]
                o.link(dve.tensor_tensor(zz, rows[:, u, :, D:W1H], got[:, :, 0:H], ALU.add))
                o.link(dve.scalar_tensor_tensor(out=zz, in0=zz, scalar=SLOPE, in1=zz, op0=ALU.mult, op1=ALU.max))
                dve.tensor_tensor(zz, zz, got[:, :, H:2 * H], ALU.subtract).then_inc(z_ready, 1)

            def weigh(s, u):
                dve.wait_ge(p_ready, s + 1)
                x = rows[:, u, :, 0:D].rearrange("p g (h c) -> p g h c", c=C)
                p = rows[:, u, :, D:W1H]
                dve.tensor_tensor(x, x, p[:, :, :, None].to_broadcast([P, GE, H, C]), ALU.mult).then_inc(weighted, 1)

            def add(s, u):
                j = dve.value_load(tables.tile[0:1, ds(s, 1)], min_val=0, max_val=SPARE)
                dve.wait_ge(product_ready, s + 1)
                after(dve, added, s)
                total = a.sums[:, ds(j, 1), :].rearrange("p o d -> p (o d)")
                dve.tensor_tensor(total, total, part[u % 2][:, :], ALU.add).then_inc(added, 1)

            dve.wait_ge(tables.loaded, tables.count)
            steps(dve, (0, 1, 2, 3), (one_hot, logits, weigh, add))

        @block.tensor
        def _(pe):
            def spread(s, u):
                j = pe.value_load(tables.tile[0:1, ds(s, 1)], min_val=0, max_val=SPARE)
                pe.wait_ge(turned_copied, s + 1)
                after(pe, z_ready, s - 1)
                for g in range(GE):
                    mm = pe.matmul(ps_logit[u % 2][:, g, :], hot_turned[:, u % 2, g, :],
                                   a.attention[:, ds(j, 1), :].rearrange("p o d -> p (o d)"), start=True, stop=True)
                mm.then_inc(logit_ready, 1)

            def turn(s, u):
                pe.wait_ge(hot_ready, s + 1)
                after(pe, turned_copied, s - 1)
                for g in range(GE):
                    mm = pe.transpose(ps_hot[u % 2][:, g, :], hot[:, u % 4, g, :], a.ident[:, :])
                mm.then_inc(turned, 1)

            def product(s, u):
                pe.wait_ge(weighted, s + 1)
                after(pe, added, s - 1)
                for g in range(GE):
                    mm = pe.matmul(part[u % 2][:, :], hot[:, u % 4, g, :], rows[:, u, g, :],
                                   start=(g == 0), stop=(g == GE - 1))
                mm.then_inc(product_ready, 1)

            pe.wait_ge(tables.loaded, tables.count)
            steps(pe, (1, 0, 2), (spread, turn, product))


def finish_attention(nc, a, w):
    with Stage(nc, "fin") as st:
        bias = st.sbuf("bias", [P, D])
        share = st.sbuf("share", [P, NT, H])
        own, bias_in = st.sem("own"), st.sem("bias_in")
        block = st.stack.enter_context(nc.Block())

        @block.sync
        def _(sp):
            sp.dma_start(bias[:, :], w["L1_gnn_bias"].to_broadcast([P, D])).then_inc(bias_in, 16)

        @block.vector
        def _(dve):
            o = Order(dve, own)
            o.link(dve.tensor_scalar(share[:, :, :], a.sums[:, 0:NT, D:W1H], 1e-16, None, ALU.add))
            o.link(dve.reciprocal(share[:, :, :], share[:, :, :]))
            dve.wait_ge(bias_in, 16)
            for h in range(H):
                x = a.sums[:, 0:NT, h * C:(h + 1) * C]
                o.mark(dve.tensor_tensor(x, x, share[:, :, h:h + 1].to_broadcast([P, NT, C]), ALU.mult))
            o.wait()
            x = a.sums[:, 0:NT, 0:D]
            o.link(dve.tensor_tensor(x, x, bias[:, None, :].to_broadcast([P, NT, D]), ALU.add))
            o.link(dve.scalar_tensor_tensor(out=a.nodes[:, :, :], in0=x, scalar=0.0, in1=a.nodes[:, :, :],
                                            op0=ALU.max, op1=ALU.add))


def first_mixture(w):
    n = "L0_ffn_"
    return Mixture(E0, 2, ACT.Relu, True, False, [w[n + "expert_w1"], w[n + "expert_w2"], w[n + "expert_w3"]],
                   [w[n + "expert_b1"], w[n + "expert_b2"]], w[n + "expert_b3"],
                   [w[n + "router_w1"], w[n + "router_b1"], w[n + "router_w2"], w[n + "router_b2"]])


def second_mixture(w):
    n = "L1_ffn_"
    return Mixture(E1, 1, ACT.Gelu, False, True, [w[n + "w1"], w[n + "w2"]], [w[n + "b1"]], w[n + "b2"],
                   [w[n + "router_w"]])




def program(nc, aps):
    with ExitStack() as stack:
        a = Arena(nc, stack)
        make_constants(nc, a)
        plan_walk(nc, a, aps["src"], aps["dst"], aps["edge_weight"])
        with a.edge_sums("sums"):
            normalize_input(nc, a, aps["x"])
            aggregate_messages(nc, a)
            convolve(nc, a, aps["x"], aps)
        mix(nc, a, "mix0", first_mixture(aps), aps)
        with a.edge_sums("attention_sums"), a.attention_tables():
            project(nc, a, aps)
            find_maxima(nc, a, aps["src_of_edge"], aps["dst_of_edge"])
            start_softmax(nc, a)
            attend(nc, a)
            finish_attention(nc, a, aps)
        mix(nc, a, "mix1", second_mixture(aps), aps, out=aps["out"])


def lay_out(inputs):
    import numpy as np

    more_edges, more_nodes = EP - E, NP - N
    edges = {
        "src": np.pad(inputs["src"], (0, more_edges)),
        "dst": np.pad(inputs["dst"], (0, more_edges), constant_values=PAD_DST),
        "edge_weight": np.pad(inputs["edge_weight"], (0, more_edges)),
    }
    out = {name: x.reshape(NG, GE * P) for name, x in edges.items()}
    out["src_of_edge"] = edges["src"].reshape(P, EC)
    out["dst_of_edge"] = edges["dst"].reshape(P, EC)
    out["x"] = np.pad(inputs["x"], ((0, more_nodes), (0, 0)))
    for name in ("L0_gnn_W_rel", "L0_gnn_W_root"):
        out[name] = inputs[name].transpose(2, 0, 1).reshape(D, LAYERS * D)
    for name in ("L0_gnn_W1", "L0_gnn_W2", "L1_ffn_router_w"):
        out[name] = inputs[name].T
    for name in ("L0_gnn_b_rel", "L0_gnn_ln_g", "L0_gnn_ln_b", "L0_gnn_b1", "L0_gnn_mg1", "L0_gnn_mb1", "L0_gnn_b2",
                 "L0_gnn_mg2", "L0_gnn_mb2", "L0_ffn_router_b2", "L1_gnn_att_src", "L1_gnn_att_dst", "L1_gnn_bias"):
        out[name] = inputs[name].reshape(1, -1)
    out["L0_ffn_router_b1"] = inputs["L0_ffn_router_b1"].reshape(-1, 1)
    for name in ("L0_ffn_expert_b1", "L0_ffn_expert_b2", "L1_ffn_b1"):
        out[name] = inputs[name].reshape(-1, KD, P).transpose(2, 0, 1)
    for name in ("L0_ffn_router_w1", "L0_ffn_router_w2", "L0_ffn_expert_w1", "L0_ffn_expert_w2", "L0_ffn_expert_w3",
                 "L0_ffn_expert_b3", "L1_gnn_W", "L1_ffn_w1", "L1_ffn_w2", "L1_ffn_b2"):
        out[name] = inputs[name]
    return {name: np.ascontiguousarray(x) for name, x in out.items()}


def kernel(**inputs):
    import concourse.bacc as bacc
    import numpy as np
    from concourse.bass_utils import run_bass_kernel_spmd

    nc = bacc.Bacc("TRN2", target_bir_lowering=False, num_devices=1)
    arrays = lay_out({name: np.asarray(x) for name, x in inputs.items()})
    aps = {name: nc.dram_tensor(name, x.shape, mybir.dt.from_np(x.dtype), kind="ExternalInput").ap()
           for name, x in arrays.items()}
    aps["out"] = nc.dram_tensor("out", (NP, D), F32, kind="ExternalOutput").ap()
    program(nc, aps)
    result = run_bass_kernel_spmd(nc, [arrays], core_ids=[0])
    return result.results[0]["out"][:N]
```

```python
from contextlib import ExitStack, contextmanager

import concourse.bass as bass
from concourse import mybir

ALU = mybir.AluOpType
ACT = mybir.ActivationFunctionType
AX = mybir.AxisListType.X
F32 = mybir.dt.float32
I32 = mybir.dt.int32
U32 = mybir.dt.uint32

P = 128
N = 6250
E = 100000
D = 256
KD = D // P
NT = -(-N // P)
NP = NT * P
BT = 7
NB = NT // BT
BN = BT * P
HALF = BN // 2
EC = -(-E // P)
EP = EC * P
GE = 2
NG = EP // (GE * P)
U = 4
RING = 2 * U
SPARE = NT
STEPS = -(-(NG + NT - 1) // RING) * RING
SB = -(-STEPS // P)
SW = SB * P
PAD_DST = NP + 10 * P
LAYERS = 4
H, C = 4, 64
W1H = D + H
E0, R0 = 6, 128
E1 = 8
EPS = 1e-5
SLOPE = 0.2
LOW = -1e30
ds = bass.ds


class Arena:

    def __init__(self, nc, stack):
        self.nc, self.stack = nc, stack
        sb = self.sbuf
        self.nodes = sb("nodes", [P, NT, D], F32)
        self.degree = sb("degree", [P, NT])
        self.ident = sb("ident", [P, P], F32)
        self.columns = sb("columns", [P, P], F32)
        self.ones_row = sb("ones_row", [1, P], F32)
        self.ones_col = sb("ones_col", [P, 1], F32)
        self.step_src_dram = nc.dram_tensor("step_src", [P, SW, GE], I32)
        self.step_dst_dram = nc.dram_tensor("step_dst", [P, SW, GE], F32)
        self.step_weight_dram = nc.dram_tensor("step_weight", [P, SW, GE], F32)
        self.step_tile_dram = nc.dram_tensor("step_tile", [1, SW], I32)
        self.normed_dram = nc.dram_tensor("normed", [NP, D], F32)
        self.projected_dram = nc.dram_tensor("projected", [NP, W1H], F32)
        self.logit_dram = nc.dram_tensor("source_logit", [NP, H], F32)
        self.running_dram = nc.dram_tensor("running_max", [EP, H], F32)

    def sbuf(self, name, shape, dtype=F32):
        return self.stack.enter_context(self.nc.sbuf_tensor(name, shape, dtype))

    @contextmanager
    def edge_sums(self, name):
        with self.nc.sbuf_tensor(name, [P, NT + 1, W1H], F32) as self.sums:
            yield

    @contextmanager
    def attention_tables(self):
        sb = self.nc.sbuf_tensor
        with (
            sb("attention", [P, NT + 1, 2 * H], F32) as self.attention,
            sb("best", [P, NT, H], F32) as self.best,
        ):
            yield


class Stage:

    def __init__(self, nc, name):
        self.nc, self.name, self.stack, self.sems = nc, name, ExitStack(), []

    def __enter__(self):
        return self

    def __exit__(self, *error):
        self.stack.__exit__(*error)
        if error[0] is None:
            self.nc.clear_and_free_semaphores(self.sems)
            self.nc.all_engine_barrier()

    def sbuf(self, name, shape, dtype=F32):
        return self.stack.enter_context(self.nc.sbuf_tensor(f"{self.name}_{name}", shape, dtype))

    def psum(self, name, shape, dtype=F32):
        return self.stack.enter_context(self.nc.psum_tensor(f"{self.name}_{name}", shape, dtype))

    def sem(self, name):
        self.sems.append(self.nc.alloc_semaphore(f"{self.name}_{name}"))
        return self.sems[-1]


class Order:

    def __init__(self, eng, sem, base=0):
        self.eng, self.sem, self.base, self.n = eng, sem, base, 0

    def mark(self, ins):
        ins.then_inc(self.sem, 1)
        self.n += 1

    def wait(self):
        self.eng.wait_ge(self.sem, self.base + self.n)

    def wait_apart(self, settled):
        self.wait()
        self.eng.sem_inc(settled, 1)

    def link(self, ins):
        self.mark(ins)
        self.wait()


def make_constants(nc, a):
    with Stage(nc, "const") as st:
        index = st.sbuf("index", [P, P], I32)
        filled = st.sem("filled")
        block = st.stack.enter_context(nc.Block())

        @block.gpsimd
        def _(pool):
            o = Order(pool, filled)
            o.mark(pool.memset(a.ones_row[:, :], 1.0))
            o.mark(pool.memset(a.ones_col[:, :], 1.0))
            o.mark(pool.iota(index[:, :], [[1, P]], base=0, channel_multiplier=0))
            o.link(pool.memset(a.ident[:, :], 0.0))
            o.mark(pool.tensor_copy(a.columns[:, :], index[:, :]))
            o.link(pool.affine_select(out=a.ident[:, :], in_=a.ident[:, :], compare_op=ALU.not_equal, fill=1.0,
                                      base=0, pattern=[[-1, P]], channel_multiplier=1))


def plan_walk(nc, a, src, dst, weight):
    with Stage(nc, "plan") as st:
        last = st.sbuf("last", [1, NG], I32)
        last_tile = st.sbuf("last_tile", [1, NG], I32)
        ends = st.sbuf("ends", [1, NG])
        group_index = st.sbuf("group_index", [1, NG], I32)
        group_number = st.sbuf("group_number", [1, NG])
        ends_all = st.sbuf("ends_all", [P, NG])
        step_index = st.sbuf("step_index", [P, SB], I32)
        step_number = st.sbuf("step_number", [P, SB])
        ended = st.sbuf("ended", [P, SB, NG])
        group = st.sbuf("group", [P, SB])
        group_id = st.sbuf("group_id", [P, SB], I32)
        tile = st.sbuf("tile", [P, SB])
        tile_base = st.sbuf("tile_base", [P, SB])
        ints = st.sbuf("ints", [P, 2, SB, GE * P], I32)
        rows = st.sbuf("rows", [P, 3, SB, GE * P])
        step_src = st.sbuf("step_src", [P, SW, GE], I32)
        step_dst = st.sbuf("step_dst", [P, SW, GE])
        step_weight = st.sbuf("step_weight", [P, SW, GE])
        step_tile = st.sbuf("step_tile", [1, SW], I32)
        tables_ready, tables_stored = st.sem("tables_ready"), st.sem("tables_stored")
        spread = st.psum("spread", [P, NG])
        turned = [st.psum(f"turned{k}", [P, 4, P]) for k in range(2)]
        tile_row = st.psum("tile_row", [1, SW])
        last_in, numbered, own = st.sem("last_in"), st.sem("numbered"), st.sem("own")
        ends_ready, spread_ready, group_ready = st.sem("ends_ready"), st.sem("spread_ready"), st.sem("group_ready")
        rows_in, rows_ready, turned_ready, turned_used = (
            st.sem("rows_in"), st.sem("rows_ready"), st.sem("turned_ready"), st.sem("turned_used"))
        tile_ready, tile_row_ready = st.sem("tile_ready"), st.sem("tile_row_ready")
        block = st.stack.enter_context(nc.Block())
        tables = [src, dst, weight]
        turns = [(t, g) for t in range(3) for g in range(GE)]

        @block.sync
        def _(sp):
            with nc.allow_non_contiguous_dma(reason="one element of each edge group"):
                sp.dma_start(last[:, :], dst[:, GE * P - 1:GE * P].rearrange("g o -> o g")).then_inc(last_in, 16)
            sp.wait_ge(tables_ready, 1)
            sp.wait_ge(turned_used, len(turns))
            for out, table in ((a.step_src_dram, step_src), (a.step_dst_dram, step_dst),
                               (a.step_weight_dram, step_weight), (a.step_tile_dram, step_tile)):
                sp.dma_start(out.ap(), table.ap()).then_inc(tables_stored, 16)
            sp.wait_ge(tables_stored, 16 * 4)

        @block.gpsimd
        def _(pool):
            o = Order(pool, numbered)
            o.mark(pool.iota(group_index[:, :], [[1, NG]], base=0, channel_multiplier=0))
            o.link(pool.iota(step_index[:, :], [[P, SB]], base=0, channel_multiplier=1))
            o.mark(pool.tensor_copy(group_number[:, :], group_index[:, :]))
            o.mark(pool.tensor_copy(step_number[:, :], step_index[:, :]))
            pool.wait_ge(group_ready, 1)
            for t, table in enumerate(tables):
                for k in range(SB):
                    out = ints[:, t, k, :] if t < 2 else rows[:, 2, k, :]
                    pool.indirect_dma_start(
                        out, None, table, bass.IndirectOffsetOnAxis(group_id[:, k:k + 1].bitcast(U32), 0)
                    ).then_inc(rows_in, 16)

        @block.vector
        def _(dve):
            o = Order(dve, own)
            dve.wait_ge(last_in, 16)
            o.link(dve.tensor_scalar(last_tile[:, :], last[:, :], 7, None, ALU.arith_shift_right))
            o.link(dve.tensor_scalar(ends[:, :], last_tile[:, :], float(NT - 1), None, ALU.min))
            dve.wait_ge(numbered, 4)
            dve.tensor_tensor(ends[:, :], ends[:, :], group_number[:, :], ALU.add).then_inc(ends_ready, 1)
            dve.wait_ge(spread_ready, 1)
            o.link(dve.tensor_copy(ends_all[:, :], spread[:, :]))
            for k in range(SB):
                o.mark(dve.tensor_scalar(ended[:, k, :], ends_all[:, :], step_number[:, k:k + 1], None, ALU.is_lt))
            o.wait()
            o.link(dve.tensor_reduce(group[:, :], ended[:, :, :], AX, ALU.add))
            o.link(dve.tensor_scalar(group[:, :], group[:, :], float(NG - 1), None, ALU.min))
            dve.tensor_copy(group_id[:, :], group[:, :]).then_inc(group_ready, 1)
            o.link(dve.tensor_tensor(tile[:, :], step_number[:, :], group[:, :], ALU.subtract))
            o.link(dve.tensor_scalar(tile[:, :], tile[:, :], float(SPARE), None, ALU.min))
            dve.tensor_scalar(tile_base[:, :], tile[:, :], float(P), None, ALU.mult).then_inc(tile_ready, 1)
            dve.wait_ge(tile_ready, 1)
            dve.wait_ge(rows_in, 16 * 3 * SB)
            o.link(dve.tensor_copy(rows[:, 0:2, :, :], ints[:, :, :, :]))
            for k in range(SB):
                dve.tensor_scalar(rows[:, 1, k, :], rows[:, 1, k, :], tile_base[:, k:k + 1], None,
                                  ALU.subtract).then_inc(rows_ready, 1)
            outs = [step_src, step_dst, step_weight]
            for n, (t, g) in enumerate(turns):
                dve.wait_ge(turned_ready, n + 1)
                dve.tensor_copy(outs[t][:, :, g].rearrange("p (k s) -> p k s", k=SB),
                                turned[n % 2][:, 0:SB, :]).then_inc(turned_used, 1)
            dve.wait_ge(tile_row_ready, 1)
            dve.tensor_copy(step_tile[:, :], tile_row[:, :]).then_inc(tables_ready, 1)

        @block.tensor
        def _(pe):
            pe.wait_ge(ends_ready, 1)
            pe.matmul(spread[:, :], a.ones_row[:, :], ends[:, :], start=True, stop=True).then_inc(spread_ready, 1)
            pe.wait_ge(tile_ready, 1)
            for k in range(SB):
                last_mm = pe.matmul(tile_row[:, k * P:(k + 1) * P], tile[:, k:k + 1], a.ident[:, :],
                                    start=True, stop=True)
            last_mm.then_inc(tile_row_ready, 1)
            pe.wait_ge(rows_ready, SB)
            for n, (t, g) in enumerate(turns):
                if n >= 2:
                    pe.wait_ge(turned_used, n - 1)
                for k in range(SB):
                    last_mm = pe.transpose(turned[n % 2][:, k, :], rows[:, t, k, g * P:(g + 1) * P], a.ident[:, :])
                last_mm.then_inc(turned_ready, 1)


def normalize(dve, o, x, stats, moments, scale_ready, var_ready, out, base, n):
    for k in range(n):
        o.mark(dve.bn_stats(stats[:, k, :], x(k)))
    o.wait()
    for k in range(n):
        o.mark(dve.bn_aggr(moments[:, k, 0:2], stats[:, k, :]))
    o.wait()
    o.link(dve.tensor_scalar(moments[:, 0:n, 2], moments[:, 0:n, 1], EPS, None, ALU.add))
    dve.reciprocal(moments[:, 0:n, 2], moments[:, 0:n, 2]).then_inc(var_ready, 1)
    dve.wait_ge(scale_ready, base + 1)
    for k in range(n):
        o.mark(dve.tensor_scalar(out(k), x(k), moments[:, k, 0:1], moments[:, k, 3:4], ALU.subtract, ALU.mult))


def normalize_input(nc, a, x):
    with Stage(nc, "norm") as st:
        raw = [st.sbuf(f"raw{i}", [P, BT, D]) for i in range(2)]
        stats = st.sbuf("stats", [P, BT, 6])
        moments = st.sbuf("moments", [P, BT, 4])
        raw_in = [st.sem(f"raw_in{i}") for i in range(2)]
        own, var_ready, scale_ready, normed, stored = (
            st.sem("own"), st.sem("var_ready"), st.sem("scale_ready"), st.sem("normed"), st.sem("stored"))
        block = st.stack.enter_context(nc.Block())
        rows = x.rearrange("(t p) d -> p t d", p=P)
        out = a.normed_dram.ap().rearrange("(t p) d -> p t d", p=P)

        @block.sync
        def _(sp):
            for b in range(NB):
                if b >= 2:
                    sp.wait_ge(normed, b - 1)
                sp.dma_start(raw[b % 2][:, :, :], rows[:, b * BT:(b + 1) * BT, :]).then_inc(raw_in[b % 2], 16)
            for b in range(NB):
                sp.wait_ge(normed, b + 1)
                sp.dma_start(out[:, b * BT:(b + 1) * BT, :], a.nodes[:, b * BT:(b + 1) * BT, :]).then_inc(stored, 16)
            sp.wait_ge(stored, 16 * NB)

        @block.vector
        def _(dve):
            o = Order(dve, own)
            for b in range(NB):
                dve.wait_ge(raw_in[b % 2], 16 * (b // 2 + 1))
                normalize(dve, o, lambda k: raw[b % 2][:, k, :], stats, moments, scale_ready, var_ready,
                          lambda k: a.nodes[:, b * BT + k, :], b, BT)
                o.wait()
                dve.sem_inc(normed, 1)

        @block.scalar
        def _(act):
            for b in range(NB):
                act.wait_ge(var_ready, b + 1)
                act.activation(moments[:, :, 3], moments[:, :, 2], ACT.Sqrt).then_inc(scale_ready, 1)


class WalkTables:

    def __init__(self, st, a, weights):
        self.a = a
        self.src = st.sbuf("step_src", [P, SW, GE], I32)
        self.dst = st.sbuf("step_dst", [P, SW, GE])
        self.weight = st.sbuf("step_weight", [P, SW, GE]) if weights else None
        self.tile = st.sbuf("step_tile", [1, SW], I32)
        self.loaded = st.sem("tables_loaded")
        self.count = 16 * (4 if weights else 3)

    def load(self, sp):
        pairs = [(self.src, self.a.step_src_dram), (self.dst, self.a.step_dst_dram), (self.tile, self.a.step_tile_dram)]
        if self.weight is not None:
            pairs.append((self.weight, self.a.step_weight_dram))
        for table, stored in pairs:
            sp.dma_start(table.ap(), stored.ap()).then_inc(self.loaded, 16)


def aggregate_messages(nc, a):
    with Stage(nc, "agg") as st:
        tables = WalkTables(st, a, weights=True)
        rows = st.sbuf("rows", [P, RING, GE, D])
        picked = st.sbuf("picked", [P, 2, U * GE], I32)
        hot = st.sbuf("hot", [P, 4, GE, P])
        weighted = st.sbuf("weighted", [P, 4, GE, P])
        part = [st.psum(f"part{i}", [P, D]) for i in range(2)]
        count = [st.psum(f"count{i}", [P, 1]) for i in range(2)]
        rows_in = [st.sem(f"rows_in{i}") for i in range(RING)]
        gathers_begun = st.sem("gathers_begun")
        cleared, picked_ready, hot_ready, weighted_ready, product_ready, sums_added = (
            st.sem("cleared"), st.sem("picked_ready"), st.sem("hot_ready"), st.sem("weighted_ready"),
            st.sem("product_ready"), st.sem("sums_added"))
        block = st.stack.enter_context(nc.Block())
        src_of = tables.src[:, :, :].rearrange("p s g -> p (s g)")

        @block.sync
        def _(sp):
            tables.load(sp)

        @block.gpsimd
        def _(pool):
            pool.memset(a.sums[:, :, :], 0.0).then_inc(cleared, 1)
            pool.wait_ge(tables.loaded, tables.count)

            def gather(half, t, first):
                if not first:
                    pool.wait_ge(product_ready, t * U - U)
                pool.tensor_copy(picked[:, half, :],
                                 src_of[:, ds(t * (U * GE), U * GE)]).then_inc(picked_ready, 1)
                pool.wait_ge(picked_ready, t + 1)
                pool.sem_inc(gathers_begun, 1)
                for u in range(U):
                    for g in range(GE):
                        pool.indirect_dma_start(
                            rows[:, half * U + u, g, :], None, a.normed_dram.ap(),
                            bass.IndirectOffsetOnAxis(picked[:, half, u * GE + g:u * GE + g + 1].bitcast(U32), 0)
                        ).then_inc(rows_in[half * U + u], 16)

            gather(0, 0, True)
            gather(1, 1, True)
            with pool.Fori(2, STEPS // U, 2) as t:
                gather(0, t, False)
                gather(1, t + 1, False)

        @block.vector
        def _(dve):
            dve.wait_ge(cleared, 1)
            dve.wait_ge(tables.loaded, tables.count)

            def one_hot(s, u):
                at = u % 4
                d = tables.dst[:, ds(s, 1), :].rearrange("p o g -> p (o g)")
                w = tables.weight[:, ds(s, 1), :].rearrange("p o g -> p (o g)")
                dve.tensor_tensor(hot[:, at, :, :], a.columns[:, None, :].to_broadcast([P, GE, P]),
                                  d[:, :, None].to_broadcast([P, GE, P]), ALU.is_equal).then_inc(hot_ready, 1)
                dve.wait_ge(hot_ready, s + 1)
                dve.tensor_tensor(weighted[:, at, :, :], hot[:, at, :, :],
                                  w[:, :, None].to_broadcast([P, GE, P]), ALU.mult).then_inc(weighted_ready, 1)

            def add(s, u):
                j = dve.value_load(tables.tile[0:1, ds(s, 1)], min_val=0, max_val=SPARE)
                dve.wait_ge(product_ready, s + 1)
                dve.wait_ge(sums_added, 2 * s)
                total = a.sums[:, ds(j, 1), 0:D].rearrange("p o d -> p (o d)")
                degree = a.sums[:, ds(j, 1), D:D + 1].rearrange("p o d -> p (o d)")
                dve.tensor_tensor(total, total, part[u % 2][:, :], ALU.add).then_inc(sums_added, 1)
                dve.tensor_tensor(degree, degree, count[u % 2][:, :], ALU.add).then_inc(sums_added, 1)

            def steps(t, first):
                for u in range(RING):
                    s = t * RING + u
                    if not (first and u < 4):
                        dve.wait_ge(product_ready, s - 3)
                    one_hot(s, u)
                    if not (first and u < 1):
                        add(s - 1, (u - 1) % RING)

            steps(0, True)
            with dve.Fori(1, STEPS // RING) as t:
                steps(t, False)
            add(STEPS - 1, RING - 1)

        @block.tensor
        def _(pe):
            def steps(t, first):
                for u in range(RING):
                    s = t * RING + u
                    pe.wait_ge(weighted_ready, s + 1)
                    pe.wait_ge(rows_in[u], t * (16 * GE) + 16 * GE)
                    if not (first and u < 2):
                        pe.wait_ge(sums_added, 2 * s - 2)
                    for g in range(GE):
                        pe.matmul(count[u % 2][:, :], hot[:, u % 4, g, :], a.ones_col[:, :],
                                  start=(g == 0), stop=(g == GE - 1))
                    for g in range(GE):
                        last_mm = pe.matmul(part[u % 2][:, :], weighted[:, u % 4, g, :], rows[:, u, g, :],
                                            start=(g == 0), stop=(g == GE - 1))
                    last_mm.then_inc(product_ready, 1)

            steps(0, True)
            with pe.Fori(1, STEPS // RING) as t:
                steps(t, False)


def after(eng, sem, value):
    if not isinstance(value, int) or value > 0:
        eng.wait_ge(sem, value)


def in_pairs(eng, head, first, last, tail, body):
    for j in range(head, first):
        body(j, j % 2)
    with eng.Fori(first, last, 2) as j:
        body(j, first % 2)
        body(j + 1, 1 - first % 2)
    for j in range(last, tail):
        body(j, j % 2)


def convolve(nc, a, x, w):
    FB, FC = 4, 6
    PASSES = NT + FC + 1
    LD = LAYERS * D
    KB = 33
    F32R = mybir.dt.float32r
    with Stage(nc, "conv") as st:
        w_hi = st.sbuf("w_hi", [P, 2 * KD, LD], F32R)
        w_lo = st.sbuf("w_lo", [P, 2 * KD, LD], F32R)
        m_hi = st.sbuf("m_hi", [P, 2, KD, D], F32R)
        m_lo = st.sbuf("m_lo", [P, 2, KD, D], F32R)
        b_hi = st.sbuf("b_hi", [KB, LD + 2 * D], F32R)
        b_rows = st.sbuf("b_rows", [KB, LD + 2 * D], F32R)
        ones = st.sbuf("ones", [KB, P])
        ones_r = st.sbuf("ones_r", [KB, P], F32R)
        gain = st.sbuf("gain", [P, LAYERS, D])
        shift = st.sbuf("shift", [P, LAYERS, D])
        gain_mlp = st.sbuf("gain_mlp", [P, 2, D])
        shift_mlp = st.sbuf("shift_mlp", [P, 2, D])
        per_degree = st.sbuf("per_degree", [P, NT])
        x_in = st.sbuf("x_in", [P, 2, D])
        lhs_hi = st.sbuf("lhs_hi", [P, 2, 2 * KD, P], F32R)
        lhs_lo = st.sbuf("lhs_lo", [P, 2, 2 * KD, P], F32R)
        layer_work = st.sbuf("layer_work", [P, 2 * KD, LD])
        w_raw = layer_work[:, :, :]
        conv = layer_work[:, 0:2, :].rearrange("p i (l d) -> p i l d", d=D)
        positive = layer_work[:, 2, :].rearrange("p (l d) -> p l d", d=D)
        pair, summed = (layer_work[:, 3, n * 2 * D:(n + 1) * 2 * D].rearrange("p (i d) -> p i d", d=D)
                        for n in range(2))
        bc_lhs_hi = st.sbuf("bc_lhs_hi", [P, 2, KD, P], F32R)
        bc_lhs_lo = st.sbuf("bc_lhs_lo", [P, 2, KD, P], F32R)
        out_bc = st.sbuf("out_bc", [P, 2, 2, D])
        m_raw = out_bc[:, :, :, :]
        input_work = st.sbuf("input_work", [P, LD + 2 * D])
        b_raw = input_work[0:KB, :]
        staged = input_work[:, 0:LD].rearrange("p (i d) -> p i d", i=2)
        act_b = input_work[:, LD:LD + 2 * D].rearrange("p (i d) -> p i d", i=2)
        stats = st.sbuf("stats", [P, LAYERS + 2, 6])
        moments = st.sbuf("moments", [P, 2, LAYERS + 2, 4])
        turn = st.psum("turn", [P, 2 * KD, P])
        turn_bc = st.psum("turn_bc", [P, 2, KD, P])
        ps_conv = [[st.psum(f"ps_conv{i}{h}", [P, 2, D]) for h in range(2)] for i in range(2)]
        ps_bc = [st.psum(f"ps_bc{i}", [P, 2, D]) for i in range(2)]
        weights_in, affine_in, degrees_ready, ones_ready, b_cleared, raw_fixed, hi_split, lo_split = (
            st.sem(n) for n in ("weights_in", "affine_in", "degrees_ready", "ones_ready", "b_cleared", "raw_fixed",
                                "hi_split", "lo_split"))
        x_ready = [st.sem(f"x_ready{i}") for i in range(2)]
        staged_ready, turned, hi_ready, lo_ready, conv_ready, centered, normed, shifted, relued, pair_ready, first_sum, \
            summed_ready = (st.sem(n) for n in (
                "staged_ready", "turned", "hi_ready", "lo_ready", "conv_ready", "centered", "normed", "shifted",
                "relued", "pair_ready", "first_sum", "summed_ready"))
        bc_turned, bc_hi, bc_lo, bc_ready, bc_read, out_b_ready, act_b_ready, tile_done = (
            st.sem(n) for n in ("bc_turned", "bc_hi", "bc_lo", "bc_ready", "bc_read", "out_b_ready", "act_b_ready",
                                "tile_done"))
        own, settled, var, scale = st.sem("own"), st.sem("settled"), st.sem("var"), st.sem("scale")
        block = st.stack.enter_context(nc.Block())
        x_rows = x.rearrange("(t p) d -> p t d", p=P)
        tile_of = lambda t, j: t[:, ds(j, 1), 0:D].rearrange("p o d -> p (o d)")

        def runs(i, back, extra=0):
            return not isinstance(i, int) or 0 <= i - back < NT + extra

        def passes(eng, body):
            in_pairs(eng, 0, 9, NT - 2, PASSES, body)

        BOTH = FC - FB

        @block.sync
        def _(sp):
            k_rows = lambda t: t.rearrange("(k p) n -> p k n", p=P)
            sp.dma_start(w_raw[:, 0:KD, :], k_rows(w["L0_gnn_W_rel"])).then_inc(weights_in, 16)
            sp.dma_start(w_raw[:, KD:2 * KD, :], k_rows(w["L0_gnn_W_root"])).then_inc(weights_in, 16)
            sp.dma_start(m_raw[:, 0, :, :], k_rows(w["L0_gnn_W1"])).then_inc(weights_in, 16)
            sp.dma_start(m_raw[:, 1, :, :], k_rows(w["L0_gnn_W2"])).then_inc(weights_in, 16)
            sp.wait_ge(b_cleared, 1)
            for row in (0, KB - 1):
                sp.dma_start(b_raw[row:row + 1, 0:LD], w["L0_gnn_b_rel"]).then_inc(weights_in, 16)
                for i, name in enumerate(("L0_gnn_b1", "L0_gnn_b2")):
                    sp.dma_start(b_raw[row:row + 1, LD + i * D:LD + (i + 1) * D], w[name]).then_inc(weights_in, 16)
            for out, name in ((gain[:, :, :], "L0_gnn_ln_g"), (shift[:, :, :], "L0_gnn_ln_b")):
                sp.dma_start(out.rearrange("p l d -> p (l d)"), w[name].to_broadcast([P, LD])).then_inc(affine_in, 16)
            for i, (g, b) in enumerate((("L0_gnn_mg1", "L0_gnn_mb1"), ("L0_gnn_mg2", "L0_gnn_mb2"))):
                sp.dma_start(gain_mlp[:, i, :], w[g].to_broadcast([P, D])).then_inc(affine_in, 16)
                sp.dma_start(shift_mlp[:, i, :], w[b].to_broadcast([P, D])).then_inc(affine_in, 16)

            def load(j, par):
                after(sp, tile_done, j - 1)
                sp.dma_start(x_in[:, par, :], tile_of(x_rows, j)).then_inc(x_ready[par], 16)

            in_pairs(sp, 0, 5, 47, NT, load)

        @block.scalar
        def _(act):
            def stage(j, par):
                after(act, turned, j - 1)
                act.activation(staged[:, par, 0:D], tile_of(a.sums, j), ACT.Copy, scale=per_degree[:, ds(j, 1)])
                act.activation(staged[:, par, D:2 * D], tile_of(a.nodes, j), ACT.Copy).then_inc(staged_ready, 1)

            def one_pass(i, par):
                if runs(i, 0):
                    act.wait_ge(turned, i + 1)
                    after(act, conv_ready, i - 1)
                    act.activation(lhs_hi[:, par, :, :], turn[:, :, :], ACT.Copy).then_inc(hi_ready, 1)
                if runs(i, -1):
                    stage(i + 1, 1 - par)
                if runs(i, FB, BOTH):
                    act.wait_ge(bc_turned, i - FB + 1)
                    after(act, bc_ready, i - FB)
                    side = slice(0 if runs(i, FB) else 1, 2 if runs(i, FC) else 1)
                    act.activation(bc_lhs_hi[:, side, :, :], turn_bc[:, side, :, :], ACT.Copy).then_inc(bc_hi, 1)
                if runs(i, 3):
                    act.wait_ge(shifted, i - 2)
                    after(act, summed_ready, i - 3)
                    act.activation(positive[:, :, :], conv[:, 1 - par, :, :], ACT.Relu).then_inc(relued, 1)
                if runs(i, 2, FC - 1):
                    act.wait_ge(var, i - 1)
                    side = slice(0 if runs(i, 2) else LAYERS + (0 if runs(i, FB + 1) else 1),
                                 LAYERS + (2 if runs(i, FC + 1) else 1 if runs(i, FB + 1) else 0))
                    act.activation(moments[:, par, side, 3], moments[:, par, side, 2], ACT.Sqrt).then_inc(scale, 1)
                if runs(i, 2):
                    act.wait_ge(centered, i - 1)
                    act.wait_ge(scale, i - 1)
                    for l in range(LAYERS):
                        c = conv[:, par, l, :]
                        last = act.activation(c, c, ACT.Copy, scale=moments[:, par, l, 3:4])
                    last.then_inc(normed, 1)
                if runs(i, FB + 1):
                    act.wait_ge(out_b_ready, i - FB)
                    act.activation(act_b[:, 1 - par, :], out_bc[:, 1 - par, 0, :], ACT.Relu).then_inc(act_b_ready, 1)

            act.wait_ge(raw_fixed, KD * LAYERS)
            act.wait_ge(weights_in, 16 * 10)
            act.activation(b_hi[:, :], b_raw[:, :], ACT.Copy).then_inc(hi_split, 1)
            act.activation(m_hi[:, :, :, :], m_raw[:, :, :, :], ACT.Copy).then_inc(hi_split, 1)
            act.activation(w_hi[:, :, :], w_raw[:, :, :], ACT.Copy).then_inc(hi_split, 1)
            act.wait_ge(degrees_ready, 2)
            act.wait_ge(lo_split, 5)
            stage(0, 0)
            passes(act, one_pass)

        @block.gpsimd
        def _(pool):
            pool.memset(b_raw[:, :], 0.0).then_inc(b_cleared, 1)
            pool.memset(ones[:, :], 1.0).then_inc(ones_ready, 1)

            def one_pass(i, par):
                if runs(i, 2):
                    pool.wait_ge(normed, i - 1)
                    pool.tensor_tensor(conv[:, par, :, :], conv[:, par, :, :], shift[:, :, :], ALU.add
                                       ).then_inc(shifted, 1)
                if runs(i, 3):
                    k = i - 3
                    pool.wait_ge(relued, k + 1)
                    pool.tensor_tensor(pair[:, :, :], positive[:, 0:2, :], positive[:, 2:4, :], ALU.add
                                       ).then_inc(pair_ready, 1)
                    pool.wait_ge(pair_ready, k + 1)
                    after(pool, bc_turned, k - 1)
                    pool.tensor_tensor(summed[:, 1 - par, :], pair[:, 0, :], pair[:, 1, :], ALU.add
                                       ).then_inc(summed_ready, 1)

            pool.wait_ge(affine_in, 16 * 6)
            passes(pool, one_pass)

        @block.vector
        def _(dve):
            dve.tensor_scalar(per_degree[:, :], a.sums[:, 0:NT, D], 1.0, None, ALU.max).then_inc(degrees_ready, 1)
            dve.wait_ge(degrees_ready, 1)
            dve.reciprocal(per_degree[:, :], per_degree[:, :]).then_inc(degrees_ready, 1)
            dve.tensor_copy(a.degree[:, :], a.sums[:, 0:NT, D])
            dve.wait_ge(weights_in, 16 * 10)
            for l in range(LAYERS):
                for k in range(KD):
                    c = slice(l * D + k * P, l * D + (k + 1) * P)
                    dve.tensor_tensor(w_raw[:, KD + k, c], w_raw[:, KD + k, c], a.ident[:, :], ALU.add
                                      ).then_inc(raw_fixed, 1)
            dve.wait_ge(ones_ready, 1)
            dve.tensor_copy(ones_r[:, :], ones[:, :]).then_inc(lo_split, 1)
            dve.wait_ge(hi_split, 3)
            dve.wait_ge(raw_fixed, KD * LAYERS)
            dve.tensor_tensor(m_lo[:, :, :, :], m_raw[:, :, :, :], m_hi[:, :, :, :].bitcast(F32), ALU.subtract
                              ).then_inc(lo_split, 1)
            dve.tensor_tensor(b_rows[:, :], b_raw[:, :], b_hi[:, :].bitcast(F32), ALU.subtract).then_inc(lo_split, 1)
            dve.tensor_tensor(w_lo[:, :, :], w_raw[:, :, :], w_hi[:, :, :].bitcast(F32), ALU.subtract
                              ).then_inc(lo_split, 1)
            dve.wait_ge(lo_split, 4)
            dve.tensor_copy(b_rows[0:1, :], b_hi[0:1, :].bitcast(F32)).then_inc(lo_split, 1)

            def own_of(i):
                n = (LAYERS if runs(i, 2) else 0) + int(runs(i, FB + 1)) + int(runs(i, FC + 1))
                late = (1 if runs(i, FB + 1) else 0) + (2 if runs(i, FC + 1) else 0)
                return (2 * n + 1 if n else 0) + late

            def own_before(i):
                if isinstance(i, int):
                    return sum(own_of(k) for k in range(i))
                full = own_of(i)
                return (i - 9) * full + own_before(9)

            def one_pass(i, par):
                o = Order(dve, own, own_before(i))
                if runs(i, 0):
                    dve.wait_ge(hi_ready, i + 1)
                    after(dve, conv_ready, i - 1)
                    dve.tensor_tensor(lhs_lo[:, par, :, :], turn[:, :, :], lhs_hi[:, par, :, :].bitcast(F32),
                                      ALU.subtract).then_inc(lo_ready, 1)
                slots = []
                if runs(i, 2):
                    dve.wait_ge(conv_ready, i - 1)
                    slots += [(l, ps_conv[par][l // 2][:, l % 2, :]) for l in range(LAYERS)]
                bc = [n for n, back in enumerate((FB, FC)) if runs(i, back + 1)]
                if bc:
                    dve.wait_ge(bc_ready, i - FB)
                    slots += [(LAYERS + n, ps_bc[1 - par][:, n, :]) for n in bc]
                for l, source in slots:
                    o.mark(dve.bn_stats(stats[:, l, :], source))
                if slots:
                    if not isinstance(i, int) or i >= 4:
                        dve.wait_ge(normed, min(i - 3, NT) if isinstance(i, int) else i - 3)
                    o.wait_apart(settled)
                    for l, _source in slots:
                        o.mark(dve.bn_aggr(moments[:, par, l, 0:2], stats[:, l, :]))
                    o.wait()
                    m = moments[:, par, slots[0][0]:slots[-1][0] + 1, :]
                    o.link(dve.tensor_scalar(m[:, :, 2], m[:, :, 1], EPS, None, ALU.add))
                    dve.reciprocal(m[:, :, 2], m[:, :, 2]).then_inc(var, 1)
                if runs(i, 2):
                    after(dve, relued, i - 3)
                    for l in range(LAYERS):
                        last = dve.scalar_tensor_tensor(out=conv[:, par, l, :], in0=ps_conv[par][l // 2][:, l % 2, :],
                                                        scalar=moments[:, par, l, 0:1], in1=gain[:, l, :],
                                                        op0=ALU.subtract, op1=ALU.mult)
                    last.then_inc(centered, 1)
                if runs(i, FB, BOTH):
                    side = slice(0 if runs(i, FB) else 1, 2 if runs(i, FC) else 1)
                    dve.wait_ge(bc_hi, i - FB + 1)
                    after(dve, bc_ready, i - FB)
                    dve.tensor_tensor(bc_lhs_lo[:, side, :, :], turn_bc[:, side, :, :],
                                      bc_lhs_hi[:, side, :, :].bitcast(F32), ALU.subtract).then_inc(bc_lo, 1)
                if bc:
                    out = lambda n: out_bc[:, 1 - par, n, :]
                    if 0 in bc:
                        after(dve, act_b_ready, i - FB - 2)
                    for n in bc:
                        ins = dve.scalar_tensor_tensor(
                            out=out(n), in0=ps_bc[1 - par][:, n, :], scalar=moments[:, par, LAYERS + n, 0:1],
                            in1=gain_mlp[:, n, :], op0=ALU.subtract, op1=ALU.mult)
                        o.mark(ins)
                    o.wait()
                    dve.sem_inc(bc_read, 1)
                    dve.wait_ge(scale, i - 1)
                    for n in reversed(bc):
                        ins = dve.scalar_tensor_tensor(out=out(n), in0=out(n), scalar=moments[:, par, LAYERS + n, 3:4],
                                                       in1=shift_mlp[:, n, :], op0=ALU.mult, op1=ALU.add)
                        if n == 0:
                            ins.then_inc(out_b_ready, 1)
                        else:
                            o.mark(ins)
                    if 1 in bc:
                        k, side = i - FC - 1, 1 - par
                        dve.wait_ge(x_ready[side], 16 * (k // 2 + 1) if isinstance(k, int) else (k - side) * 8 + 16)
                        o.wait()
                        dve.scalar_tensor_tensor(out=tile_of(a.nodes, k), in0=out(1), scalar=0.0, in1=x_in[:, side, :],
                                                 op0=ALU.max, op1=ALU.add).then_inc(tile_done, 1)
                assert o.n == own_of(i), (i, o.n, own_of(i))

            dve.wait_ge(affine_in, 16 * 6)
            passes(dve, one_pass)

        @block.tensor
        def _(pe):
            def triple(out, hi, lo, right_hi, right_lo, bias):
                n = len(hi)
                terms = [(x_, y) for x_, y in zip(hi, right_hi)] + list(zip(hi, right_lo)) + list(zip(lo, right_hi))
                for q, (x_, y) in enumerate(terms):
                    pe.matmul(out, x_, y, start=(q == 0), stop=False)
                return pe.matmul(out, ones_r[:, :], bias, start=False, stop=True)

            def one_pass(i, par):
                if runs(i, 0):
                    pe.wait_ge(staged_ready, i + 1)
                    after(pe, lo_ready, i)
                    for k in range(2 * KD):
                        mm = pe.transpose(turn[:, k, :], staged[:, par, k * P:(k + 1) * P], a.ident[:, :])
                    mm.then_inc(turned, 1)
                if runs(i, FB, BOTH):
                    after(pe, bc_lo, i - FB)
                    if runs(i, FC):
                        pe.wait_ge(act_b_ready, i - FC + 1)
                        for k in range(KD):
                            mm = pe.transpose(turn_bc[:, 1, k, :], act_b[:, par, k * P:(k + 1) * P], a.ident[:, :])
                    if runs(i, FB):
                        pe.wait_ge(summed_ready, i - FB + 1)
                        for k in range(KD):
                            mm = pe.transpose(turn_bc[:, 0, k, :], summed[:, par, k * P:(k + 1) * P], a.ident[:, :])
                    mm.then_inc(bc_turned, 1)
                if runs(i, 1):
                    pe.wait_ge(lo_ready, i)
                    after(pe, centered, i - 2)
                    for h in range(2):
                        half = slice(h * 2 * D, (h + 1) * 2 * D)
                        ks = range(2 * KD)
                        mm = triple(ps_conv[1 - par][h][:, :, :].rearrange("p l d -> p (l d)"),
                                    [lhs_hi[:, 1 - par, k, :] for k in ks], [lhs_lo[:, 1 - par, k, :] for k in ks],
                                    [w_hi[:, k, half] for k in ks], [w_lo[:, k, half] for k in ks], b_rows[:, half])
                    mm.then_inc(conv_ready, 1)
                if runs(i, FB, BOTH):
                    pe.wait_ge(bc_lo, i - FB + 1)
                    after(pe, bc_read, i - FB - 1)
                    for n, back in enumerate((FB, FC)):
                        if runs(i, back):
                            ks = range(KD)
                            mm = triple(ps_bc[par][:, n, :],
                                        [bc_lhs_hi[:, n, k, :] for k in ks], [bc_lhs_lo[:, n, k, :] for k in ks],
                                        [m_hi[:, n, k, :] for k in ks], [m_lo[:, n, k, :] for k in ks],
                                        b_rows[:, LD + n * D:LD + (n + 1) * D])
                    mm.then_inc(bc_ready, 1)

            pe.wait_ge(lo_split, 5)
            passes(pe, one_pass)




class Mixture:

    def __init__(self, experts, hidden, func, router_hidden, adds_input, weights, biases, out_bias, router):
        self.experts, self.hidden, self.func, self.router_hidden = experts, hidden, func, router_hidden
        self.adds_input = adds_input
        self.weights, self.biases, self.out_bias, self.router = weights, biases, out_bias, router


HEADS = (4, BT - 4)
SLOTS = 8


def mix(nc, a, name, moe, w, out=None):
    NE, NH = moe.experts, moe.hidden
    NL = NH + 1
    UNITS = [(e, h) for e in range(NE) for h in range(2)]
    NU = len(UNITS)
    F32R = mybir.dt.float32r
    WIDE = HEADS[0] * P
    TILES = {1: (0, 1), 2: (2, 3), 3: (4, 5), 4: (6,)}
    PAIRS = list(TILES.values())
    ROUTE, PICK, TURN = 5, 8, 11
    PARTS = 13
    NEXP = 2 if moe.router_hidden else 1
    OWN_INPUT = BT if moe.adds_input else 0
    OWN_STATS = 2 * BT + 1
    OWN_PICK = [2, 2 * BT + 4, 7 if moe.router_hidden else 8]
    OWN_BLOCK = OWN_STATS + OWN_INPUT + sum(OWN_PICK)
    with Stage(nc, name) as st:
        w_hi = st.sbuf("w_hi", [P, NE, NL, KD, D], F32R)
        w_lo = st.sbuf("w_lo", [P, NE, NL, KD, D], F32R)
        bias = st.sbuf("bias", [P, NH, NE, KD])
        out_bias = st.sbuf("out_bias", [NE, D])
        RW = R0 if moe.router_hidden else SLOTS
        r_raw = st.sbuf("r_raw", [P, KD, RW])
        r_hi = st.sbuf("r_hi", [P, KD, RW], F32R)
        r_lo = st.sbuf("r_lo", [P, KD, RW], F32R)
        f_hi = st.sbuf("f_hi", [P, 2, KD, BN], F32R)
        f_lo = st.sbuf("f_lo", [P, 2, KD, BN], F32R)
        normed = st.sbuf("normed", [P, 2, D])
        full = [st.sbuf(f"full{l}", [P, KD, WIDE]) for l in range(NH)]
        raw = full if NH > 1 else full + [st.sbuf("raw", [P, KD, WIDE])]
        w_raw = [t[:, i, :].rearrange("p (k n) -> p k n", k=KD) for t in raw for i in range(2)]
        NR = len(w_raw)
        h_hi = [st.sbuf(f"h_hi{l}", [P, 2, KD, WIDE], F32R) for l in range(NH)]
        h_lo = [st.sbuf(f"h_lo{l}", [P, 2, KD, WIDE], F32R) for l in range(NH)]
        stats = st.sbuf("stats", [P, BT, 6])
        moments = st.sbuf("moments", [P, BT, 4])
        logits = st.sbuf("logits", [P, BT, SLOTS])
        probs = st.sbuf("probs", [P, BT, SLOTS])
        top = st.sbuf("top", [P, BT, SLOTS])
        top_index = st.sbuf("top_index", [P, BT, SLOTS], U32)
        chosen = st.sbuf("chosen", [P, BT, 2])
        share = st.sbuf("share", [P, BT, 2])
        row = st.sbuf("row", [P, BT, 2])
        picks = st.sbuf("picks", [P, BT, SLOTS])
        combine = st.sbuf("combine", [P, 2, BT, SLOTS])
        combine_turned = st.sbuf("combine_turned", [SLOTS, BT, P])
        if moe.router_hidden:
            rh_bias = st.sbuf("rh_bias", [P, 1])
            rh = st.sbuf("rh", [P, WIDE])
            r_out = st.sbuf("r_out", [P, NE])
            r_out_bias = st.sbuf("r_out_bias", [P, NE])
        ps_h = [[st.psum(f"ps_h{l}{m}", [P, WIDE]) for m in range(KD)] for l in range(NH)]
        ps_out = [st.psum(f"ps_out{i}", [P, 2, D]) for i in range(2)]
        ps_turn = st.psum("ps_turn", [P, 2, KD, P])
        turned_tiles = ps_turn[:, :, :, :].rearrange("p i k n -> p (i k) n")
        route_logits = ps_turn[:, 0, 0, 0:BT * SLOTS].rearrange("p (t e) -> p t e", t=BT)
        ps_route = st.psum("ps_route", [P, 512])
        names = ["small_in", "weight_used", "weights_ready", "cleared", "own", "var", "scale", "normed_ready",
                 "turned", "hi_ready", "features_ready", "rh_ready", "rh_read", "half_routed", "exp_in", "exp_out",
                 "combine_ready", "combine_turn", "combine_turned_ready", "bias_product", "bias_added", "pre_own",
                 "out_product", "out_added", "stored", "weight_hi", "settled"]
        s = {n: st.sem(n) for n in names}
        prod = [st.sem(f"prod{l}") for l in range(NH)]
        evac = [st.sem(f"evac{l}") for l in range(NH)]
        split = [st.sem(f"split{l}") for l in range(NH)]
        MATS = [(e, l) for e in range(NE) for l in range(NL)]
        raw_in = [st.sem(f"raw_in{n}") for n in range(len(MATS))]
        block = st.stack.enter_context(nc.Block())
        n_small = [0]

        def tiles_of(f, par, t0, n):
            return f[:, par, :, t0 * P:(t0 + n) * P].rearrange("p k (t n) -> p t k n", n=P)

        def out_count(b, u):
            return b * (2 * NU) + 2 * u

        def prologue(early, late, split_off):
            for part in range(PARTS):
                early(0, 0, part)
                late(0, 0, part)
                for n in range(len(MATS)):
                    if n * PARTS // len(MATS) == part:
                        split_off(n)

        def stream(b, hidden, output, bias_unit, other, early, late):
            more = not isinstance(b, int) or b + 1 < NB
            for v in range(NU + NH):
                for l in range(NH):
                    if 0 <= v - l < NU:
                        hidden(l, v - l)
                    if l == 0 and more and v < PARTS:
                        early(b + 1, other, v)
                if v == 0:
                    bias_unit(b)
                if v >= NH:
                    output(v - NH)
                if more and v < PARTS:
                    late(b + 1, other, v)

        @block.sync
        def _(sp):
            def small(dst, src):
                sp.dma_start(dst, src).then_inc(s["small_in"], 16)
                n_small[0] += 16

            small(r_raw[:, :, :], moe.router[0].rearrange("(k p) n -> p k n", p=P))
            for l in range(NH):
                small(bias[:, l, :, :], moe.biases[l])
            small(out_bias[:, :], moe.out_bias)
            if moe.router_hidden:
                small(rh_bias[:, :], moe.router[1])
                small(r_out[:, :], moe.router[2])
                small(r_out_bias[:, :], moe.router[3].to_broadcast([P, NE]))
            for n, (e, l) in enumerate(MATS):
                if n >= NR:
                    sp.wait_ge(s["weight_used"], n - NR + 1)
                sp.dma_start(w_raw[n % NR], moe.weights[l][e].rearrange("(k p) n -> p k n", p=P)
                             ).then_inc(raw_in[n], 16)
            if out is not None:
                rows = out.rearrange("(t p) d -> p t d", p=P)

                def store(b, par):
                    sp.wait_ge(s["out_added"], b * (2 * NU) + 2 * NU)
                    sp.dma_start(rows[:, ds(b * BT, BT), :], a.nodes[:, ds(b * BT, BT), :]).then_inc(s["stored"], 16)

                in_pairs(sp, 0, 1, 5, NB, store)
                sp.wait_ge(s["stored"], 16 * NB)

        @block.gpsimd
        def _(pool):
            pool.memset(logits[:, :, :], LOW).then_inc(s["cleared"], 1)

        @block.scalar
        def _(act):
            act.wait_ge(s["small_in"], n_small[0])
            act.activation(r_hi[:, :, :], r_raw[:, :, :], ACT.Copy).then_inc(s["weight_hi"], 1)

            def split_off(n):
                e, l = MATS[n]
                act.wait_ge(raw_in[n], 16)
                act.activation(w_hi[:, e, l, :, :], w_raw[n % NR], ACT.Copy).then_inc(s["weight_hi"], 1)

            def features(b, par, part):
                t0, n = TILES[part][0], len(TILES[part])
                act.wait_ge(s["turned"], b * len(TILES) + part)
                act.activation(tiles_of(f_hi, par, t0, n), ps_turn[:, 0:n, :, :], ACT.Copy).then_inc(s["hi_ready"], 1)

            def early(b, par, part):
                if part == 1:
                    act.wait_ge(s["var"], b + 1)
                    act.activation(moments[:, :, 3], moments[:, :, 2], ACT.Sqrt).then_inc(s["scale"], 1)
                if part - 1 in TILES:
                    features(b, par, part - 1)
                if part in (ROUTE + 1, ROUTE + 2) and moe.router_hidden:
                    h = part - ROUTE - 1
                    n = HEADS[h] * P
                    act.wait_ge(s["rh_ready"], b * 2 + (h + 1))
                    after(act, s["half_routed"], b * 2 + h)
                    act.activation(rh[:, 0:n], ps_route[:, 0:n], ACT.Relu, bias=rh_bias[:, 0:1]
                                   ).then_inc(s["rh_read"], 1)
                if part == PICK + 1:
                    act.wait_ge(s["exp_in"], b * NEXP + 1)
                    act.activation(probs[:, :, :], logits[:, :, :], ACT.Exp).then_inc(s["exp_out"], 1)
                if part == PICK + 2 and NEXP == 2:
                    act.wait_ge(s["exp_in"], b * NEXP + 2)
                    act.activation(share[:, :, 1], row[:, :, 0], ACT.Exp).then_inc(s["exp_out"], 1)

            def late(b, par, part):
                if part in (TURN, TURN + 1):
                    h = part - TURN
                    act.wait_ge(s["combine_turn"], b * 2 + (h + 1))
                    t0 = h * HEADS[0]
                    act.activation(combine_turned[:, t0:t0 + HEADS[h], :],
                                   turned_tiles[0:SLOTS, 0:HEADS[h], :], ACT.Copy
                                   ).then_inc(s["combine_turned_ready"], 1)

            def hidden(b, l, u):
                e, h = UNITS[u]
                n = HEADS[h] * P
                for m in range(KD):
                    c = b * (2 * NU) + (2 * u + m)
                    act.wait_ge(prod[l], c + 1)
                    if l + 1 < NH:
                        after(act, prod[l + 1], c - m - 2)
                    else:
                        if not isinstance(b, int) or b > 0 or u >= 2:
                            act.wait_ge(s["out_product"], out_count(b, u - 1))
                    after(act, split[l], c - 1)
                    act.activation(h_hi[l][:, u % 2, m, 0:n], ps_h[l][m][:, 0:n], moe.func, bias=bias[:, l, e, m:m + 1])
                    act.activation(full[l][:, m, 0:n], ps_h[l][m][:, 0:n], moe.func, bias=bias[:, l, e, m:m + 1]
                                   ).then_inc(evac[l], 1)

            def body(b, par):
                stream(b, lambda l, u: hidden(b, l, u), lambda u: None, lambda u: None, 1 - par,
                       early, late)

            prologue(early, late, split_off)
            in_pairs(act, 0, 1, 5, NB, body)

        @block.vector
        def _(dve):
            dve.wait_ge(s["weight_hi"], 1)
            dve.wait_ge(s["small_in"], n_small[0])
            dve.tensor_tensor(r_lo[:, :, :], r_raw[:, :, :], r_hi[:, :, :].bitcast(F32), ALU.subtract
                              ).then_inc(s["weights_ready"], 1)
            dve.wait_ge(s["cleared"], 1)

            def split_off(n):
                e, l = MATS[n]
                dve.wait_ge(s["weight_hi"], n + 2)
                dve.wait_ge(raw_in[n], 16)
                dve.tensor_tensor(w_lo[:, e, l, :, :], w_raw[n % NR], w_hi[:, e, l, :, :].bitcast(F32),
                                  ALU.subtract).then_inc(s["weight_used"], 1)

            def own_before(part):
                tiles = sum(len(ts) for p, ts in TILES.items() if p < part) if moe.adds_input else 0
                return tiles + (OWN_STATS if part else 0) + sum(OWN_PICK[0:max(part - PICK, 0)])

            def early(b, par, part):
                if part - 1 in TILES:
                    t0, n = TILES[part - 1][0], len(TILES[part - 1])
                    dve.wait_ge(s["hi_ready"], b * len(TILES) + part - 1)
                    dve.tensor_tensor(tiles_of(f_lo, par, t0, n), ps_turn[:, 0:n, :, :],
                                      tiles_of(f_hi, par, t0, n).bitcast(F32), ALU.subtract
                                      ).then_inc(s["features_ready"], 1)

            def late(b, par, part):
                o = Order(dve, s["pre_own"], b * OWN_BLOCK + own_before(part))
                node = lambda t: a.nodes[:, ds(b * BT + t, 1), :].rearrange("p o d -> p (o d)")
                if part == 0:
                    for t in range(BT):
                        o.mark(dve.bn_stats(stats[:, t, :], node(t)))
                    o.wait_apart(s["settled"])
                    for t in range(BT):
                        o.mark(dve.bn_aggr(moments[:, t, 0:2], stats[:, t, :]))
                    o.wait()
                    o.link(dve.tensor_scalar(moments[:, :, 2], moments[:, :, 1], EPS, None, ALU.add))
                    dve.reciprocal(moments[:, :, 2], moments[:, :, 2]).then_inc(s["var"], 1)
                if part in TILES:
                    if part == 1:
                        dve.wait_ge(s["scale"], b + 1)
                    after(dve, s["turned"], b * len(TILES) + part - 1)
                    for t in TILES[part]:
                        last = dve.tensor_scalar(normed[:, t % 2, :], node(t), moments[:, t, 0:1], moments[:, t, 3:4],
                                                 ALU.subtract, ALU.mult)
                    last.then_inc(s["normed_ready"], 1)
                    if moe.adds_input:
                        dve.wait_ge(s["normed_ready"], b * len(TILES) + part)
                        for t in TILES[part]:
                            o.mark(dve.tensor_tensor(node(t), node(t), normed[:, t % 2, :], ALU.add))
                        o.wait()
                got = route_logits[:, :, 0:NE]
                z = logits[:, :, 0:NE]
                if part == PICK:
                    dve.wait_ge(s["half_routed"], b * 2 + 2)
                    if moe.router_hidden:
                        o.link(dve.tensor_tensor(z, got, r_out_bias[:, None, :].to_broadcast([P, BT, NE]), ALU.add))
                    else:
                        o.link(dve.tensor_copy(z, got))
                    o.link(dve.tensor_reduce(row[:, :, 1], z, AX, ALU.max))
                    dve.tensor_tensor(z, z, row[:, :, 1:2].to_broadcast([P, BT, NE]), ALU.subtract
                                      ).then_inc(s["exp_in"], 1)
                if part == PICK + 1:
                    dve.wait_ge(s["exp_out"], b * NEXP + 1)
                    o.link(dve.tensor_reduce(row[:, :, 1], probs[:, :, :], AX, ALU.add))
                    o.link(dve.reciprocal(row[:, :, 1], row[:, :, 1]))
                    o.mark(dve.tensor_tensor(probs[:, :, :], probs[:, :, :],
                                             row[:, :, 1:2].to_broadcast([P, BT, SLOTS]), ALU.mult))
                    o.wait_apart(s["settled"])
                    for t in range(BT):
                        o.mark(dve.max(top[:, t, :], probs[:, t, :]))
                    o.wait_apart(s["settled"])
                    for t in range(BT):
                        o.mark(dve.max_index(top_index[:, t, :], top[:, t, :], probs[:, t, :]))
                    o.wait()
                    o.mark(dve.tensor_copy(chosen[:, :, :], top_index[:, :, 0:2]))
                    if NEXP == 2:
                        dve.tensor_tensor(row[:, :, 0], top[:, :, 1], top[:, :, 0], ALU.subtract
                                          ).then_inc(s["exp_in"], 1)
                if part == PICK + 2:
                    if NEXP == 2:
                        dve.wait_ge(s["exp_out"], b * NEXP + 2)
                        o.link(dve.tensor_scalar(row[:, :, 1], share[:, :, 1], 1.0, None, ALU.add))
                        o.link(dve.reciprocal(share[:, :, 0], row[:, :, 1]))
                        o.link(dve.tensor_tensor(share[:, :, 1], share[:, :, 1], share[:, :, 0], ALU.mult))
                    else:
                        o.link(dve.tensor_tensor(row[:, :, 0], top[:, :, 0], top[:, :, 1], ALU.add))
                        o.link(dve.tensor_scalar(row[:, :, 0], row[:, :, 0], 1e-12, None, ALU.max))
                        o.link(dve.reciprocal(row[:, :, 1], row[:, :, 0]))
                        o.link(dve.tensor_tensor(share[:, :, :], top[:, :, 0:2],
                                                 row[:, :, 1:2].to_broadcast([P, BT, 2]), ALU.mult))
                    index = a.columns[:, None, 0:SLOTS].to_broadcast([P, BT, SLOTS])
                    wide = lambda x: x.to_broadcast([P, BT, SLOTS])
                    o.mark(dve.tensor_tensor(combine[:, par, :, :], index, wide(chosen[:, :, 0:1]), ALU.is_equal))
                    o.link(dve.tensor_tensor(picks[:, :, :], index, wide(chosen[:, :, 1:2]), ALU.is_equal))
                    o.mark(dve.tensor_tensor(combine[:, par, :, :], combine[:, par, :, :], wide(share[:, :, 0:1]),
                                             ALU.mult))
                    o.link(dve.tensor_tensor(picks[:, :, :], picks[:, :, :], wide(share[:, :, 1:2]), ALU.mult))
                    dve.tensor_tensor(combine[:, par, :, :], combine[:, par, :, :], picks[:, :, :], ALU.add
                                      ).then_inc(s["combine_ready"], 1)
                assert o.base + o.n == b * OWN_BLOCK + own_before(part + 1) if isinstance(b, int) else True

            def hidden(b, l, u):
                e, h = UNITS[u]
                n = HEADS[h] * P
                for m in range(KD):
                    c = b * (2 * NU) + (2 * u + m)
                    dve.wait_ge(evac[l], c + 1)
                    dve.tensor_tensor(h_lo[l][:, u % 2, m, 0:n], full[l][:, m, 0:n],
                                      h_hi[l][:, u % 2, m, 0:n].bitcast(F32), ALU.subtract).then_inc(split[l], 1)

            def add_bias(b, par):
                for j, tiles in enumerate(PAIRS):
                    dve.wait_ge(s["bias_product"], b * len(PAIRS) + (j + 1))
                    for i, t in enumerate(tiles):
                        x = a.nodes[:, ds(b * BT + t, 1), :].rearrange("p o d -> p (o d)")
                        last = dve.tensor_tensor(x, x, ps_out[j % 2][:, i, :], ALU.add)
                    last.then_inc(s["bias_added"], 1)

            def output(b, par, u):
                e, h = UNITS[u]
                for j in range(2):
                    q = out_count(b, u) + j
                    dve.wait_ge(s["out_product"], q + 1)
                    if u < 2:
                        dve.wait_ge(s["bias_added"], b * len(PAIRS) + (2 * h + j + 1))
                    else:
                        dve.wait_ge(s["out_added"], q - len(PAIRS) + 1)
                    for i, t in enumerate(PAIRS[2 * h + j]):
                        x = a.nodes[:, ds(b * BT + t, 1), :].rearrange("p o d -> p (o d)")
                        last = dve.scalar_tensor_tensor(out=x, in0=ps_out[j][:, i, :],
                                                        scalar=combine[:, par, t, e:e + 1], in1=x,
                                                        op0=ALU.mult, op1=ALU.add)
                    last.then_inc(s["out_added"], 1)

            def body(b, par):
                stream(b, lambda l, u: hidden(b, l, u), lambda u: output(b, par, u),
                       lambda b_: add_bias(b, par), 1 - par, early, late)

            prologue(early, late, split_off)
            in_pairs(dve, 0, 1, 5, NB, body)

        @block.tensor
        def _(pe):
            pe.wait_ge(s["weights_ready"], 1)

            def triple(out_, pairs, first=True, last=True):
                terms = [(lh, rh_) for lh, ll, rh_, rl in pairs] + [(lh, rl) for lh, ll, rh_, rl in pairs] + [
                    (ll, rh_) for lh, ll, rh_, rl in pairs]
                for i, (x, y) in enumerate(terms):
                    mm = pe.matmul(out_, x, y, start=first and i == 0, stop=last and i == len(terms) - 1)
                return mm

            def early(b, par, part):
                if part - 1 in TILES:
                    pe.wait_ge(s["normed_ready"], b * len(TILES) + part - 1)
                    after(pe, s["features_ready"], b * len(TILES) + part - 2)
                    after(pe, s["combine_turned_ready"], b * 2)
                    for i, t in enumerate(TILES[part - 1]):
                        for k in range(KD):
                            mm = pe.transpose(ps_turn[:, i, k, :], normed[:, t % 2, k * P:(k + 1) * P], a.ident[:, :])
                    mm.then_inc(s["turned"], 1)
                if part in (TURN, TURN + 1):
                    h = part - TURN
                    pe.wait_ge(s["combine_ready"], b + 1)
                    after(pe, s["combine_turned_ready"], b * 2 + h)
                    for i in range(HEADS[h]):
                        mm = pe.transpose(turned_tiles[0:SLOTS, i, :], combine[:, par, h * HEADS[0] + i, :],
                                          a.ident[:, :])
                    mm.then_inc(s["combine_turn"], 1)

            def late(b, par, part):
                if part == ROUTE:
                    pe.wait_ge(s["features_ready"], b * len(TILES) + len(TILES))
                    after(pe, s["combine_ready"], b)
                if moe.router_hidden and part in (ROUTE + 1, ROUTE + 2):
                    h = part - ROUTE - 1
                    pe.wait_ge(s["rh_read"], b * 2 + (h + 1))
                    for i in range(HEADS[h]):
                        mm = pe.matmul(route_logits[:, h * HEADS[0] + i, 0:NE], rh[:, i * P:(i + 1) * P], r_out[:, :],
                                       start=True, stop=True)
                    mm.then_inc(s["half_routed"], 1)
                if moe.router_hidden and part in (ROUTE, ROUTE + 1):
                    h = part - ROUTE
                    c0, n = h * WIDE, HEADS[h] * P
                    after(pe, s["rh_read"], b * 2 + h)
                    triple(ps_route[:, 0:n],
                           [(r_hi[:, k, :], r_lo[:, k, :], f_hi[:, par, k, c0:c0 + n], f_lo[:, par, k, c0:c0 + n])
                            for k in range(KD)]).then_inc(s["rh_ready"], 1)
                if not moe.router_hidden and part == ROUTE:
                    for t in range(BT):
                        c = slice(t * P, (t + 1) * P)
                        mm = triple(route_logits[:, t, :],
                                    [(f_hi[:, par, k, c], f_lo[:, par, k, c], r_hi[:, k, :], r_lo[:, k, :])
                                     for k in range(KD)])
                    mm.then_inc(s["half_routed"], 2)

            def hidden(b, par, l, u):
                e, h = UNITS[u]
                c0, n = h * WIDE, HEADS[h] * P
                if l > 0:
                    pe.wait_ge(split[l - 1], b * (2 * NU) + 2 * (u + 1))
                for m in range(KD):
                    c = b * (2 * NU) + (2 * u + m)
                    after(pe, evac[l], c - 1)
                    cols = slice(m * P, (m + 1) * P)
                    x = [(f_hi[:, par, k, c0:c0 + n], f_lo[:, par, k, c0:c0 + n]) if l == 0 else
                         (h_hi[l - 1][:, u % 2, k, 0:n], h_lo[l - 1][:, u % 2, k, 0:n]) for k in range(KD)]
                    triple(ps_h[l][m][:, 0:n],
                           [(w_hi[:, e, l, k, cols], w_lo[:, e, l, k, cols], *x[k]) for k in range(KD)]
                           ).then_inc(prod[l], 1)

            def bias_products(b, par):
                pe.wait_ge(s["combine_turned_ready"], b * 2 + 2)
                for j, tiles in enumerate(PAIRS):
                    if j < 2:
                        after(pe, s["out_added"], b * (2 * NU))
                    else:
                        pe.wait_ge(s["bias_added"], b * len(PAIRS) + j - 1)
                    for i, t in enumerate(tiles):
                        mm = pe.matmul(ps_out[j % 2][:, i, :], combine_turned[0:NE, t, :], out_bias[:, :],
                                       start=True, stop=True)
                    mm.then_inc(s["bias_product"], 1)

            def output(b, par, u):
                e, h = UNITS[u]
                pe.wait_ge(split[NH - 1], b * (2 * NU) + 2 * (u + 1))
                if u == 0:
                    pe.wait_ge(s["bias_added"], b * len(PAIRS) + len(PAIRS))
                for j in range(2):
                    q = out_count(b, u) + j
                    if u > 0:
                        pe.wait_ge(s["out_added"], q - 1)
                    for i, t in enumerate(PAIRS[2 * h + j]):
                        c = slice((2 * j + i) * P, (2 * j + i + 1) * P)
                        mm = triple(ps_out[j][:, i, :],
                                    [(h_hi[NH - 1][:, u % 2, k, c], h_lo[NH - 1][:, u % 2, k, c],
                                      w_hi[:, e, NL - 1, k, :], w_lo[:, e, NL - 1, k, :]) for k in range(KD)])
                    mm.then_inc(s["out_product"], 1)

            def body(b, par):
                stream(b, lambda l, u: hidden(b, par, l, u), lambda u: output(b, par, u),
                       lambda b_: bias_products(b, par), 1 - par, early, late)

            prologue(early, late, lambda n: None)
            pe.wait_ge(s["weight_used"], len(MATS))
            in_pairs(pe, 0, 1, 5, NB, body)


def project(nc, a, w):
    F32R = mybir.dt.float32r
    PAIRS = [(0, 1), (2, 3), (4, 5), (6,)]
    NPAIR = len(PAIRS)
    with Stage(nc, "proj") as st:
        w_raw = st.sbuf("w_raw", [P, KD, D])
        w_hi = st.sbuf("w_hi", [P, KD, D], F32R)
        w_lo = st.sbuf("w_lo", [P, KD, D], F32R)
        att = st.sbuf("att", [P, 2, D])
        stats = st.sbuf("stats", [P, BT, 6])
        moments = st.sbuf("moments", [P, BT, 4])
        normed = st.sbuf("normed", [P, 2, 2, D])
        f_hi = st.sbuf("f_hi", [P, 2, 2, KD, P], F32R)
        f_lo = st.sbuf("f_lo", [P, 2, 2, KD, P], F32R)
        terms = st.sbuf("terms", [P, 2, 2, 2, D])
        logit = st.sbuf("logit", [P, 2, 2, 2 * H])
        turn = [st.psum(f"turn{i}", [P, 2, KD, P]) for i in range(2)]
        ps_h = [st.psum(f"ps_h{i}", [P, 2, D]) for i in range(2)]
        weights_in, w_hi_ready, w_ready, own, settled = (
            st.sem("weights_in"), st.sem("w_hi_ready"), st.sem("w_ready"), st.sem("own"), st.sem("settled"))
        var, scale, normed_ready, turned, hi_ready, f_ready, h_ready, h_copied, terms_ready, logit_ready, pair_done = (
            st.sem(n) for n in ("var", "scale", "normed_ready", "turned", "hi_ready", "f_ready", "h_ready", "h_copied",
                                "terms_ready", "logit_ready", "pair_done"))
        spare_cleared, stored, pool_begun = st.sem("spare_cleared"), st.sem("stored"), st.sem("pool_begun")
        block = st.stack.enter_context(nc.Block())
        node = lambda b, t: a.nodes[:, ds(b * BT + t, 1), :].rearrange("p o d -> p (o d)")

        def blocks(eng, body):
            with eng.Fori(0, NB) as b:
                body(b)

        @block.sync
        def _(sp):
            sp.dma_start(w_raw[:, :, :], w["L1_gnn_W"].rearrange("(k p) n -> p k n", p=P)).then_inc(weights_in, 16)
            for i, name in enumerate(("L1_gnn_att_src", "L1_gnn_att_dst")):
                sp.dma_start(att[:, i, :], w[name].to_broadcast([P, D])).then_inc(weights_in, 16)
            rows = a.projected_dram.ap().rearrange("(t p) d -> p t d", p=P)
            logits = a.logit_dram.ap().rearrange("(t p) d -> p t d", p=P)

            def store(b):
                sp.wait_ge(pair_done, b * NPAIR + NPAIR)
                sp.dma_start(rows[:, ds(b * BT, BT), :], a.sums[:, ds(b * BT, BT), :]).then_inc(stored, 16)
                with nc.allow_non_contiguous_dma(reason="the heads' logits of each node"):
                    sp.dma_start(logits[:, ds(b * BT, BT), :], a.sums[:, ds(b * BT, BT), D:W1H]).then_inc(stored, 16)

            blocks(sp, store)
            sp.wait_ge(stored, 16 * 2 * NB)

        @block.gpsimd
        def _(pool):
            pool.memset(a.sums[:, SPARE, :], 0.0).then_inc(spare_cleared, 1)
            pool.memset(a.attention[:, :, :], 0.0).then_inc(spare_cleared, 1)

            def tiles(b):
                for j, ts in enumerate(PAIRS):
                    i, n = j % 2, len(ts)
                    pool.wait_ge(h_copied, b * NPAIR + j + 1)
                    if j >= 2:
                        pool.wait_ge(logit_ready, b * NPAIR + j - 1)
                    for k, t in enumerate(ts):
                        h = a.sums[:, ds(b * BT + t, 1), 0:D]
                        last = pool.tensor_tensor(terms[:, i, k, :, :], h.to_broadcast([P, 2, D]), att[:, :, :], ALU.mult)
                    last.then_inc(terms_ready, 1)

            pool.wait_ge(weights_in, 16 * 3)
            blocks(pool, tiles)

        @block.scalar
        def _(act):
            act.wait_ge(weights_in, 16 * 3)
            act.activation(w_hi[:, :, :], w_raw[:, :, :], ACT.Copy).then_inc(w_hi_ready, 1)

            def tiles(b):
                act.wait_ge(var, b + 1)
                act.activation(moments[:, :, 3], moments[:, :, 2], ACT.Sqrt).then_inc(scale, 1)

                def copy_h(j):
                    ts = PAIRS[j]
                    act.wait_ge(h_ready, b * NPAIR + j + 1)
                    act.activation(a.sums[:, ds(b * BT + ts[0], len(ts)), 0:D], ps_h[j % 2][:, 0:len(ts), :], ACT.Copy
                                   ).then_inc(h_copied, 1)

                for j, ts in enumerate(PAIRS):
                    i, n = j % 2, len(ts)
                    act.wait_ge(turned, b * NPAIR + j + 1)
                    if j >= 2:
                        act.wait_ge(h_ready, b * NPAIR + j - 1)
                    act.activation(f_hi[:, i, 0:n, :, :], turn[i][:, 0:n, :, :], ACT.Copy).then_inc(hi_ready, 1)
                    if j:
                        copy_h(j - 1)
                copy_h(NPAIR - 1)

            blocks(act, tiles)

        @block.vector
        def _(dve):
            dve.wait_ge(w_hi_ready, 1)
            dve.tensor_tensor(w_lo[:, :, :], w_raw[:, :, :], w_hi[:, :, :].bitcast(F32), ALU.subtract).then_inc(w_ready, 1)
            dve.wait_ge(spare_cleared, 2)

            def tiles(b):
                o = Order(dve, own, b * (2 * BT + 1 + NPAIR))
                for t in range(BT):
                    o.mark(dve.bn_stats(stats[:, t, :], node(b, t)))
                o.wait_apart(settled)
                for t in range(BT):
                    o.mark(dve.bn_aggr(moments[:, t, 0:2], stats[:, t, :]))
                o.wait()
                o.link(dve.tensor_scalar(moments[:, :, 2], moments[:, :, 1], EPS, None, ALU.add))
                dve.reciprocal(moments[:, :, 2], moments[:, :, 2]).then_inc(var, 1)
                dve.wait_ge(scale, b + 1)

                def norm(j):
                    if j >= 2:
                        dve.wait_ge(turned, b * NPAIR + j - 1)
                    for k, t in enumerate(PAIRS[j]):
                        last = dve.tensor_scalar(normed[:, j % 2, k, :], node(b, t), moments[:, t, 0:1],
                                                 moments[:, t, 3:4], ALU.subtract, ALU.mult)
                    last.then_inc(normed_ready, 1)

                def sum_terms(j):
                    ts = PAIRS[j]
                    i, n = j % 2, len(ts)
                    dve.wait_ge(terms_ready, b * NPAIR + j + 1)
                    o.mark(dve.tensor_reduce(logit[:, i, 0:n, :],
                                             terms[:, i, 0:n, :, :].rearrange("p t a (h c) -> p t (a h) c", c=C), AX,
                                             ALU.add))
                    o.wait()
                    dve.sem_inc(logit_ready, 1)
                    rows = ds(b * BT + ts[0], n)
                    dve.tensor_copy(a.attention[:, rows, 0:H], logit[:, i, 0:n, H:2 * H])
                    dve.tensor_copy(a.sums[:, rows, D:W1H], logit[:, i, 0:n, 0:H]).then_inc(pair_done, 1)

                norm(0)
                norm(1)
                for j, ts in enumerate(PAIRS):
                    i, n = j % 2, len(ts)
                    dve.wait_ge(hi_ready, b * NPAIR + j + 1)
                    dve.tensor_tensor(f_lo[:, i, 0:n, :, :], turn[i][:, 0:n, :, :], f_hi[:, i, 0:n, :, :].bitcast(F32),
                                      ALU.subtract).then_inc(f_ready, 1)
                    if j + 2 < NPAIR:
                        norm(j + 2)
                    if j:
                        sum_terms(j - 1)
                sum_terms(NPAIR - 1)

            blocks(dve, tiles)

        @block.tensor
        def _(pe):
            pe.wait_ge(w_ready, 1)

            def tiles(b):
                def turn_pair(j):
                    pe.wait_ge(normed_ready, b * NPAIR + j + 1)
                    if j >= 2:
                        pe.wait_ge(f_ready, b * NPAIR + j - 1)
                    for k in range(len(PAIRS[j])):
                        for c in range(KD):
                            mm = pe.transpose(turn[j % 2][:, k, c, :], normed[:, j % 2, k, c * P:(c + 1) * P],
                                              a.ident[:, :])
                    mm.then_inc(turned, 1)

                turn_pair(0)
                for j, ts in enumerate(PAIRS):
                    if j + 1 < NPAIR:
                        turn_pair(j + 1)
                    i = j % 2
                    pe.wait_ge(f_ready, b * NPAIR + j + 1)
                    if j >= 2:
                        pe.wait_ge(h_copied, b * NPAIR + j - 1)
                    for k in range(len(ts)):
                        pairs = [(f_hi, w_hi), (f_hi, w_lo), (f_lo, w_hi)]
                        for q, (f, ww) in enumerate(pairs):
                            for c in range(KD):
                                mm = pe.matmul(ps_h[i][:, k, :], f[:, i, k, c, :], ww[:, c, :],
                                               start=(q == 0 and c == 0), stop=(q == 2 and c == KD - 1))
                    mm.then_inc(h_ready, 1)

            blocks(pe, tiles)


def find_maxima(nc, a, src_of_edge, dst_of_edge):
    CH = 23
    NCH = EC // CH
    assert NCH * CH == EC and NCH % 2 == 0
    with Stage(nc, "maxima") as st:
        src = st.sbuf("src", [P, EC + CH], I32)
        dst = st.sbuf("dst", [P, EC], I32)
        before = st.sbuf("before", [P, 1], I32)
        picked = st.sbuf("picked", [P, 2, CH], I32)
        got = st.sbuf("got", [P, 2, CH, H])
        logit = st.sbuf("logit", [P, EC + CH, H])
        running = st.sbuf("running", [P, EC, H])
        dest = st.sbuf("dest", [P, EC])
        dest_before = st.sbuf("dest_before", [P, 1])
        reset = st.sbuf("reset", [P, EC])
        in_first = st.sbuf("in_first", [P, EC])
        flags = st.sbuf("flags", [P, 4])
        tail = st.sbuf("tail", [P, 2, H])
        tail_rows = st.sbuf("tail_rows", [H, 2, P])
        carried = st.sbuf("carried", [H, P + 1])
        carry = st.sbuf("carry", [P, H])
        upto = st.sbuf("upto", [P, P])
        ones = st.sbuf("ones", [P, P])
        ones_nt = st.sbuf("ones_nt", [P, NT])
        before_tile = st.sbuf("before_tile", [P, NT])
        last_edge = st.sbuf("last_edge", [P, NT])
        last_edge_id = st.sbuf("last_edge_id", [P, NT], I32)
        edgeless = st.sbuf("edgeless", [P, NT])
        ps_tail = [st.psum(f"ps_tail{i}", [H, P]) for i in range(2)]
        ps_carry = st.psum("ps_carry", [P, H])
        ps_count = [st.psum(f"ps_count{i}", [P, NT]) for i in range(2)]
        edges_in, own, pool_own, picked_ready, gathers_begun, copied = (
            st.sem(n) for n in ("edges_in", "own", "pool_own", "picked_ready", "gathers_begun", "copied"))
        before_in = st.sem("before_in")
        got_in = [st.sem(f"got_in{i}") for i in range(2)]
        counts_ready, tails_ready, tail_turned, carried_ready, carry_turned, running_ready, running_stored, best_in, \
            last_ready = (st.sem(n) for n in ("counts_ready", "tails_ready", "tail_turned", "carried_ready",
                                              "carry_turned", "running_ready", "running_stored", "best_in", "last_ready"))
        block = st.stack.enter_context(nc.Block())

        @block.sync
        def _(sp):
            sp.dma_start(src[:, 0:EC], src_of_edge).then_inc(edges_in, 16)
            sp.dma_start(dst[:, :], dst_of_edge).then_inc(edges_in, 16)
            sp.wait_ge(pool_own, 1)
            with nc.allow_non_contiguous_dma(reason="the last edge of each partition but one"):
                sp.dma_start(before[1:P, :], dst_of_edge[0:P - 1, EC - 1:EC]).then_inc(before_in, 16)
            sp.wait_ge(running_ready, H)
            sp.dma_start(a.running_dram.ap().rearrange("(p e) h -> p (e h)", p=P),
                         running[:, :, :].rearrange("p e h -> p (e h)")).then_inc(running_stored, 16)

        @block.gpsimd
        def _(pool):
            pool.memset(before[:, :], -1).then_inc(pool_own, 1)
            pool.memset(ones[:, :], 1.0).then_inc(pool_own, 1)
            pool.memset(ones_nt[:, :], 1.0).then_inc(pool_own, 1)
            pool.memset(carried[:, :], LOW).then_inc(pool_own, 1)
            pool.wait_ge(pool_own, 4)
            pool.affine_select(out=upto[:, :], in_=ones[:, :], compare_op=ALU.is_ge, fill=0.0, base=0,
                               pattern=[[1, P]], channel_multiplier=-1).then_inc(pool_own, 1)
            pool.wait_ge(edges_in, 32)

            def gather(half, t, first):
                if not first:
                    pool.wait_ge(copied, t - 1)
                pool.tensor_copy(picked[:, half, :], src[:, ds(t * CH, CH)]).then_inc(picked_ready, 1)
                pool.wait_ge(picked_ready, t + 1)
                pool.sem_inc(gathers_begun, 1)
                for c in range(CH):
                    pool.indirect_dma_start(got[:, half, c, :], None, a.logit_dram.ap(),
                                            bass.IndirectOffsetOnAxis(picked[:, half, c:c + 1].bitcast(U32), 0)
                                            ).then_inc(got_in[half], 16)

            gather(0, 0, True)
            gather(1, 1, True)
            with pool.Fori(2, NCH, 2) as t:
                gather(0, t, False)
                gather(1, t + 1, False)
            pool.wait_ge(last_ready, 1)
            pool.wait_ge(running_stored, 16)
            for t in range(NT):
                pool.indirect_dma_start(a.best[:, t, :], None, a.running_dram.ap(),
                                        bass.IndirectOffsetOnAxis(last_edge_id[:, t:t + 1].bitcast(U32), 0)
                                        ).then_inc(best_in, 16)

        @block.scalar
        def _(act):
            with act.Fori(0, NCH, 2) as t:
                for half in range(2):
                    act.wait_ge(got_in[half], t * (CH * 8) + CH * 16)
                    act.activation(logit[:, ds((t + half) * CH, CH), :], got[:, half, :, :], ACT.Copy).then_inc(copied, 1)

        @block.tensor
        def _(pe):
            pe.wait_ge(pool_own, 5)
            pe.matmul(ps_count[0][:, :], upto[:, :], a.degree[:, :], start=True, stop=True).then_inc(counts_ready, 1)
            pe.matmul(ps_count[1][:, :], ones[:, :], a.degree[:, :], start=True, stop=True).then_inc(counts_ready, 1)
            pe.wait_ge(tails_ready, 1)
            for i in range(2):
                mm = pe.transpose(ps_tail[i][:, :], tail[:, i, :], a.ident[:, :])
            mm.then_inc(tail_turned, 1)
            pe.wait_ge(carried_ready, 1)
            pe.transpose(ps_carry[:, :], carried[:, 0:P], a.ident[0:H, 0:H]).then_inc(carry_turned, 1)

        @block.vector
        def _(dve):
            o = Order(dve, own)
            dve.wait_ge(counts_ready, 2)
            o.link(dve.tensor_copy(last_edge[:, :], ps_count[1][:, :]))
            dve.wait_ge(pool_own, 5)
            o.link(dve.tensor_tensor_scan(before_tile[:, :], ones_nt[:, :], last_edge[:, :], 0.0, ALU.mult, ALU.add))
            o.link(dve.tensor_tensor(before_tile[:, :], before_tile[:, :], last_edge[:, :], ALU.subtract))
            o.link(dve.tensor_tensor(last_edge[:, :], before_tile[:, :], ps_count[0][:, :], ALU.add))
            o.link(dve.tensor_scalar(last_edge[:, :], last_edge[:, :], -1.0, 0.0, ALU.add, ALU.max))
            dve.tensor_copy(last_edge_id[:, :], last_edge[:, :]).then_inc(last_ready, 1)
            o.mark(dve.tensor_scalar(edgeless[:, :], a.degree[:, :], 0.0, LOW, ALU.is_equal, ALU.mult))

            dve.wait_ge(edges_in, 32)
            dve.wait_ge(before_in, 16)
            o.mark(dve.tensor_copy(dest[:, :], dst[:, :]))
            o.link(dve.tensor_copy(dest_before[:, :], before[:, :]))
            o.mark(dve.memset(reset[:, 0:1], LOW))
            o.mark(dve.tensor_tensor(reset[:, 1:EC], dest[:, 1:EC], dest[:, 0:EC - 1], ALU.not_equal))
            o.mark(dve.tensor_scalar(in_first[:, :], dest[:, :], dest[:, 0:1], LOW, ALU.not_equal, ALU.mult))
            o.mark(dve.tensor_tensor(flags[:, 0:1], dest[:, 0:1], dest_before[:, :], ALU.not_equal))
            o.link(dve.tensor_tensor(flags[:, 1:2], dest[:, 0:1], dest[:, EC - 1:EC], ALU.not_equal))
            o.mark(dve.tensor_scalar(reset[:, 1:EC], reset[:, 1:EC], LOW, None, ALU.mult))
            o.mark(dve.tensor_scalar(flags[:, 2:3], flags[:, 0:1], LOW, None, ALU.mult))
            o.link(dve.tensor_tensor(flags[:, 3:4], flags[:, 0:1], flags[:, 1:2], ALU.max))
            o.link(dve.tensor_scalar(tail[:, 1, :], flags[:, 3:4].to_broadcast([P, H]), LOW, None, ALU.mult))

            dve.wait_ge(copied, NCH)
            for h in range(H):
                o.mark(dve.tensor_tensor_scan(running[:, :, h], reset[:, :], logit[:, 0:EC, h], LOW, ALU.add, ALU.max))
            o.wait()
            dve.tensor_copy(tail[:, 0, :], running[:, EC - 1, :]).then_inc(tails_ready, 1)
            dve.wait_ge(tail_turned, 1)
            for i in range(2):
                o.link(dve.tensor_copy(tail_rows[:, i, :], ps_tail[i][:, :]))
            dve.tensor_tensor_scan(carried[:, 1:P + 1], tail_rows[:, 1, :], tail_rows[:, 0, :], LOW, ALU.add, ALU.max
                                   ).then_inc(carried_ready, 1)
            dve.wait_ge(carry_turned, 1)
            o.link(dve.tensor_scalar(carry[:, :], ps_carry[:, :], flags[:, 2:3], None, ALU.add))
            for h in range(H):
                dve.scalar_tensor_tensor(out=running[:, :, h], in0=in_first[:, :], scalar=carry[:, h:h + 1],
                                         in1=running[:, :, h], op0=ALU.add, op1=ALU.max).then_inc(running_ready, 1)
            dve.wait_ge(best_in, 16 * NT)
            o.link(dve.tensor_tensor(a.best[:, :, :], a.best[:, :, :],
                                     edgeless[:, :, None].to_broadcast([P, NT, H]), ALU.add))


def start_softmax(nc, a):
    with Stage(nc, "start") as st:
        z = st.sbuf("z", [P, NT, H])
        own = st.sem("own")
        z_ready, p_ready = st.sem("z_ready"), st.sem("p_ready")
        block = st.stack.enter_context(nc.Block())

        @block.scalar
        def _(act):
            act.wait_ge(z_ready, 1)
            act.activation(a.sums[:, 0:NT, D:W1H], z[:, :, :], ACT.Exp).then_inc(p_ready, 1)

        @block.vector
        def _(dve):
            o = Order(dve, own)
            source = a.sums[:, 0:NT, D:W1H]
            ad, top = a.attention[:, 0:NT, 0:H], a.attention[:, 0:NT, H:2 * H]
            o.link(dve.tensor_tensor(top, a.best[:, :, :], source, ALU.max))
            o.mark(dve.tensor_tensor(top, top, ad, ALU.add))
            o.link(dve.tensor_tensor(z[:, :, :], source, ad, ALU.add))
            o.mark(dve.scalar_tensor_tensor(out=top, in0=top, scalar=SLOPE, in1=top, op0=ALU.mult, op1=ALU.max))
            o.link(dve.scalar_tensor_tensor(out=z[:, :, :], in0=z[:, :, :], scalar=SLOPE, in1=z[:, :, :],
                                            op0=ALU.mult, op1=ALU.max))
            dve.tensor_tensor(z[:, :, :], z[:, :, :], top, ALU.subtract).then_inc(z_ready, 1)
            dve.wait_ge(p_ready, 1)
            for h in range(H):
                x = a.sums[:, 0:NT, h * C:(h + 1) * C]
                o.mark(dve.tensor_tensor(x, x, a.sums[:, 0:NT, D + h:D + h + 1].to_broadcast([P, NT, C]), ALU.mult))
            o.wait()


def attend(nc, a):
    with Stage(nc, "att") as st:
        tables = WalkTables(st, a, weights=False)
        rows = st.sbuf("rows", [P, RING, GE, W1H])
        picked = st.sbuf("picked", [P, 4, U * GE], I32)
        hot = st.sbuf("hot", [P, RING, GE, P], mybir.dt.float32r)
        ident = st.sbuf("ident", [P, P], mybir.dt.float32r)
        hot_turned = st.sbuf("hot_turned", [P, 2, GE, P], mybir.dt.float32r)
        table = st.sbuf("table", [P, NT + 1, 2, 2 * H], mybir.dt.float32r)
        node_logits = st.sbuf("node_logits", [P, 2, GE, 2 * H])
        z = st.sbuf("z", [P, 2, GE, H])
        ps_hot = [st.psum(f"ps_hot{i}", [P, GE, P], mybir.dt.float32r) for i in range(2)]
        ps_logit = [st.psum(f"ps_logit{i}", [P, GE, 2, 2 * H]) for i in range(2)]
        part = [st.psum(f"part{i}", [P, W1H]) for i in range(2)]
        rows_in = [st.sem(f"rows_in{i}") for i in range(RING)]
        picked_ready, gathers_begun, table_ready, hot_ready, turned, turned_copied, logit_ready, parts_summed, \
            source_added, bent, z_ready, p_ready, weighted, \
            product_ready, added = (st.sem(n) for n in (
                "picked_ready", "gathers_begun", "table_ready", "hot_ready", "turned", "turned_copied", "logit_ready", "parts_summed",
                "source_added", "bent",
                "z_ready", "p_ready", "weighted", "product_ready", "added"))
        block = st.stack.enter_context(nc.Block())
        src_of = tables.src[:, :, :].rearrange("p s g -> p (s g)")

        def steps(eng, lags, after_last):
            end = max(lags)

            def run(i, u, stages):
                for lag, stage in zip(lags, stages):
                    if isinstance(i, int) and not 0 <= i - lag < STEPS:
                        continue
                    stage(i - lag, (u - lag) % RING)

            for u in range(RING):
                run(u, u, after_last)
            with eng.Fori(1, STEPS // RING) as t:
                for u in range(RING):
                    run(t * RING + u, u, after_last)
            for u in range(end):
                run(STEPS + u, u, after_last)

        def landed(eng, s, u):
            if isinstance(s, int):
                eng.wait_ge(rows_in[u], 16 * GE * (s // RING + 1))
            else:
                eng.wait_ge(rows_in[u], (s - u) * (16 * GE // RING) + 16 * GE)

        @block.sync
        def _(sp):
            tables.load(sp)

        @block.gpsimd
        def _(pool):
            pool.wait_ge(tables.loaded, tables.count)

            def gather(at, t):
                half, first = at % 2, isinstance(t, int) and t < 2
                pool.tensor_copy(picked[:, at, :],
                                 src_of[:, ds(t * (U * GE), U * GE)]).then_inc(picked_ready, 1)
                pool.wait_ge(picked_ready, t + 1)
                pool.sem_inc(gathers_begun, 1)
                for u in range(U):
                    if not first and u % 2 == 0:
                        pool.wait_ge(product_ready, t * U + u + 2 - RING)
                        pool.sem_inc(gathers_begun, 1)
                    for g in range(GE):
                        pool.indirect_dma_start(
                            rows[:, half * U + u, g, :], None, a.projected_dram.ap(),
                            bass.IndirectOffsetOnAxis(picked[:, at, u * GE + g:u * GE + g + 1].bitcast(U32), 0)
                        ).then_inc(rows_in[half * U + u], 16)

            gather(0, 0)
            gather(1, 1)
            with pool.Fori(2, STEPS // U, 4) as t:
                for n in range(4):
                    gather((2 + n) % 4, t + n)

        @block.scalar
        def _(act):
            def copy_turned(s, u):
                act.wait_ge(turned, s + 1)
                after(act, logit_ready, s - 1)
                act.activation(hot_turned[:, u % 2, :, :], ps_hot[u % 2][:, :, :], ACT.Copy).then_inc(turned_copied, 1)

            def exponent(s, u):
                act.wait_ge(z_ready, s + 1)
                act.activation(rows[:, u, :, D:W1H], z[:, u % 2, :, :], ACT.Exp).then_inc(p_ready, 1)

            steps(act, (1, 2), (copy_turned, exponent))

        @block.vector
        def _(dve):
            def one_hot(s, u):
                after(dve, product_ready, s + 1 - RING)
                d = tables.dst[:, ds(s, 1), :].rearrange("p o g -> p (o g)")
                dve.tensor_tensor(hot[:, u, :, :], a.columns[:, None, :].to_broadcast([P, GE, P]),
                                  d[:, :, None].to_broadcast([P, GE, P]), ALU.is_equal).then_inc(hot_ready, 1)

            def sum_parts(s, u):
                dve.wait_ge(logit_ready, s + 1)
                dve.tensor_reduce(node_logits[:, u % 2, :, :], ps_logit[u % 2][:, :, :, :].rearrange("p g k d -> p g d k"),
                                  AX, ALU.add).then_inc(parts_summed, 1)

            def add_source(s, u):
                dve.wait_ge(parts_summed, s + 1)
                landed(dve, s, u)
                dve.tensor_tensor(z[:, u % 2, :, :], rows[:, u, :, D:W1H], node_logits[:, u % 2, :, 0:H], ALU.add
                                  ).then_inc(source_added, 1)

            def bend(s, u):
                dve.wait_ge(source_added, s + 1)
                zz = z[:, u % 2, :, :]
                dve.scalar_tensor_tensor(out=zz, in0=zz, scalar=SLOPE, in1=zz, op0=ALU.mult, op1=ALU.max
                                         ).then_inc(bent, 1)

            def subtract_maximum(s, u):
                dve.wait_ge(bent, s + 1)
                zz = z[:, u % 2, :, :]
                dve.tensor_tensor(zz, zz, node_logits[:, u % 2, :, H:2 * H], ALU.subtract).then_inc(z_ready, 1)

            def weigh(s, u):
                dve.wait_ge(p_ready, s + 1)
                x = rows[:, u, :, 0:D].rearrange("p g (h c) -> p g h c", c=C)
                p = rows[:, u, :, D:W1H]
                dve.tensor_tensor(x, x, p[:, :, :, None].to_broadcast([P, GE, H, C]), ALU.mult).then_inc(weighted, 1)

            def add(s, u):
                j = dve.value_load(tables.tile[0:1, ds(s, 1)], min_val=0, max_val=SPARE)
                dve.wait_ge(product_ready, s + 1)
                after(dve, added, s)
                total = a.sums[:, ds(j, 1), :].rearrange("p o d -> p (o d)")
                dve.tensor_tensor(total, total, part[u % 2][:, :], ALU.add).then_inc(added, 1)

            dve.tensor_copy(ident[:, :], a.ident[:, :]).then_inc(table_ready, 1)
            dve.tensor_copy(table[:, :, 0, :], a.attention[:, :, :]).then_inc(table_ready, 1)
            dve.wait_ge(table_ready, 2)
            dve.tensor_tensor(table[:, :, 1, :], a.attention[:, :, :], table[:, :, 0, :].bitcast(F32), ALU.subtract
                              ).then_inc(table_ready, 1)
            dve.wait_ge(tables.loaded, tables.count)
            steps(dve, (2, 0, 2, 5, 2, 3, 2),
                  (sum_parts, one_hot, add_source, add, bend, weigh, subtract_maximum))

        @block.tensor
        def _(pe):
            def spread(s, u):
                j = pe.value_load(tables.tile[0:1, ds(s, 1)], min_val=0, max_val=SPARE)
                pe.wait_ge(turned_copied, s + 1)
                after(pe, z_ready, s - 1)
                for g in range(GE):
                    mm = pe.matmul(ps_logit[u % 2][:, g, :, :].rearrange("p k d -> p (k d)"),
                                   hot_turned[:, u % 2, g, :],
                                   table[:, ds(j, 1), :, :].rearrange("p o k d -> p (o k d)"), start=True, stop=True)
                mm.then_inc(logit_ready, 1)

            def turn(s, u):
                pe.wait_ge(hot_ready, s + 1)
                after(pe, turned_copied, s - 1)
                for g in range(GE):
                    mm = pe.transpose(ps_hot[u % 2][:, g, :], hot[:, u, g, :], ident[:, :])
                mm.then_inc(turned, 1)

            def product(s, u):
                pe.wait_ge(weighted, s + 1)
                after(pe, added, s - 1)
                for g in range(GE):
                    mm = pe.matmul(part[u % 2][:, :], hot[:, u, g, :].bitcast(F32), rows[:, u, g, :],
                                   start=(g == 0), stop=(g == GE - 1))
                mm.then_inc(product_ready, 1)

            pe.wait_ge(table_ready, 3)
            pe.wait_ge(tables.loaded, tables.count)
            steps(pe, (2, 1, 4), (spread, turn, product))


def finish_attention(nc, a, w):
    with Stage(nc, "fin") as st:
        bias = st.sbuf("bias", [P, D])
        share = st.sbuf("share", [P, NT, H])
        own, bias_in = st.sem("own"), st.sem("bias_in")
        block = st.stack.enter_context(nc.Block())

        @block.sync
        def _(sp):
            sp.dma_start(bias[:, :], w["L1_gnn_bias"].to_broadcast([P, D])).then_inc(bias_in, 16)

        @block.vector
        def _(dve):
            o = Order(dve, own)
            o.link(dve.tensor_scalar(share[:, :, :], a.sums[:, 0:NT, D:W1H], 1e-16, None, ALU.add))
            o.link(dve.reciprocal(share[:, :, :], share[:, :, :]))
            dve.wait_ge(bias_in, 16)
            for h in range(H):
                x = a.sums[:, 0:NT, h * C:(h + 1) * C]
                o.mark(dve.tensor_tensor(x, x, share[:, :, h:h + 1].to_broadcast([P, NT, C]), ALU.mult))
            o.wait()
            x = a.sums[:, 0:NT, 0:D]
            o.link(dve.tensor_tensor(x, x, bias[:, None, :].to_broadcast([P, NT, D]), ALU.add))
            o.link(dve.scalar_tensor_tensor(out=a.nodes[:, :, :], in0=x, scalar=0.0, in1=a.nodes[:, :, :],
                                            op0=ALU.max, op1=ALU.add))


def first_mixture(w):
    n = "L0_ffn_"
    return Mixture(E0, 2, ACT.Relu, True, False, [w[n + "expert_w1"], w[n + "expert_w2"], w[n + "expert_w3"]],
                   [w[n + "expert_b1"], w[n + "expert_b2"]], w[n + "expert_b3"],
                   [w[n + "router_w1"], w[n + "router_b1"], w[n + "router_w2"], w[n + "router_b2"]])


def second_mixture(w):
    n = "L1_ffn_"
    return Mixture(E1, 1, ACT.Gelu, False, True, [w[n + "w1"], w[n + "w2"]], [w[n + "b1"]], w[n + "b2"],
                   [w[n + "router_w"]])




def program(nc, aps):
    with ExitStack() as stack:
        a = Arena(nc, stack)
        make_constants(nc, a)
        plan_walk(nc, a, aps["src"], aps["dst"], aps["edge_weight"])
        with a.edge_sums("sums"):
            normalize_input(nc, a, aps["x"])
            aggregate_messages(nc, a)
            convolve(nc, a, aps["x"], aps)
        mix(nc, a, "mix0", first_mixture(aps), aps)
        with a.edge_sums("attention_sums"), a.attention_tables():
            project(nc, a, aps)
            find_maxima(nc, a, aps["src_of_edge"], aps["dst_of_edge"])
            start_softmax(nc, a)
            attend(nc, a)
            finish_attention(nc, a, aps)
        mix(nc, a, "mix1", second_mixture(aps), aps, out=aps["out"])


def lay_out(inputs):
    import numpy as np

    more_edges, more_nodes = EP - E, NP - N
    edges = {
        "src": np.pad(inputs["src"], (0, more_edges)),
        "dst": np.pad(inputs["dst"], (0, more_edges), constant_values=PAD_DST),
        "edge_weight": np.pad(inputs["edge_weight"], (0, more_edges)),
    }
    out = {name: x.reshape(NG, GE * P) for name, x in edges.items()}
    out["src_of_edge"] = edges["src"].reshape(P, EC)
    out["dst_of_edge"] = edges["dst"].reshape(P, EC)
    out["x"] = np.pad(inputs["x"], ((0, more_nodes), (0, 0)))
    for name in ("L0_gnn_W_rel", "L0_gnn_W_root"):
        out[name] = inputs[name].transpose(2, 0, 1).reshape(D, LAYERS * D)
    for name in ("L0_gnn_W1", "L0_gnn_W2", "L1_ffn_router_w"):
        out[name] = inputs[name].T
    for name in ("L0_gnn_b_rel", "L0_gnn_ln_g", "L0_gnn_ln_b", "L0_gnn_b1", "L0_gnn_mg1", "L0_gnn_mb1", "L0_gnn_b2",
                 "L0_gnn_mg2", "L0_gnn_mb2", "L0_ffn_router_b2", "L1_gnn_att_src", "L1_gnn_att_dst", "L1_gnn_bias"):
        out[name] = inputs[name].reshape(1, -1)
    out["L0_ffn_router_b1"] = inputs["L0_ffn_router_b1"].reshape(-1, 1)
    for name in ("L0_ffn_expert_b1", "L0_ffn_expert_b2", "L1_ffn_b1"):
        out[name] = inputs[name].reshape(-1, KD, P).transpose(2, 0, 1)
    for name in ("L0_ffn_router_w1", "L0_ffn_router_w2", "L0_ffn_expert_w1", "L0_ffn_expert_w2", "L0_ffn_expert_w3",
                 "L0_ffn_expert_b3", "L1_gnn_W", "L1_ffn_w1", "L1_ffn_w2", "L1_ffn_b2"):
        out[name] = inputs[name]
    return {name: np.ascontiguousarray(x) for name, x in out.items()}


def kernel(**inputs):
    import concourse.bacc as bacc
    import numpy as np
    from concourse.bass_utils import run_bass_kernel_spmd

    nc = bacc.Bacc("TRN2", target_bir_lowering=False, num_devices=1)
    arrays = lay_out({name: np.asarray(x) for name, x in inputs.items()})
    aps = {name: nc.dram_tensor(name, x.shape, mybir.dt.from_np(x.dtype), kind="ExternalInput").ap()
           for name, x in arrays.items()}
    aps["out"] = nc.dram_tensor("out", (NP, D), F32, kind="ExternalOutput").ap()
    program(nc, aps)
    result = run_bass_kernel_spmd(nc, [arrays], core_ids=[0])
    return result.results[0]["out"][:N]
```

```python
from contextlib import ExitStack, contextmanager

import concourse.bass as bass
from concourse import mybir

ALU = mybir.AluOpType
ACT = mybir.ActivationFunctionType
AX = mybir.AxisListType.X
F32 = mybir.dt.float32
I32 = mybir.dt.int32
U32 = mybir.dt.uint32

P = 128
N = 6250
E = 100000
D = 256
KD = D // P
NT = -(-N // P)
NP = NT * P
BT = 7
NB = NT // BT
BN = BT * P
HALF = BN // 2
EC = -(-E // P)
EP = EC * P
GE = 2
NG = EP // (GE * P)
U = 5
RING = 2 * U
SPARE = NT
HOT = RING // 2
STEPS = -(-(NG + NT - 1) // RING) * RING
SB = -(-STEPS // P)
SW = SB * P
PAD_DST = NP + 10 * P
LAYERS = 4
H, C = 4, 64
W1H = D + H
E0, R0 = 6, 128
E1 = 8
EPS = 1e-5
SLOPE = 0.2
LOW = -1e30
ds = bass.ds


class Arena:

    def __init__(self, nc, stack):
        self.nc, self.stack = nc, stack
        sb = self.sbuf
        self.nodes = sb("nodes", [P, NT, D], F32)
        self.degree = sb("degree", [P, NT])
        self.ident = sb("ident", [P, P], F32)
        self.columns = sb("columns", [P, P], F32)
        self.ones_row = sb("ones_row", [1, P], F32)
        self.ones_col = sb("ones_col", [P, 1], F32)
        self.step_src_dram = nc.dram_tensor("step_src", [P, SW, GE], I32)
        self.step_dst_dram = nc.dram_tensor("step_dst", [P, SW, GE], F32)
        self.step_weight_dram = nc.dram_tensor("step_weight", [P, SW, GE], F32)
        self.step_tile_dram = nc.dram_tensor("step_tile", [1, SW], I32)
        self.normed_dram = nc.dram_tensor("normed", [NP, D], F32)
        self.projected_dram = nc.dram_tensor("projected", [NP, W1H], F32)
        self.logit_dram = nc.dram_tensor("source_logit", [NP, H], F32)
        self.running_dram = nc.dram_tensor("running_max", [EP, H], F32)

    def sbuf(self, name, shape, dtype=F32):
        return self.stack.enter_context(self.nc.sbuf_tensor(name, shape, dtype))

    @contextmanager
    def edge_sums(self, name):
        with self.nc.sbuf_tensor(name, [P, NT + 1, W1H], F32) as self.sums:
            yield

    @contextmanager
    def attention_tables(self):
        sb = self.nc.sbuf_tensor
        with (
            sb("attention", [P, NT + 1, 2 * H], F32) as self.attention,
            sb("best", [P, NT, H], F32) as self.best,
        ):
            yield


class Stage:

    def __init__(self, nc, name):
        self.nc, self.name, self.stack, self.sems = nc, name, ExitStack(), []

    def __enter__(self):
        return self

    def __exit__(self, *error):
        self.stack.__exit__(*error)
        if error[0] is None:
            self.nc.clear_and_free_semaphores(self.sems)
            self.nc.all_engine_barrier()

    def sbuf(self, name, shape, dtype=F32):
        return self.stack.enter_context(self.nc.sbuf_tensor(f"{self.name}_{name}", shape, dtype))

    def psum(self, name, shape, dtype=F32):
        return self.stack.enter_context(self.nc.psum_tensor(f"{self.name}_{name}", shape, dtype))

    def sem(self, name):
        self.sems.append(self.nc.alloc_semaphore(f"{self.name}_{name}"))
        return self.sems[-1]


class Order:

    def __init__(self, eng, sem, base=0):
        self.eng, self.sem, self.base, self.n = eng, sem, base, 0

    def mark(self, ins):
        ins.then_inc(self.sem, 1)
        self.n += 1

    def wait(self):
        self.eng.wait_ge(self.sem, self.base + self.n)

    def wait_apart(self, settled):
        self.wait()
        self.eng.sem_inc(settled, 1)

    def link(self, ins):
        self.mark(ins)
        self.wait()


def make_constants(nc, a):
    with Stage(nc, "const") as st:
        index = st.sbuf("index", [P, P], I32)
        filled = st.sem("filled")
        block = st.stack.enter_context(nc.Block())

        @block.gpsimd
        def _(pool):
            o = Order(pool, filled)
            o.mark(pool.memset(a.ones_row[:, :], 1.0))
            o.mark(pool.memset(a.ones_col[:, :], 1.0))
            o.mark(pool.iota(index[:, :], [[1, P]], base=0, channel_multiplier=0))
            o.link(pool.memset(a.ident[:, :], 0.0))
            o.mark(pool.tensor_copy(a.columns[:, :], index[:, :]))
            o.link(pool.affine_select(out=a.ident[:, :], in_=a.ident[:, :], compare_op=ALU.not_equal, fill=1.0,
                                      base=0, pattern=[[-1, P]], channel_multiplier=1))


class InputNorm:

    def __init__(self, st, a, x):
        self.a, self.x = a, x.rearrange("(t p) d -> p t d", p=P)
        self.stats = st.sbuf("stats", [P, NT, 6])
        self.moments = st.sbuf("moments", [P, NT, 4])
        self.x_in = [st.sem(f"x_in{b}") for b in range(NB)]
        self.own, self.settled, self.var, self.scale, self.normed, self.stored = (
            st.sem(f"norm_{n}") for n in ("own", "settled", "var", "scale", "normed", "stored"))

    def load(self, sp):
        for b in range(NB):
            at = slice(b * BT, (b + 1) * BT)
            sp.dma_start(self.a.nodes[:, at, :], self.x[:, at, :]).then_inc(self.x_in[b], 16)

    def measure_and_scale(self, dve):
        o, m, nodes = Order(dve, self.own), self.moments, self.a.nodes
        for b in range(NB):
            dve.wait_ge(self.x_in[b], 16)
            for t in range(b * BT, (b + 1) * BT):
                o.mark(dve.bn_stats(self.stats[:, t, :], nodes[:, t, :]))
        o.wait_apart(self.settled)
        for t in range(NT):
            o.mark(dve.bn_aggr(m[:, t, 0:2], self.stats[:, t, :]))
        o.wait()
        o.link(dve.tensor_scalar(m[:, :, 2], m[:, :, 1], EPS, None, ALU.add))
        dve.reciprocal(m[:, :, 2], m[:, :, 2]).then_inc(self.var, 1)
        dve.wait_ge(self.scale, 1)
        for b in range(NB):
            for t in range(b * BT, (b + 1) * BT):
                last = dve.tensor_scalar(nodes[:, t, :], nodes[:, t, :], m[:, t, 0:1], m[:, t, 3:4],
                                         ALU.subtract, ALU.mult)
            last.then_inc(self.normed, 1)

    def root(self, act):
        act.wait_ge(self.var, 1)
        act.activation(self.moments[:, :, 3], self.moments[:, :, 2], ACT.Sqrt).then_inc(self.scale, 1)

    def store(self, sp):
        out = self.a.normed_dram.ap().rearrange("(t p) d -> p t d", p=P)
        for b in range(NB):
            at = slice(b * BT, (b + 1) * BT)
            sp.wait_ge(self.normed, b + 1)
            sp.dma_start(out[:, at, :], self.a.nodes[:, at, :]).then_inc(self.stored, 16)


def plan_walk(nc, a, src, dst, weight, x):
    with Stage(nc, "plan") as st:
        last = st.sbuf("last", [1, NG], I32)
        last_tile = st.sbuf("last_tile", [1, NG], I32)
        ends = st.sbuf("ends", [1, NG])
        group_index = st.sbuf("group_index", [1, NG], I32)
        group_number = st.sbuf("group_number", [1, NG])
        ends_all = st.sbuf("ends_all", [P, NG])
        step_index = st.sbuf("step_index", [P, SB], I32)
        step_number = st.sbuf("step_number", [P, SB])
        ended = st.sbuf("ended", [P, SB, NG])
        group = st.sbuf("group", [P, SB])
        group_id = st.sbuf("group_id", [P, SB], I32)
        tile = st.sbuf("tile", [P, SB])
        tile_base = st.sbuf("tile_base", [P, SB])
        ints = st.sbuf("ints", [P, 2, SB, GE * P], I32)
        rows = st.sbuf("rows", [P, 3, SB, GE * P])
        step_src = st.sbuf("step_src", [P, SW, GE], I32)
        step_dst = st.sbuf("step_dst", [P, SW, GE])
        step_weight = st.sbuf("step_weight", [P, SW, GE])
        step_tile = st.sbuf("step_tile", [1, SW], I32)
        tables_ready, tables_stored = st.sem("tables_ready"), st.sem("tables_stored")
        spread = st.psum("spread", [P, NG])
        turned = [st.psum(f"turned{k}", [P, 4, P]) for k in range(2)]
        tile_row = st.psum("tile_row", [1, SW])
        last_in, numbered, own = st.sem("last_in"), st.sem("numbered"), st.sem("own")
        ends_ready, spread_ready, group_ready = st.sem("ends_ready"), st.sem("spread_ready"), st.sem("group_ready")
        rows_in, rows_ready, turned_ready, turned_used = (
            st.sem("rows_in"), st.sem("rows_ready"), st.sem("turned_ready"), st.sem("turned_used"))
        tile_ready, tile_row_ready = st.sem("tile_ready"), st.sem("tile_row_ready")
        sums_cleared = st.sem("sums_cleared")
        norm = InputNorm(st, a, x)
        block = st.stack.enter_context(nc.Block())
        tables = [src, dst, weight]
        turns = [(t, g) for t in range(3) for g in range(GE)]

        @block.sync
        def _(sp):
            with nc.allow_non_contiguous_dma(reason="one element of each edge group"):
                sp.dma_start(last[:, :], dst[:, GE * P - 1:GE * P].rearrange("g o -> o g")).then_inc(last_in, 16)
            norm.load(sp)
            norm.store(sp)
            sp.wait_ge(tables_ready, 1)
            sp.wait_ge(turned_used, len(turns))
            for out, table in ((a.step_src_dram, step_src), (a.step_dst_dram, step_dst),
                               (a.step_weight_dram, step_weight), (a.step_tile_dram, step_tile)):
                sp.dma_start(out.ap(), table.ap()).then_inc(tables_stored, 16)
            sp.wait_ge(tables_stored, 16 * 4)
            sp.wait_ge(norm.stored, 16 * NB)

        @block.scalar
        def _(act):
            norm.root(act)

        @block.gpsimd
        def _(pool):
            o = Order(pool, numbered)
            o.mark(pool.iota(group_index[:, :], [[1, NG]], base=0, channel_multiplier=0))
            o.link(pool.iota(step_index[:, :], [[P, SB]], base=0, channel_multiplier=1))
            o.mark(pool.tensor_copy(group_number[:, :], group_index[:, :]))
            o.mark(pool.tensor_copy(step_number[:, :], step_index[:, :]))
            pool.wait_ge(group_ready, 1)
            for t, table in enumerate(tables):
                for k in range(SB):
                    out = ints[:, t, k, :] if t < 2 else rows[:, 2, k, :]
                    pool.indirect_dma_start(
                        out, None, table, bass.IndirectOffsetOnAxis(group_id[:, k:k + 1].bitcast(U32), 0)
                    ).then_inc(rows_in, 16)
            pool.memset(a.sums[:, :, :], 0.0).then_inc(sums_cleared, 1)
            pool.wait_ge(sums_cleared, 1)

        @block.vector
        def _(dve):
            o = Order(dve, own)
            dve.wait_ge(last_in, 16)
            o.link(dve.tensor_scalar(last_tile[:, :], last[:, :], 7, None, ALU.arith_shift_right))
            o.link(dve.tensor_scalar(ends[:, :], last_tile[:, :], float(NT - 1), None, ALU.min))
            dve.wait_ge(numbered, 4)
            dve.tensor_tensor(ends[:, :], ends[:, :], group_number[:, :], ALU.add).then_inc(ends_ready, 1)
            dve.wait_ge(spread_ready, 1)
            o.link(dve.tensor_copy(ends_all[:, :], spread[:, :]))
            for k in range(SB):
                o.mark(dve.tensor_scalar(ended[:, k, :], ends_all[:, :], step_number[:, k:k + 1], None, ALU.is_lt))
            o.wait()
            o.link(dve.tensor_reduce(group[:, :], ended[:, :, :], AX, ALU.add))
            o.link(dve.tensor_scalar(group[:, :], group[:, :], float(NG - 1), None, ALU.min))
            dve.tensor_copy(group_id[:, :], group[:, :]).then_inc(group_ready, 1)
            o.link(dve.tensor_tensor(tile[:, :], step_number[:, :], group[:, :], ALU.subtract))
            o.link(dve.tensor_scalar(tile[:, :], tile[:, :], float(SPARE), None, ALU.min))
            dve.tensor_scalar(tile_base[:, :], tile[:, :], float(P), None, ALU.mult).then_inc(tile_ready, 1)
            norm.measure_and_scale(dve)
            dve.wait_ge(tile_ready, 1)
            dve.wait_ge(rows_in, 16 * 3 * SB)
            o.link(dve.tensor_copy(rows[:, 0:2, :, :], ints[:, :, :, :]))
            for k in range(SB):
                dve.tensor_scalar(rows[:, 1, k, :], rows[:, 1, k, :], tile_base[:, k:k + 1], None,
                                  ALU.subtract).then_inc(rows_ready, 1)
            outs = [step_src, step_dst, step_weight]
            for n, (t, g) in enumerate(turns):
                dve.wait_ge(turned_ready, n + 1)
                dve.tensor_copy(outs[t][:, :, g].rearrange("p (k s) -> p k s", k=SB),
                                turned[n % 2][:, 0:SB, :]).then_inc(turned_used, 1)
            dve.wait_ge(tile_row_ready, 1)
            dve.tensor_copy(step_tile[:, :], tile_row[:, :]).then_inc(tables_ready, 1)

        @block.tensor
        def _(pe):
            pe.wait_ge(ends_ready, 1)
            pe.matmul(spread[:, :], a.ones_row[:, :], ends[:, :], start=True, stop=True).then_inc(spread_ready, 1)
            pe.wait_ge(tile_ready, 1)
            for k in range(SB):
                last_mm = pe.matmul(tile_row[:, k * P:(k + 1) * P], tile[:, k:k + 1], a.ident[:, :],
                                    start=True, stop=True)
            last_mm.then_inc(tile_row_ready, 1)
            pe.wait_ge(rows_ready, SB)
            for n, (t, g) in enumerate(turns):
                if n >= 2:
                    pe.wait_ge(turned_used, n - 1)
                for k in range(SB):
                    last_mm = pe.transpose(turned[n % 2][:, k, :], rows[:, t, k, g * P:(g + 1) * P], a.ident[:, :])
                last_mm.then_inc(turned_ready, 1)


class WalkTables:

    def __init__(self, st, a, weights):
        self.a = a
        self.src = st.sbuf("step_src", [P, SW, GE], I32)
        self.dst = st.sbuf("step_dst", [P, SW, GE])
        self.weight = st.sbuf("step_weight", [P, SW, GE]) if weights else None
        self.tile = st.sbuf("step_tile", [1, SW], I32)
        self.loaded = st.sem("tables_loaded")
        self.count = 16 * (4 if weights else 3)

    def load(self, sp):
        pairs = [(self.src, self.a.step_src_dram), (self.dst, self.a.step_dst_dram), (self.tile, self.a.step_tile_dram)]
        if self.weight is not None:
            pairs.append((self.weight, self.a.step_weight_dram))
        for table, stored in pairs:
            sp.dma_start(table.ap(), stored.ap()).then_inc(self.loaded, 16)


def gather_rows(pool, tables, source, rows, rows_in, picked, picked_ready, gathers_begun, product_ready):
    src_of = tables.src[:, :, :].rearrange("p s g -> p (s g)")
    chunks = STEPS // U

    def pick(at, t):
        pool.tensor_copy(picked[:, at, :], src_of[:, ds(t * (U * GE), U * GE)]).then_inc(picked_ready, 1)

    def gather(at, t):
        half, first = at % 2, isinstance(t, int) and t < 2
        pick((at + 1) % 4, t + 1)
        pool.wait_ge(picked_ready, t + 1)
        pool.sem_inc(gathers_begun, 1)
        for u in range(U):
            if not first and u % 2 == 0:
                pool.wait_ge(product_ready, t * U + min(u + 2, U) - RING)
                pool.sem_inc(gathers_begun, 1)
            for g in range(GE):
                pool.indirect_dma_start(
                    rows[:, half * U + u, g, :], None, source,
                    bass.IndirectOffsetOnAxis(picked[:, at, u * GE + g:u * GE + g + 1].bitcast(U32), 0)
                ).then_inc(rows_in[half * U + u], 16)

    pool.wait_ge(tables.loaded, tables.count)
    pick(0, 0)
    for t in range(chunks % 4 + 4):
        gather(t % 4, t)
    with pool.Fori(chunks % 4 + 4, chunks, 4) as t:
        for n in range(4):
            gather((chunks + n) % 4, t + n)
    pool.wait_ge(picked_ready, chunks + 1)


def aggregate_messages(nc, a):
    with Stage(nc, "agg") as st:
        tables = WalkTables(st, a, weights=True)
        rows = st.sbuf("rows", [P, RING, GE, D])
        picked = st.sbuf("picked", [P, 4, U * GE], I32)
        hot = st.sbuf("hot", [P, HOT, GE, P])
        weighted = st.sbuf("weighted", [P, HOT, GE, P])
        part = [st.psum(f"part{i}", [P, D]) for i in range(2)]
        count = [st.psum(f"count{i}", [P, 1]) for i in range(2)]
        rows_in = [st.sem(f"rows_in{i}") for i in range(RING)]
        gathers_begun = st.sem("gathers_begun")
        picked_ready, hot_ready, weighted_ready, product_ready, sums_added = (
            st.sem("picked_ready"), st.sem("hot_ready"), st.sem("weighted_ready"),
            st.sem("product_ready"), st.sem("sums_added"))
        block = st.stack.enter_context(nc.Block())

        @block.sync
        def _(sp):
            tables.load(sp)

        @block.gpsimd
        def _(pool):
            gather_rows(pool, tables, a.normed_dram.ap(), rows, rows_in, picked, picked_ready, gathers_begun,
                        product_ready)

        @block.vector
        def _(dve):
            dve.wait_ge(tables.loaded, tables.count)

            def one_hot(s, u):
                at = u % HOT
                d = tables.dst[:, ds(s, 1), :].rearrange("p o g -> p (o g)")
                w = tables.weight[:, ds(s, 1), :].rearrange("p o g -> p (o g)")
                dve.tensor_tensor(hot[:, at, :, :], a.columns[:, None, :].to_broadcast([P, GE, P]),
                                  d[:, :, None].to_broadcast([P, GE, P]), ALU.is_equal).then_inc(hot_ready, 1)
                dve.wait_ge(hot_ready, s + 1)
                dve.tensor_tensor(weighted[:, at, :, :], hot[:, at, :, :],
                                  w[:, :, None].to_broadcast([P, GE, P]), ALU.mult).then_inc(weighted_ready, 1)

            def add(s, u):
                j = dve.value_load(tables.tile[0:1, ds(s, 1)], min_val=0, max_val=SPARE)
                dve.wait_ge(product_ready, s + 1)
                dve.wait_ge(sums_added, 2 * s)
                total = a.sums[:, ds(j, 1), 0:D].rearrange("p o d -> p (o d)")
                degree = a.sums[:, ds(j, 1), D:D + 1].rearrange("p o d -> p (o d)")
                dve.tensor_tensor(total, total, part[u % 2][:, :], ALU.add).then_inc(sums_added, 1)
                dve.tensor_tensor(degree, degree, count[u % 2][:, :], ALU.add).then_inc(sums_added, 1)

            def steps(t, first):
                for u in range(RING):
                    s = t * RING + u
                    if not (first and u < HOT):
                        dve.wait_ge(product_ready, s + 1 - HOT)
                    one_hot(s, u)
                    if not (first and u < 1):
                        add(s - 1, (u - 1) % RING)

            steps(0, True)
            with dve.Fori(1, STEPS // RING) as t:
                steps(t, False)
            add(STEPS - 1, RING - 1)

        @block.tensor
        def _(pe):
            def steps(t, first):
                for u in range(RING):
                    s = t * RING + u
                    pe.wait_ge(weighted_ready, s + 1)
                    pe.wait_ge(rows_in[u], t * (16 * GE) + 16 * GE)
                    if not (first and u < 2):
                        pe.wait_ge(sums_added, 2 * s - 2)
                    for g in range(GE):
                        pe.matmul(count[u % 2][:, :], hot[:, u % HOT, g, :], a.ones_col[:, :],
                                  start=(g == 0), stop=(g == GE - 1))
                    for g in range(GE):
                        last_mm = pe.matmul(part[u % 2][:, :], weighted[:, u % HOT, g, :], rows[:, u, g, :],
                                            start=(g == 0), stop=(g == GE - 1))
                    last_mm.then_inc(product_ready, 1)

            steps(0, True)
            with pe.Fori(1, STEPS // RING) as t:
                steps(t, False)


def after(eng, sem, value):
    if not isinstance(value, int) or value > 0:
        eng.wait_ge(sem, value)


def in_pairs(eng, head, first, last, tail, body):
    for j in range(head, first):
        body(j, j % 2)
    with eng.Fori(first, last, 2) as j:
        body(j, first % 2)
        body(j + 1, 1 - first % 2)
    for j in range(last, tail):
        body(j, j % 2)


def convolve(nc, a, x, w):
    FB, FC = 4, 6
    PASSES = NT + FC + 1
    LD = LAYERS * D
    KB = 33
    F32R = mybir.dt.float32r
    with Stage(nc, "conv") as st:
        w_hi = st.sbuf("w_hi", [P, 2 * KD, LD], F32R)
        w_lo = st.sbuf("w_lo", [P, 2 * KD, LD], F32R)
        m_hi = st.sbuf("m_hi", [P, 2, KD, D], F32R)
        m_lo = st.sbuf("m_lo", [P, 2, KD, D], F32R)
        b_hi = st.sbuf("b_hi", [KB, LD + 2 * D], F32R)
        b_rows = st.sbuf("b_rows", [KB, LD + 2 * D], F32R)
        ones = st.sbuf("ones", [KB, P])
        ones_r = st.sbuf("ones_r", [KB, P], F32R)
        gain = st.sbuf("gain", [P, LAYERS, D])
        shift = st.sbuf("shift", [P, LAYERS, D])
        gain_mlp = st.sbuf("gain_mlp", [P, 2, D])
        shift_mlp = st.sbuf("shift_mlp", [P, 2, D])
        per_degree = st.sbuf("per_degree", [P, NT])
        x_in = st.sbuf("x_in", [P, 2, D])
        lhs_hi = st.sbuf("lhs_hi", [P, 2, 2 * KD, P], F32R)
        lhs_lo = st.sbuf("lhs_lo", [P, 2, 2 * KD, P], F32R)
        layer_work = st.sbuf("layer_work", [P, 2 * KD, LD])
        w_raw = layer_work[:, :, :]
        conv = layer_work[:, 0:2, :].rearrange("p i (l d) -> p i l d", d=D)
        positive = layer_work[:, 2, :].rearrange("p (l d) -> p l d", d=D)
        pair, summed = (layer_work[:, 3, n * 2 * D:(n + 1) * 2 * D].rearrange("p (i d) -> p i d", d=D)
                        for n in range(2))
        bc_lhs_hi = st.sbuf("bc_lhs_hi", [P, 2, KD, P], F32R)
        bc_lhs_lo = st.sbuf("bc_lhs_lo", [P, 2, KD, P], F32R)
        out_bc = st.sbuf("out_bc", [P, 2, 2, D])
        m_raw = out_bc[:, :, :, :]
        input_work = st.sbuf("input_work", [P, LD + 2 * D])
        b_raw = input_work[0:KB, :]
        staged = input_work[:, 0:LD].rearrange("p (i d) -> p i d", i=2)
        act_b = input_work[:, LD:LD + 2 * D].rearrange("p (i d) -> p i d", i=2)
        stats = st.sbuf("stats", [P, LAYERS + 2, 6])
        moments = st.sbuf("moments", [P, 2, LAYERS + 2, 4])
        turn = st.psum("turn", [P, 2 * KD, P])
        turn_bc = st.psum("turn_bc", [P, 2, KD, P])
        ps_conv = [[st.psum(f"ps_conv{i}{h}", [P, 2, D]) for h in range(2)] for i in range(2)]
        ps_bc = [st.psum(f"ps_bc{i}", [P, 2, D]) for i in range(2)]
        rel_in, root_in, weights_in, affine_in, degrees_ready, ones_ready, b_cleared, raw_fixed, hi_split, lo_split = (
            st.sem(n) for n in ("rel_in", "root_in", "weights_in", "affine_in", "degrees_ready", "ones_ready", "b_cleared", "raw_fixed",
                                "hi_split", "lo_split"))
        x_ready = [st.sem(f"x_ready{i}") for i in range(2)]
        staged_ready, turned, hi_ready, lo_ready, conv_ready, centered, normed, shifted, relued, pair_ready, \
            summed_ready = (st.sem(n) for n in (
                "staged_ready", "turned", "hi_ready", "lo_ready", "conv_ready", "centered", "normed", "shifted",
                "relued", "pair_ready", "summed_ready"))
        bc_turned, bc_hi, bc_lo, bc_ready, bc_read, out_b_ready, act_b_ready, tile_done = (
            st.sem(n) for n in ("bc_turned", "bc_hi", "bc_lo", "bc_ready", "bc_read", "out_b_ready", "act_b_ready",
                                "tile_done"))
        own, settled, var, scale = st.sem("own"), st.sem("settled"), st.sem("var"), st.sem("scale")
        block = st.stack.enter_context(nc.Block())
        x_rows = x.rearrange("(t p) d -> p t d", p=P)
        tile_of = lambda t, j: t[:, ds(j, 1), 0:D].rearrange("p o d -> p (o d)")

        def runs(i, back, extra=0):
            return not isinstance(i, int) or 0 <= i - back < NT + extra

        def passes(eng, body):
            in_pairs(eng, 0, 9, NT - 2, PASSES, body)

        BOTH = FC - FB

        @block.sync
        def _(sp):
            k_rows = lambda t: t.rearrange("(k p) n -> p k n", p=P)
            sp.dma_start(w_raw[:, 0:KD, :], k_rows(w["L0_gnn_W_rel"])).then_inc(rel_in, 16)
            sp.dma_start(w_raw[:, KD:2 * KD, :], k_rows(w["L0_gnn_W_root"])).then_inc(root_in, 16)
            sp.dma_start(m_raw[:, 0, :, :], k_rows(w["L0_gnn_W1"])).then_inc(weights_in, 16)
            sp.dma_start(m_raw[:, 1, :, :], k_rows(w["L0_gnn_W2"])).then_inc(weights_in, 16)
            sp.wait_ge(b_cleared, 1)
            for row in (0, KB - 1):
                sp.dma_start(b_raw[row:row + 1, 0:LD], w["L0_gnn_b_rel"]).then_inc(weights_in, 16)
                for i, name in enumerate(("L0_gnn_b1", "L0_gnn_b2")):
                    sp.dma_start(b_raw[row:row + 1, LD + i * D:LD + (i + 1) * D], w[name]).then_inc(weights_in, 16)
            for out, name in ((gain[:, :, :], "L0_gnn_ln_g"), (shift[:, :, :], "L0_gnn_ln_b")):
                sp.dma_start(out.rearrange("p l d -> p (l d)"), w[name].to_broadcast([P, LD])).then_inc(affine_in, 16)
            for i, (g, b) in enumerate((("L0_gnn_mg1", "L0_gnn_mb1"), ("L0_gnn_mg2", "L0_gnn_mb2"))):
                sp.dma_start(gain_mlp[:, i, :], w[g].to_broadcast([P, D])).then_inc(affine_in, 16)
                sp.dma_start(shift_mlp[:, i, :], w[b].to_broadcast([P, D])).then_inc(affine_in, 16)

            def load(j, par):
                after(sp, tile_done, j - 1)
                sp.dma_start(x_in[:, par, :], tile_of(x_rows, j)).then_inc(x_ready[par], 16)

            in_pairs(sp, 0, 5, 47, NT, load)

        @block.scalar
        def _(act):
            def stage(j, par):
                after(act, turned, j - 1)
                act.activation(staged[:, par, 0:D], tile_of(a.sums, j), ACT.Copy, scale=per_degree[:, ds(j, 1)])
                act.activation(staged[:, par, D:2 * D], tile_of(a.nodes, j), ACT.Copy).then_inc(staged_ready, 1)

            def one_pass(i, par):
                if runs(i, 0):
                    act.wait_ge(turned, i + 1)
                    after(act, conv_ready, i - 1)
                    act.activation(lhs_hi[:, par, :, :], turn[:, :, :], ACT.Copy).then_inc(hi_ready, 1)
                if runs(i, -1):
                    stage(i + 1, 1 - par)
                if runs(i, 3):
                    act.wait_ge(shifted, i - 2)
                    after(act, summed_ready, i - 3)
                    act.activation(positive[:, :, :], conv[:, 1 - par, :, :], ACT.Relu).then_inc(relued, 1)
                if runs(i, FB, BOTH):
                    act.wait_ge(bc_turned, i - FB + 1)
                    after(act, bc_ready, i - FB)
                    side = slice(0 if runs(i, FB) else 1, 2 if runs(i, FC) else 1)
                    act.activation(bc_lhs_hi[:, side, :, :], turn_bc[:, side, :, :], ACT.Copy).then_inc(bc_hi, 1)
                if runs(i, 2, FC - 1):
                    act.wait_ge(var, i - 1)
                    side = slice(0 if runs(i, 2) else LAYERS + (0 if runs(i, FB + 1) else 1),
                                 LAYERS + (2 if runs(i, FC + 1) else 1 if runs(i, FB + 1) else 0))
                    act.activation(moments[:, par, side, 3], moments[:, par, side, 2], ACT.Sqrt).then_inc(scale, 1)
                if runs(i, 2):
                    act.wait_ge(centered, i - 1)
                    act.wait_ge(scale, i - 1)
                    for l in range(LAYERS):
                        c = conv[:, par, l, :]
                        last = act.activation(c, c, ACT.Copy, scale=moments[:, par, l, 3:4])
                    last.then_inc(normed, 1)
                if runs(i, FB + 1):
                    act.wait_ge(out_b_ready, i - FB)
                    act.activation(act_b[:, 1 - par, :], out_bc[:, 1 - par, 0, :], ACT.Relu).then_inc(act_b_ready, 1)

            act.wait_ge(rel_in, 16)
            act.activation(w_hi[:, 0:KD, :], w_raw[:, 0:KD, :], ACT.Copy).then_inc(hi_split, 1)
            act.wait_ge(raw_fixed, KD * LAYERS)
            act.activation(w_hi[:, KD:2 * KD, :], w_raw[:, KD:2 * KD, :], ACT.Copy).then_inc(hi_split, 1)
            act.wait_ge(weights_in, 16 * 8)
            act.activation(b_hi[:, :], b_raw[:, :], ACT.Copy).then_inc(hi_split, 1)
            act.activation(m_hi[:, :, :, :], m_raw[:, :, :, :], ACT.Copy).then_inc(hi_split, 1)
            act.wait_ge(degrees_ready, 2)
            act.wait_ge(lo_split, 4)
            stage(0, 0)
            passes(act, one_pass)

        @block.gpsimd
        def _(pool):
            pool.memset(b_raw[:, :], 0.0).then_inc(b_cleared, 1)
            pool.memset(ones[:, :], 1.0).then_inc(ones_ready, 1)

            def one_pass(i, par):
                if runs(i, 3):
                    k = i - 3
                    pool.wait_ge(relued, k + 1)
                    pool.tensor_tensor(pair[:, :, :], positive[:, 0:2, :], positive[:, 2:4, :], ALU.add
                                       ).then_inc(pair_ready, 1)
                    pool.wait_ge(pair_ready, k + 1)
                    after(pool, bc_turned, k - 1)
                    pool.tensor_tensor(summed[:, 1 - par, :], pair[:, 0, :], pair[:, 1, :], ALU.add
                                       ).then_inc(summed_ready, 1)
                if runs(i, 2):
                    pool.wait_ge(normed, i - 1)
                    pool.tensor_tensor(conv[:, par, :, :], conv[:, par, :, :], shift[:, :, :], ALU.add
                                       ).then_inc(shifted, 1)

            pool.wait_ge(affine_in, 16 * 6)
            passes(pool, one_pass)

        @block.vector
        def _(dve):
            dve.tensor_scalar(per_degree[:, :], a.sums[:, 0:NT, D], 1.0, None, ALU.max).then_inc(degrees_ready, 1)
            dve.wait_ge(degrees_ready, 1)
            dve.reciprocal(per_degree[:, :], per_degree[:, :]).then_inc(degrees_ready, 1)
            dve.tensor_copy(a.degree[:, :], a.sums[:, 0:NT, D])
            dve.wait_ge(root_in, 16)
            for l in range(LAYERS):
                for k in range(KD):
                    c = slice(l * D + k * P, l * D + (k + 1) * P)
                    dve.tensor_tensor(w_raw[:, KD + k, c], w_raw[:, KD + k, c], a.ident[:, :], ALU.add
                                      ).then_inc(raw_fixed, 1)
            dve.wait_ge(ones_ready, 1)
            dve.tensor_copy(ones_r[:, :], ones[:, :]).then_inc(lo_split, 1)
            dve.wait_ge(hi_split, 1)
            dve.wait_ge(rel_in, 16)
            dve.tensor_tensor(w_lo[:, 0:KD, :], w_raw[:, 0:KD, :], w_hi[:, 0:KD, :].bitcast(F32), ALU.subtract
                              ).then_inc(lo_split, 1)
            dve.wait_ge(hi_split, 2)
            dve.wait_ge(raw_fixed, KD * LAYERS)
            dve.tensor_tensor(w_lo[:, KD:2 * KD, :], w_raw[:, KD:2 * KD, :], w_hi[:, KD:2 * KD, :].bitcast(F32),
                              ALU.subtract).then_inc(lo_split, 1)
            dve.wait_ge(hi_split, 4)
            dve.wait_ge(weights_in, 16 * 8)
            dve.tensor_tensor(b_rows[:, :], b_raw[:, :], b_hi[:, :].bitcast(F32), ALU.subtract).then_inc(lo_split, 1)
            dve.tensor_tensor(m_lo[:, :, :, :], m_raw[:, :, :, :], m_hi[:, :, :, :].bitcast(F32), ALU.subtract
                              ).then_inc(lo_split, 1)
            dve.wait_ge(lo_split, 5)
            dve.tensor_copy(b_rows[0:1, :], b_hi[0:1, :].bitcast(F32)).then_inc(lo_split, 1)

            def own_of(i):
                n = (LAYERS if runs(i, 2) else 0) + int(runs(i, FB + 1)) + int(runs(i, FC + 1))
                late = (1 if runs(i, FB + 1) else 0) + (2 if runs(i, FC + 1) else 0)
                return (2 * n + 1 if n else 0) + late

            def own_before(i):
                if isinstance(i, int):
                    return sum(own_of(k) for k in range(i))
                full = own_of(i)
                return (i - 9) * full + own_before(9)

            def one_pass(i, par):
                o = Order(dve, own, own_before(i))
                if runs(i, 0):
                    dve.wait_ge(hi_ready, i + 1)
                    after(dve, conv_ready, i - 1)
                    dve.tensor_tensor(lhs_lo[:, par, :, :], turn[:, :, :], lhs_hi[:, par, :, :].bitcast(F32),
                                      ALU.subtract).then_inc(lo_ready, 1)
                slots = []
                if runs(i, 2):
                    dve.wait_ge(conv_ready, i - 1)
                    slots += [(l, ps_conv[par][l // 2][:, l % 2, :]) for l in range(LAYERS)]
                bc = [n for n, back in enumerate((FB, FC)) if runs(i, back + 1)]
                if bc:
                    dve.wait_ge(bc_ready, i - FB)
                    slots += [(LAYERS + n, ps_bc[1 - par][:, n, :]) for n in bc]
                for l, source in slots:
                    o.mark(dve.bn_stats(stats[:, l, :], source))
                if slots:
                    if not isinstance(i, int) or i >= 4:
                        dve.wait_ge(normed, min(i - 3, NT) if isinstance(i, int) else i - 3)
                    o.wait_apart(settled)
                    for l, _source in slots:
                        o.mark(dve.bn_aggr(moments[:, par, l, 0:2], stats[:, l, :]))
                    o.wait()
                    m = moments[:, par, slots[0][0]:slots[-1][0] + 1, :]
                    o.link(dve.tensor_scalar(m[:, :, 2], m[:, :, 1], EPS, None, ALU.add))
                    dve.reciprocal(m[:, :, 2], m[:, :, 2]).then_inc(var, 1)
                if runs(i, FB, BOTH):
                    side = slice(0 if runs(i, FB) else 1, 2 if runs(i, FC) else 1)
                    dve.wait_ge(bc_hi, i - FB + 1)
                    after(dve, bc_ready, i - FB)
                    dve.tensor_tensor(bc_lhs_lo[:, side, :, :], turn_bc[:, side, :, :],
                                      bc_lhs_hi[:, side, :, :].bitcast(F32), ALU.subtract).then_inc(bc_lo, 1)
                if runs(i, 2):
                    after(dve, relued, i - 3)
                    for l in range(LAYERS):
                        last = dve.scalar_tensor_tensor(out=conv[:, par, l, :], in0=ps_conv[par][l // 2][:, l % 2, :],
                                                        scalar=moments[:, par, l, 0:1], in1=gain[:, l, :],
                                                        op0=ALU.subtract, op1=ALU.mult)
                    last.then_inc(centered, 1)
                if bc:
                    out = lambda n: out_bc[:, 1 - par, n, :]
                    if 0 in bc:
                        after(dve, act_b_ready, i - FB - 2)
                    for n in bc:
                        ins = dve.scalar_tensor_tensor(
                            out=out(n), in0=ps_bc[1 - par][:, n, :], scalar=moments[:, par, LAYERS + n, 0:1],
                            in1=gain_mlp[:, n, :], op0=ALU.subtract, op1=ALU.mult)
                        o.mark(ins)
                    o.wait()
                    dve.sem_inc(bc_read, 1)
                    dve.wait_ge(scale, i - 1)
                    for n in reversed(bc):
                        ins = dve.scalar_tensor_tensor(out=out(n), in0=out(n), scalar=moments[:, par, LAYERS + n, 3:4],
                                                       in1=shift_mlp[:, n, :], op0=ALU.mult, op1=ALU.add)
                        if n == 0:
                            ins.then_inc(out_b_ready, 1)
                        else:
                            o.mark(ins)
                    if 1 in bc:
                        k, side = i - FC - 1, 1 - par
                        dve.wait_ge(x_ready[side], 16 * (k // 2 + 1) if isinstance(k, int) else (k - side) * 8 + 16)
                        o.wait()
                        dve.scalar_tensor_tensor(out=tile_of(a.nodes, k), in0=out(1), scalar=0.0, in1=x_in[:, side, :],
                                                 op0=ALU.max, op1=ALU.add).then_inc(tile_done, 1)
                assert o.n == own_of(i), (i, o.n, own_of(i))

            dve.wait_ge(affine_in, 16 * 6)
            passes(dve, one_pass)

        @block.tensor
        def _(pe):
            def triple(out, hi, lo, right_hi, right_lo, bias):
                n = len(hi)
                terms = [(x_, y) for x_, y in zip(hi, right_hi)] + list(zip(hi, right_lo)) + list(zip(lo, right_hi))
                for q, (x_, y) in enumerate(terms):
                    pe.matmul(out, x_, y, start=(q == 0), stop=False)
                return pe.matmul(out, ones_r[:, :], bias, start=False, stop=True)

            def multiply(h, par):
                half, ks = slice(h * 2 * D, (h + 1) * 2 * D), range(2 * KD)
                return triple(ps_conv[1 - par][h][:, :, :].rearrange("p l d -> p (l d)"),
                              [lhs_hi[:, 1 - par, k, :] for k in ks], [lhs_lo[:, 1 - par, k, :] for k in ks],
                              [w_hi[:, k, half] for k in ks], [w_lo[:, k, half] for k in ks], b_rows[:, half])

            def one_pass(i, par):
                if runs(i, 0):
                    pe.wait_ge(staged_ready, i + 1)
                    after(pe, lo_ready, i)
                    for k in range(2 * KD):
                        mm = pe.transpose(turn[:, k, :], staged[:, par, k * P:(k + 1) * P], a.ident[:, :])
                    mm.then_inc(turned, 1)
                if runs(i, 1):
                    pe.wait_ge(lo_ready, i)
                    after(pe, centered, i - 2)
                    multiply(0, par)
                if runs(i, FB, BOTH):
                    after(pe, bc_lo, i - FB)
                    if runs(i, FC):
                        pe.wait_ge(act_b_ready, i - FC + 1)
                        for k in range(KD):
                            mm = pe.transpose(turn_bc[:, 1, k, :], act_b[:, par, k * P:(k + 1) * P], a.ident[:, :])
                    if runs(i, FB):
                        pe.wait_ge(summed_ready, i - FB + 1)
                        for k in range(KD):
                            mm = pe.transpose(turn_bc[:, 0, k, :], summed[:, par, k * P:(k + 1) * P], a.ident[:, :])
                    mm.then_inc(bc_turned, 1)
                if runs(i, 1):
                    multiply(1, par).then_inc(conv_ready, 1)
                if runs(i, FB, BOTH):
                    pe.wait_ge(bc_lo, i - FB + 1)
                    after(pe, bc_read, i - FB - 1)
                    for n, back in enumerate((FB, FC)):
                        if runs(i, back):
                            ks = range(KD)
                            mm = triple(ps_bc[par][:, n, :],
                                        [bc_lhs_hi[:, n, k, :] for k in ks], [bc_lhs_lo[:, n, k, :] for k in ks],
                                        [m_hi[:, n, k, :] for k in ks], [m_lo[:, n, k, :] for k in ks],
                                        b_rows[:, LD + n * D:LD + (n + 1) * D])
                    mm.then_inc(bc_ready, 1)

            pe.wait_ge(lo_split, 6)
            passes(pe, one_pass)




class Mixture:

    def __init__(self, experts, hidden, func, router_hidden, adds_input, weights, biases, out_bias, router):
        self.experts, self.hidden, self.func, self.router_hidden = experts, hidden, func, router_hidden
        self.adds_input = adds_input
        self.weights, self.biases, self.out_bias, self.router = weights, biases, out_bias, router


HEADS = (4, BT - 4)
SLOTS = 8


def mix(nc, a, name, moe, w, out=None):
    NE, NH = moe.experts, moe.hidden
    NL = NH + 1
    UNITS = [(e, h) for e in range(NE) for h in range(2)]
    NU = len(UNITS)
    F32R = mybir.dt.float32r
    WIDE = HEADS[0] * P
    TILES = {1: (0, 1), 2: (2, 3), 3: (4, 5), 4: (6,)}
    PAIRS = list(TILES.values())
    ROUTE, PICK, TURN = 5, 8, 11
    PARTS = 13
    NEXP = 2 if moe.router_hidden else 1
    OWN_INPUT = BT if moe.adds_input else 0
    OWN_STATS = 2 * BT + 1
    OWN_PICK = [2, 2 * BT + 4, 7 if moe.router_hidden else 8]
    OWN_BLOCK = OWN_STATS + OWN_INPUT + sum(OWN_PICK)
    with Stage(nc, name) as st:
        w_hi = st.sbuf("w_hi", [P, NE, NL, KD, D], F32R)
        w_lo = st.sbuf("w_lo", [P, NE, NL, KD, D], F32R)
        bias = st.sbuf("bias", [P, NH, NE, KD])
        out_bias = st.sbuf("out_bias", [NE, D])
        RW = R0 if moe.router_hidden else SLOTS
        r_raw = st.sbuf("r_raw", [P, KD, RW])
        r_hi = st.sbuf("r_hi", [P, KD, RW], F32R)
        r_lo = st.sbuf("r_lo", [P, KD, RW], F32R)
        f_hi = st.sbuf("f_hi", [P, 2, KD, BN], F32R)
        f_lo = st.sbuf("f_lo", [P, 2, KD, BN], F32R)
        normed = st.sbuf("normed", [P, 2, D])
        full = [st.sbuf(f"full{l}", [P, KD, WIDE]) for l in range(NH)]
        raw = full if NH > 1 else full + [st.sbuf("raw", [P, KD, WIDE])]
        w_raw = [t[:, i, :].rearrange("p (k n) -> p k n", k=KD) for t in raw for i in range(2)]
        NR = len(w_raw)
        h_hi = [st.sbuf(f"h_hi{l}", [P, 2, KD, WIDE], F32R) for l in range(NH)]
        h_lo = [st.sbuf(f"h_lo{l}", [P, 2, KD, WIDE], F32R) for l in range(NH)]
        stats = st.sbuf("stats", [P, BT, 6])
        moments = st.sbuf("moments", [P, BT, 4])
        logits = st.sbuf("logits", [P, BT, SLOTS])
        probs = st.sbuf("probs", [P, BT, SLOTS])
        top = st.sbuf("top", [P, BT, SLOTS])
        top_index = st.sbuf("top_index", [P, BT, SLOTS], U32)
        chosen = st.sbuf("chosen", [P, BT, 2])
        share = st.sbuf("share", [P, BT, 2])
        row = st.sbuf("row", [P, BT, 2])
        picks = st.sbuf("picks", [P, BT, SLOTS])
        combine = st.sbuf("combine", [P, 2, BT, SLOTS])
        combine_turned = st.sbuf("combine_turned", [SLOTS, BT, P])
        if moe.router_hidden:
            rh_bias = st.sbuf("rh_bias", [P, 1])
            rh = st.sbuf("rh", [P, WIDE])
            r_out = st.sbuf("r_out", [P, NE])
            r_out_bias = st.sbuf("r_out_bias", [P, NE])
        ps_h = [[st.psum(f"ps_h{l}{m}", [P, WIDE]) for m in range(KD)] for l in range(NH)]
        ps_out = [st.psum(f"ps_out{i}", [P, 2, D]) for i in range(2)]
        ps_turn = st.psum("ps_turn", [P, 2, KD, P])
        turned_tiles = ps_turn[:, :, :, :].rearrange("p i k n -> p (i k) n")
        route_logits = ps_turn[:, 0, 0, 0:BT * SLOTS].rearrange("p (t e) -> p t e", t=BT)
        ps_route = st.psum("ps_route", [P, 512])
        names = ["small_in", "weight_used", "weights_ready", "cleared", "own", "var", "scale", "normed_ready",
                 "turned", "hi_ready", "features_ready", "rh_ready", "rh_read", "half_routed", "exp_in", "exp_out",
                 "combine_ready", "combine_turn", "combine_turned_ready", "bias_product", "bias_added", "pre_own",
                 "out_product", "out_added", "stored", "weight_hi", "settled"]
        s = {n: st.sem(n) for n in names}
        prod = [st.sem(f"prod{l}") for l in range(NH)]
        evac = [st.sem(f"evac{l}") for l in range(NH)]
        split = [st.sem(f"split{l}") for l in range(NH)]
        MATS = [(e, l) for e in range(NE) for l in range(NL)]
        raw_in = [st.sem(f"raw_in{n}") for n in range(len(MATS))]
        block = st.stack.enter_context(nc.Block())
        n_small = [0]

        def tiles_of(f, par, t0, n):
            return f[:, par, :, t0 * P:(t0 + n) * P].rearrange("p k (t n) -> p t k n", n=P)

        def out_count(b, u):
            return b * (2 * NU) + 2 * u

        def prologue(early, late, split_off):
            for part in range(PARTS):
                early(0, 0, part)
                late(0, 0, part)
                for n in range(len(MATS)):
                    if n * PARTS // len(MATS) == part:
                        split_off(n)

        def stream(b, hidden, output, bias_unit, other, early, late):
            more = not isinstance(b, int) or b + 1 < NB
            for v in range(NU + NH):
                for l in range(NH):
                    if 0 <= v - l < NU:
                        hidden(l, v - l)
                    if l == 0 and more and v < PARTS:
                        early(b + 1, other, v)
                if v == 0:
                    bias_unit(b)
                if v >= NH:
                    output(v - NH)
                if more and v < PARTS:
                    late(b + 1, other, v)

        @block.sync
        def _(sp):
            def small(dst, src):
                sp.dma_start(dst, src).then_inc(s["small_in"], 16)
                n_small[0] += 16

            small(r_raw[:, :, :], moe.router[0].rearrange("(k p) n -> p k n", p=P))
            for l in range(NH):
                small(bias[:, l, :, :], moe.biases[l])
            small(out_bias[:, :], moe.out_bias)
            if moe.router_hidden:
                small(rh_bias[:, :], moe.router[1])
                small(r_out[:, :], moe.router[2])
                small(r_out_bias[:, :], moe.router[3].to_broadcast([P, NE]))
            for n, (e, l) in enumerate(MATS):
                if n >= NR:
                    sp.wait_ge(s["weight_used"], n - NR + 1)
                sp.dma_start(w_raw[n % NR], moe.weights[l][e].rearrange("(k p) n -> p k n", p=P)
                             ).then_inc(raw_in[n], 16)
            if out is not None:
                rows = out.rearrange("(t p) d -> p t d", p=P)

                def store(b, par):
                    sp.wait_ge(s["out_added"], b * (2 * NU) + 2 * NU)
                    sp.dma_start(rows[:, ds(b * BT, BT), :], a.nodes[:, ds(b * BT, BT), :]).then_inc(s["stored"], 16)

                in_pairs(sp, 0, 1, 5, NB, store)
                sp.wait_ge(s["stored"], 16 * NB)

        @block.gpsimd
        def _(pool):
            pool.memset(logits[:, :, :], LOW).then_inc(s["cleared"], 1)

        @block.scalar
        def _(act):
            act.wait_ge(s["small_in"], n_small[0])
            act.activation(r_hi[:, :, :], r_raw[:, :, :], ACT.Copy).then_inc(s["weight_hi"], 1)

            def split_off(n):
                e, l = MATS[n]
                act.wait_ge(raw_in[n], 16)
                act.activation(w_hi[:, e, l, :, :], w_raw[n % NR], ACT.Copy).then_inc(s["weight_hi"], 1)

            def features(b, par, part):
                t0, n = TILES[part][0], len(TILES[part])
                act.wait_ge(s["turned"], b * len(TILES) + part)
                act.activation(tiles_of(f_hi, par, t0, n), ps_turn[:, 0:n, :, :], ACT.Copy).then_inc(s["hi_ready"], 1)

            def early(b, par, part):
                if part == 1:
                    act.wait_ge(s["var"], b + 1)
                    act.activation(moments[:, :, 3], moments[:, :, 2], ACT.Sqrt).then_inc(s["scale"], 1)
                if part - 1 in TILES:
                    features(b, par, part - 1)
                if part in (ROUTE + 1, ROUTE + 2) and moe.router_hidden:
                    h = part - ROUTE - 1
                    n = HEADS[h] * P
                    act.wait_ge(s["rh_ready"], b * 2 + (h + 1))
                    after(act, s["half_routed"], b * 2 + h)
                    act.activation(rh[:, 0:n], ps_route[:, 0:n], ACT.Relu, bias=rh_bias[:, 0:1]
                                   ).then_inc(s["rh_read"], 1)
                if part == PICK + 1:
                    act.wait_ge(s["exp_in"], b * NEXP + 1)
                    act.activation(probs[:, :, :], logits[:, :, :], ACT.Exp).then_inc(s["exp_out"], 1)
                if part == PICK + 2 and NEXP == 2:
                    act.wait_ge(s["exp_in"], b * NEXP + 2)
                    act.activation(share[:, :, 1], row[:, :, 0], ACT.Exp).then_inc(s["exp_out"], 1)

            def late(b, par, part):
                if part in (TURN, TURN + 1):
                    h = part - TURN
                    act.wait_ge(s["combine_turn"], b * 2 + (h + 1))
                    t0 = h * HEADS[0]
                    act.activation(combine_turned[:, t0:t0 + HEADS[h], :],
                                   turned_tiles[0:SLOTS, 0:HEADS[h], :], ACT.Copy
                                   ).then_inc(s["combine_turned_ready"], 1)

            def hidden(b, l, u):
                e, h = UNITS[u]
                n = HEADS[h] * P
                for m in range(KD):
                    c = b * (2 * NU) + (2 * u + m)
                    act.wait_ge(prod[l], c + 1)
                    if l + 1 < NH:
                        after(act, prod[l + 1], c - m - 2)
                    else:
                        if not isinstance(b, int) or b > 0 or u >= 2:
                            act.wait_ge(s["out_product"], out_count(b, u - 1))
                    after(act, split[l], c - 1)
                    act.activation(h_hi[l][:, u % 2, m, 0:n], ps_h[l][m][:, 0:n], moe.func, bias=bias[:, l, e, m:m + 1])
                    act.activation(full[l][:, m, 0:n], ps_h[l][m][:, 0:n], moe.func, bias=bias[:, l, e, m:m + 1]
                                   ).then_inc(evac[l], 1)

            def body(b, par):
                stream(b, lambda l, u: hidden(b, l, u), lambda u: None, lambda u: None, 1 - par,
                       early, late)

            prologue(early, late, split_off)
            in_pairs(act, 0, 1, 5, NB, body)

        @block.vector
        def _(dve):
            dve.wait_ge(s["weight_hi"], 1)
            dve.wait_ge(s["small_in"], n_small[0])
            dve.tensor_tensor(r_lo[:, :, :], r_raw[:, :, :], r_hi[:, :, :].bitcast(F32), ALU.subtract
                              ).then_inc(s["weights_ready"], 1)
            dve.wait_ge(s["cleared"], 1)

            def split_off(n):
                e, l = MATS[n]
                dve.wait_ge(s["weight_hi"], n + 2)
                dve.wait_ge(raw_in[n], 16)
                dve.tensor_tensor(w_lo[:, e, l, :, :], w_raw[n % NR], w_hi[:, e, l, :, :].bitcast(F32),
                                  ALU.subtract).then_inc(s["weight_used"], 1)

            def own_before(part):
                tiles = sum(len(ts) for p, ts in TILES.items() if p < part) if moe.adds_input else 0
                return tiles + (OWN_STATS if part else 0) + sum(OWN_PICK[0:max(part - PICK, 0)])

            def early(b, par, part):
                if part - 1 in TILES:
                    t0, n = TILES[part - 1][0], len(TILES[part - 1])
                    dve.wait_ge(s["hi_ready"], b * len(TILES) + part - 1)
                    dve.tensor_tensor(tiles_of(f_lo, par, t0, n), ps_turn[:, 0:n, :, :],
                                      tiles_of(f_hi, par, t0, n).bitcast(F32), ALU.subtract
                                      ).then_inc(s["features_ready"], 1)

            def late(b, par, part):
                o = Order(dve, s["pre_own"], b * OWN_BLOCK + own_before(part))
                node = lambda t: a.nodes[:, ds(b * BT + t, 1), :].rearrange("p o d -> p (o d)")
                if part == 0:
                    for t in range(BT):
                        o.mark(dve.bn_stats(stats[:, t, :], node(t)))
                    o.wait_apart(s["settled"])
                    for t in range(BT):
                        o.mark(dve.bn_aggr(moments[:, t, 0:2], stats[:, t, :]))
                    o.wait()
                    o.link(dve.tensor_scalar(moments[:, :, 2], moments[:, :, 1], EPS, None, ALU.add))
                    dve.reciprocal(moments[:, :, 2], moments[:, :, 2]).then_inc(s["var"], 1)
                if part in TILES:
                    if part == 1:
                        dve.wait_ge(s["scale"], b + 1)
                    after(dve, s["turned"], b * len(TILES) + part - 1)
                    for t in TILES[part]:
                        last = dve.tensor_scalar(normed[:, t % 2, :], node(t), moments[:, t, 0:1], moments[:, t, 3:4],
                                                 ALU.subtract, ALU.mult)
                    last.then_inc(s["normed_ready"], 1)
                    if moe.adds_input:
                        dve.wait_ge(s["normed_ready"], b * len(TILES) + part)
                        for t in TILES[part]:
                            o.mark(dve.tensor_tensor(node(t), node(t), normed[:, t % 2, :], ALU.add))
                        o.wait()
                got = route_logits[:, :, 0:NE]
                z = logits[:, :, 0:NE]
                if part == PICK:
                    dve.wait_ge(s["half_routed"], b * 2 + 2)
                    if moe.router_hidden:
                        o.link(dve.tensor_tensor(z, got, r_out_bias[:, None, :].to_broadcast([P, BT, NE]), ALU.add))
                    else:
                        o.link(dve.tensor_copy(z, got))
                    o.link(dve.tensor_reduce(row[:, :, 1], z, AX, ALU.max))
                    dve.tensor_tensor(z, z, row[:, :, 1:2].to_broadcast([P, BT, NE]), ALU.subtract
                                      ).then_inc(s["exp_in"], 1)
                if part == PICK + 1:
                    dve.wait_ge(s["exp_out"], b * NEXP + 1)
                    o.link(dve.tensor_reduce(row[:, :, 1], probs[:, :, :], AX, ALU.add))
                    o.link(dve.reciprocal(row[:, :, 1], row[:, :, 1]))
                    o.mark(dve.tensor_tensor(probs[:, :, :], probs[:, :, :],
                                             row[:, :, 1:2].to_broadcast([P, BT, SLOTS]), ALU.mult))
                    o.wait_apart(s["settled"])
                    for t in range(BT):
                        o.mark(dve.max(top[:, t, :], probs[:, t, :]))
                    o.wait_apart(s["settled"])
                    for t in range(BT):
                        o.mark(dve.max_index(top_index[:, t, :], top[:, t, :], probs[:, t, :]))
                    o.wait()
                    o.mark(dve.tensor_copy(chosen[:, :, :], top_index[:, :, 0:2]))
                    if NEXP == 2:
                        dve.tensor_tensor(row[:, :, 0], top[:, :, 1], top[:, :, 0], ALU.subtract
                                          ).then_inc(s["exp_in"], 1)
                if part == PICK + 2:
                    if NEXP == 2:
                        dve.wait_ge(s["exp_out"], b * NEXP + 2)
                        o.link(dve.tensor_scalar(row[:, :, 1], share[:, :, 1], 1.0, None, ALU.add))
                        o.link(dve.reciprocal(share[:, :, 0], row[:, :, 1]))
                        o.link(dve.tensor_tensor(share[:, :, 1], share[:, :, 1], share[:, :, 0], ALU.mult))
                    else:
                        o.link(dve.tensor_tensor(row[:, :, 0], top[:, :, 0], top[:, :, 1], ALU.add))
                        o.link(dve.tensor_scalar(row[:, :, 0], row[:, :, 0], 1e-12, None, ALU.max))
                        o.link(dve.reciprocal(row[:, :, 1], row[:, :, 0]))
                        o.link(dve.tensor_tensor(share[:, :, :], top[:, :, 0:2],
                                                 row[:, :, 1:2].to_broadcast([P, BT, 2]), ALU.mult))
                    index = a.columns[:, None, 0:SLOTS].to_broadcast([P, BT, SLOTS])
                    wide = lambda x: x.to_broadcast([P, BT, SLOTS])
                    o.mark(dve.tensor_tensor(combine[:, par, :, :], index, wide(chosen[:, :, 0:1]), ALU.is_equal))
                    o.link(dve.tensor_tensor(picks[:, :, :], index, wide(chosen[:, :, 1:2]), ALU.is_equal))
                    o.mark(dve.tensor_tensor(combine[:, par, :, :], combine[:, par, :, :], wide(share[:, :, 0:1]),
                                             ALU.mult))
                    o.link(dve.tensor_tensor(picks[:, :, :], picks[:, :, :], wide(share[:, :, 1:2]), ALU.mult))
                    dve.tensor_tensor(combine[:, par, :, :], combine[:, par, :, :], picks[:, :, :], ALU.add
                                      ).then_inc(s["combine_ready"], 1)
                assert o.base + o.n == b * OWN_BLOCK + own_before(part + 1) if isinstance(b, int) else True

            def hidden(b, l, u):
                e, h = UNITS[u]
                n = HEADS[h] * P
                for m in range(KD):
                    c = b * (2 * NU) + (2 * u + m)
                    dve.wait_ge(evac[l], c + 1)
                    dve.tensor_tensor(h_lo[l][:, u % 2, m, 0:n], full[l][:, m, 0:n],
                                      h_hi[l][:, u % 2, m, 0:n].bitcast(F32), ALU.subtract).then_inc(split[l], 1)

            def add_bias(b, par):
                for j, tiles in enumerate(PAIRS):
                    dve.wait_ge(s["bias_product"], b * len(PAIRS) + (j + 1))
                    for i, t in enumerate(tiles):
                        x = a.nodes[:, ds(b * BT + t, 1), :].rearrange("p o d -> p (o d)")
                        last = dve.tensor_tensor(x, x, ps_out[j % 2][:, i, :], ALU.add)
                    last.then_inc(s["bias_added"], 1)

            def output(b, par, u):
                e, h = UNITS[u]
                for j in range(2):
                    q = out_count(b, u) + j
                    dve.wait_ge(s["out_product"], q + 1)
                    if u < 2:
                        dve.wait_ge(s["bias_added"], b * len(PAIRS) + (2 * h + j + 1))
                    else:
                        dve.wait_ge(s["out_added"], q - len(PAIRS) + 1)
                    for i, t in enumerate(PAIRS[2 * h + j]):
                        x = a.nodes[:, ds(b * BT + t, 1), :].rearrange("p o d -> p (o d)")
                        last = dve.scalar_tensor_tensor(out=x, in0=ps_out[j][:, i, :],
                                                        scalar=combine[:, par, t, e:e + 1], in1=x,
                                                        op0=ALU.mult, op1=ALU.add)
                    last.then_inc(s["out_added"], 1)

            def body(b, par):
                stream(b, lambda l, u: hidden(b, l, u), lambda u: output(b, par, u),
                       lambda b_: add_bias(b, par), 1 - par, early, late)

            prologue(early, late, split_off)
            in_pairs(dve, 0, 1, 5, NB, body)

        @block.tensor
        def _(pe):
            pe.wait_ge(s["weights_ready"], 1)

            def triple(out_, pairs, first=True, last=True):
                terms = [(lh, rh_) for lh, ll, rh_, rl in pairs] + [(lh, rl) for lh, ll, rh_, rl in pairs] + [
                    (ll, rh_) for lh, ll, rh_, rl in pairs]
                for i, (x, y) in enumerate(terms):
                    mm = pe.matmul(out_, x, y, start=first and i == 0, stop=last and i == len(terms) - 1)
                return mm

            def early(b, par, part):
                if part - 1 in TILES:
                    pe.wait_ge(s["normed_ready"], b * len(TILES) + part - 1)
                    after(pe, s["features_ready"], b * len(TILES) + part - 2)
                    after(pe, s["combine_turned_ready"], b * 2)
                    for i, t in enumerate(TILES[part - 1]):
                        for k in range(KD):
                            mm = pe.transpose(ps_turn[:, i, k, :], normed[:, t % 2, k * P:(k + 1) * P], a.ident[:, :])
                    mm.then_inc(s["turned"], 1)
                if part in (TURN, TURN + 1):
                    h = part - TURN
                    pe.wait_ge(s["combine_ready"], b + 1)
                    after(pe, s["combine_turned_ready"], b * 2 + h)
                    for i in range(HEADS[h]):
                        mm = pe.transpose(turned_tiles[0:SLOTS, i, :], combine[:, par, h * HEADS[0] + i, :],
                                          a.ident[:, :])
                    mm.then_inc(s["combine_turn"], 1)

            def late(b, par, part):
                if part == ROUTE:
                    pe.wait_ge(s["features_ready"], b * len(TILES) + len(TILES))
                    after(pe, s["combine_ready"], b)
                if moe.router_hidden and part in (ROUTE + 1, ROUTE + 2):
                    h = part - ROUTE - 1
                    pe.wait_ge(s["rh_read"], b * 2 + (h + 1))
                    for i in range(HEADS[h]):
                        mm = pe.matmul(route_logits[:, h * HEADS[0] + i, 0:NE], rh[:, i * P:(i + 1) * P], r_out[:, :],
                                       start=True, stop=True)
                    mm.then_inc(s["half_routed"], 1)
                if moe.router_hidden and part in (ROUTE, ROUTE + 1):
                    h = part - ROUTE
                    c0, n = h * WIDE, HEADS[h] * P
                    after(pe, s["rh_read"], b * 2 + h)
                    triple(ps_route[:, 0:n],
                           [(r_hi[:, k, :], r_lo[:, k, :], f_hi[:, par, k, c0:c0 + n], f_lo[:, par, k, c0:c0 + n])
                            for k in range(KD)]).then_inc(s["rh_ready"], 1)
                if not moe.router_hidden and part == ROUTE:
                    for t in range(BT):
                        c = slice(t * P, (t + 1) * P)
                        mm = triple(route_logits[:, t, :],
                                    [(f_hi[:, par, k, c], f_lo[:, par, k, c], r_hi[:, k, :], r_lo[:, k, :])
                                     for k in range(KD)])
                    mm.then_inc(s["half_routed"], 2)

            def hidden(b, par, l, u):
                e, h = UNITS[u]
                c0, n = h * WIDE, HEADS[h] * P
                if l > 0:
                    pe.wait_ge(split[l - 1], b * (2 * NU) + 2 * (u + 1))
                for m in range(KD):
                    c = b * (2 * NU) + (2 * u + m)
                    after(pe, evac[l], c - 1)
                    cols = slice(m * P, (m + 1) * P)
                    x = [(f_hi[:, par, k, c0:c0 + n], f_lo[:, par, k, c0:c0 + n]) if l == 0 else
                         (h_hi[l - 1][:, u % 2, k, 0:n], h_lo[l - 1][:, u % 2, k, 0:n]) for k in range(KD)]
                    triple(ps_h[l][m][:, 0:n],
                           [(w_hi[:, e, l, k, cols], w_lo[:, e, l, k, cols], *x[k]) for k in range(KD)]
                           ).then_inc(prod[l], 1)

            def bias_products(b, par):
                pe.wait_ge(s["combine_turned_ready"], b * 2 + 2)
                for j, tiles in enumerate(PAIRS):
                    if j < 2:
                        after(pe, s["out_added"], b * (2 * NU))
                    else:
                        pe.wait_ge(s["bias_added"], b * len(PAIRS) + j - 1)
                    for i, t in enumerate(tiles):
                        mm = pe.matmul(ps_out[j % 2][:, i, :], combine_turned[0:NE, t, :], out_bias[:, :],
                                       start=True, stop=True)
                    mm.then_inc(s["bias_product"], 1)

            def output(b, par, u):
                e, h = UNITS[u]
                pe.wait_ge(split[NH - 1], b * (2 * NU) + 2 * (u + 1))
                if u == 0:
                    pe.wait_ge(s["bias_added"], b * len(PAIRS) + len(PAIRS))
                for j in range(2):
                    q = out_count(b, u) + j
                    if u > 0:
                        pe.wait_ge(s["out_added"], q - 1)
                    for i, t in enumerate(PAIRS[2 * h + j]):
                        c = slice((2 * j + i) * P, (2 * j + i + 1) * P)
                        mm = triple(ps_out[j][:, i, :],
                                    [(h_hi[NH - 1][:, u % 2, k, c], h_lo[NH - 1][:, u % 2, k, c],
                                      w_hi[:, e, NL - 1, k, :], w_lo[:, e, NL - 1, k, :]) for k in range(KD)])
                    mm.then_inc(s["out_product"], 1)

            def body(b, par):
                stream(b, lambda l, u: hidden(b, par, l, u), lambda u: output(b, par, u),
                       lambda b_: bias_products(b, par), 1 - par, early, late)

            prologue(early, late, lambda n: None)
            pe.wait_ge(s["weight_used"], len(MATS))
            in_pairs(pe, 0, 1, 5, NB, body)


def project(nc, a, w):
    F32R = mybir.dt.float32r
    PAIRS = [(0, 1), (2, 3), (4, 5), (6,)]
    NPAIR = len(PAIRS)
    WIDTH = D + 2 * H
    with Stage(nc, "proj") as st:
        w_raw = st.sbuf("w_raw", [P, KD, WIDTH])
        w_hi = st.sbuf("w_hi", [P, KD, WIDTH], F32R)
        w_lo = st.sbuf("w_lo", [P, KD, WIDTH], F32R)
        att = st.sbuf("att", [P, 2, D])
        terms = st.sbuf("terms", [P, KD, 2, D])
        stats = st.sbuf("stats", [P, NT, 6])
        moments = st.sbuf("moments", [P, NT, 4])
        normed = st.sbuf("normed", [P, 2, 2, D])
        f_hi = st.sbuf("f_hi", [P, 2, 2, KD, P], F32R)
        f_lo = st.sbuf("f_lo", [P, 2, 2, KD, P], F32R)
        turn = [st.psum(f"turn{i}", [P, 2, KD, P]) for i in range(2)]
        ps_h = [[st.psum(f"ps_h{i}{k}", [P, WIDTH]) for k in range(2)] for i in range(2)]
        weights_in, terms_ready, w_complete, w_hi_ready, w_ready, own, settled, var, scale = (
            st.sem(n) for n in ("weights_in", "terms_ready", "w_complete", "w_hi_ready", "w_ready", "own", "settled",
                                "var", "scale"))
        normed_ready, turned, hi_ready, f_ready, h_ready, h_copied = (
            st.sem(n) for n in ("normed_ready", "turned", "hi_ready", "f_ready", "h_ready", "h_copied"))
        spare_cleared, stored = st.sem("spare_cleared"), st.sem("stored")
        block = st.stack.enter_context(nc.Block())
        node = lambda t: a.nodes[:, ds(t, 1), :].rearrange("p o d -> p (o d)")

        def blocks(eng, body):
            with eng.Fori(0, NB) as b:
                body(b)

        @block.sync
        def _(sp):
            sp.dma_start(w_raw[:, :, 0:D], w["L1_gnn_W"].rearrange("(k p) n -> p k n", p=P)).then_inc(weights_in, 16)
            for i, name in enumerate(("L1_gnn_att_src", "L1_gnn_att_dst")):
                sp.dma_start(att[:, i, :], w[name].to_broadcast([P, D])).then_inc(weights_in, 16)
            rows = a.projected_dram.ap().rearrange("(t p) d -> p t d", p=P)
            logits = a.logit_dram.ap().rearrange("(t p) d -> p t d", p=P)

            def store(b):
                sp.wait_ge(h_copied, b * NPAIR + NPAIR)
                sp.dma_start(rows[:, ds(b * BT, BT), :], a.sums[:, ds(b * BT, BT), :]).then_inc(stored, 16)
                with nc.allow_non_contiguous_dma(reason="the heads' logits of each node"):
                    sp.dma_start(logits[:, ds(b * BT, BT), :], a.sums[:, ds(b * BT, BT), D:W1H]).then_inc(stored, 16)

            blocks(sp, store)
            sp.wait_ge(stored, 16 * 2 * NB)

        @block.gpsimd
        def _(pool):
            pool.memset(a.sums[:, SPARE, :], 0.0).then_inc(spare_cleared, 1)
            pool.memset(a.attention[:, :, :], 0.0).then_inc(spare_cleared, 1)

        @block.scalar
        def _(act):
            act.wait_ge(var, 1)
            act.activation(moments[:, :, 3], moments[:, :, 2], ACT.Sqrt).then_inc(scale, 1)
            act.wait_ge(w_complete, 1)
            act.activation(w_hi[:, :, :], w_raw[:, :, :], ACT.Copy).then_inc(w_hi_ready, 1)
            act.wait_ge(spare_cleared, 2)

            def tiles(b):
                def copy_h(j):
                    act.wait_ge(h_ready, b * NPAIR + j + 1)
                    for k, t in enumerate(PAIRS[j]):
                        got = ps_h[j % 2][k]
                        at = ds(b * BT + t, 1)
                        act.activation(a.sums[:, at, :].rearrange("p o d -> p (o d)"), got[:, 0:W1H], ACT.Copy)
                        last = act.activation(a.attention[:, at, 0:H].rearrange("p o d -> p (o d)"), got[:, W1H:WIDTH],
                                              ACT.Copy)
                    last.then_inc(h_copied, 1)

                for j, ts in enumerate(PAIRS):
                    i, n = j % 2, len(ts)
                    act.wait_ge(turned, b * NPAIR + j + 1)
                    if j >= 2:
                        act.wait_ge(h_ready, b * NPAIR + j - 1)
                    act.activation(f_hi[:, i, 0:n, :, :], turn[i][:, 0:n, :, :], ACT.Copy).then_inc(hi_ready, 1)
                    if j:
                        copy_h(j - 1)
                copy_h(NPAIR - 1)

            blocks(act, tiles)

        @block.vector
        def _(dve):
            o = Order(dve, own)
            for t in range(NT):
                o.mark(dve.bn_stats(stats[:, t, :], a.nodes[:, t, :]))
            o.wait_apart(settled)
            for t in range(NT):
                o.mark(dve.bn_aggr(moments[:, t, 0:2], stats[:, t, :]))
            o.wait()
            o.link(dve.tensor_scalar(moments[:, :, 2], moments[:, :, 1], EPS, None, ALU.add))
            dve.reciprocal(moments[:, :, 2], moments[:, :, 2]).then_inc(var, 1)
            dve.wait_ge(weights_in, 16 * 3)
            for k in range(KD):
                last = dve.tensor_tensor(terms[:, k, :, :], w_raw[:, k, None, 0:D].to_broadcast([P, 2, D]), att[:, :, :],
                                         ALU.mult)
            last.then_inc(terms_ready, 1)
            dve.wait_ge(terms_ready, 1)
            dve.tensor_reduce(w_raw[:, :, D:WIDTH], terms[:, :, :, :].rearrange("p k a (h c) -> p k (a h) c", c=C), AX,
                              ALU.add).then_inc(w_complete, 1)
            dve.wait_ge(w_hi_ready, 1)
            dve.tensor_tensor(w_lo[:, :, :], w_raw[:, :, :], w_hi[:, :, :].bitcast(F32), ALU.subtract).then_inc(w_ready, 1)
            dve.wait_ge(scale, 1)

            def tiles(b):
                def norm(j):
                    if j >= 2:
                        dve.wait_ge(turned, b * NPAIR + j - 1)
                    for k, t in enumerate(PAIRS[j]):
                        at = ds(b * BT + t, 1)
                        last = dve.tensor_scalar(normed[:, j % 2, k, :], node(b * BT + t), moments[:, at, 0:1].rearrange("p o d -> p (o d)"),
                                                 moments[:, at, 3:4].rearrange("p o d -> p (o d)"), ALU.subtract, ALU.mult)
                    last.then_inc(normed_ready, 1)

                norm(0)
                norm(1)
                for j, ts in enumerate(PAIRS):
                    i, n = j % 2, len(ts)
                    dve.wait_ge(hi_ready, b * NPAIR + j + 1)
                    dve.tensor_tensor(f_lo[:, i, 0:n, :, :], turn[i][:, 0:n, :, :], f_hi[:, i, 0:n, :, :].bitcast(F32),
                                      ALU.subtract).then_inc(f_ready, 1)
                    if j + 2 < NPAIR:
                        norm(j + 2)

            blocks(dve, tiles)

        @block.tensor
        def _(pe):
            pe.wait_ge(w_ready, 1)

            def tiles(b):
                def turn_pair(j):
                    pe.wait_ge(normed_ready, b * NPAIR + j + 1)
                    if j >= 2:
                        pe.wait_ge(f_ready, b * NPAIR + j - 1)
                    for k in range(len(PAIRS[j])):
                        for c in range(KD):
                            mm = pe.transpose(turn[j % 2][:, k, c, :], normed[:, j % 2, k, c * P:(c + 1) * P],
                                              a.ident[:, :])
                    mm.then_inc(turned, 1)

                turn_pair(0)
                for j, ts in enumerate(PAIRS):
                    if j + 1 < NPAIR:
                        turn_pair(j + 1)
                    i = j % 2
                    pe.wait_ge(f_ready, b * NPAIR + j + 1)
                    if j >= 2:
                        pe.wait_ge(h_copied, b * NPAIR + j - 1)
                    for k in range(len(ts)):
                        for q, (f, ww) in enumerate([(f_hi, w_hi), (f_hi, w_lo), (f_lo, w_hi)]):
                            for c in range(KD):
                                mm = pe.matmul(ps_h[i][k][:, :], f[:, i, k, c, :], ww[:, c, :],
                                               start=(q == 0 and c == 0), stop=(q == 2 and c == KD - 1))
                    mm.then_inc(h_ready, 1)

            blocks(pe, tiles)


def find_maxima(nc, a, src_of_edge, dst_of_edge):
    CH = 23
    NCH = 14
    GATHERED = NCH * CH
    QUAD = 4
    NQ = (EC - GATHERED) // QUAD
    assert GATHERED + NQ * QUAD == EC and NCH % 2 == 0 and NQ % 2 == 1
    F32R = mybir.dt.float32r
    with Stage(nc, "maxima") as st:
        src = st.sbuf("src", [P, EC + CH], I32)
        dst = st.sbuf("dst", [P, EC], I32)
        before = st.sbuf("before", [P, 1], I32)
        picked = st.sbuf("picked", [P, 2, CH], I32)
        got = st.sbuf("got", [P, 2, CH, H])
        logit = st.sbuf("logit", [P, EC + CH, H])
        running = st.sbuf("running", [P, EC, H])
        dest = st.sbuf("dest", [P, EC])
        dest_before = st.sbuf("dest_before", [P, 1])
        reset = st.sbuf("reset", [P, EC])
        node_row_int = st.sbuf("node_row_int", [P, EC], I32)
        node_column_int = st.sbuf("node_column_int", [P, EC], I32)
        node_row = st.sbuf("node_row", [P, EC + 2 * QUAD])
        node_column = st.sbuf("node_column", [P, EC + 2 * QUAD])
        table = st.sbuf("table", [P, NT, H])
        row_hot = st.sbuf("row_hot", [P, 2, QUAD, P], F32R)
        row_hot_turned = st.sbuf("row_hot_turned", [P, 2, QUAD, P])
        column_hot = st.sbuf("column_hot", [P, 2, QUAD, NT])
        masked = st.sbuf("masked", [P, 2, QUAD, NT, H])
        ident = st.sbuf("ident", [P, P], F32R)
        in_first = st.sbuf("in_first", [P, EC])
        flags = st.sbuf("flags", [P, 4])
        tail = st.sbuf("tail", [P, 2, H])
        tail_rows = st.sbuf("tail_rows", [H, 2, P])
        carried = st.sbuf("carried", [H, P + 1])
        carry = st.sbuf("carry", [P, H])
        upto = st.sbuf("upto", [P, P])
        ones = st.sbuf("ones", [P, P])
        ones_nt = st.sbuf("ones_nt", [P, NT])
        before_tile = st.sbuf("before_tile", [P, NT])
        last_edge = st.sbuf("last_edge", [P, NT])
        last_edge_id = st.sbuf("last_edge_id", [P, NT], I32)
        edgeless = st.sbuf("edgeless", [P, NT])
        ps_hot = [st.psum(f"ps_hot{i}", [P, QUAD, P], F32R) for i in range(2)]
        ps_rows = [[st.psum(f"ps_rows{i}{h}", [P, 512]) for h in range(2)] for i in range(2)]
        ps_tail = [ps_rows[0][i][0:H, 0:P] for i in range(2)]
        ps_carry = ps_rows[1][0][:, 0:H]
        ps_count = [ps_rows[1][i][:, 0:NT] for i in range(2)]
        edges_in, own, pool_own, picked_ready, gathers_begun, table_ready = (
            st.sem(n) for n in ("edges_in", "own", "pool_own", "picked_ready", "gathers_begun", "table_ready"))
        hot_ready, column_ready, hot_turned, hot_copied, rows_ready, rows_masked, looked_up, counts_used = (
            st.sem(n) for n in ("hot_ready", "column_ready", "hot_turned", "hot_copied", "rows_ready", "rows_masked", "looked_up",
                                "counts_used"))
        copied = [st.sem(f"copied{i}") for i in range(2)]
        before_in = st.sem("before_in")
        got_in = [st.sem(f"got_in{i}") for i in range(2)]
        counts_ready, tails_ready, tail_turned, carried_ready, carry_turned, running_ready, running_stored, best_in, \
            last_ready = (st.sem(n) for n in ("counts_ready", "tails_ready", "tail_turned", "carried_ready",
                                              "carry_turned", "running_ready", "running_stored", "best_in", "last_ready"))
        block = st.stack.enter_context(nc.Block())

        @block.sync
        def _(sp):
            sp.dma_start(src[:, 0:EC], src_of_edge).then_inc(edges_in, 16)
            sp.dma_start(dst[:, :], dst_of_edge).then_inc(edges_in, 16)
            sp.wait_ge(pool_own, 1)
            with nc.allow_non_contiguous_dma(reason="the last edge of each partition but one"):
                sp.dma_start(before[1:P, :], dst_of_edge[0:P - 1, EC - 1:EC]).then_inc(before_in, 16)
            def copy_away(half, t):
                sp.wait_ge(got_in[half], (t - half) * (CH * 8) + CH * 16)
                sp.dma_start(logit[:, ds(t * CH, CH), :], got[:, half, :, :]).then_inc(copied[half], 16)

            with sp.Fori(0, NCH, 2) as t:
                copy_away(0, t)
                copy_away(1, t + 1)
            for half in range(2):
                sp.wait_ge(copied[half], NCH * 8)
            sp.wait_ge(running_ready, H)
            sp.dma_start(a.running_dram.ap().rearrange("(p e) h -> p (e h)", p=P),
                         running[:, :, :].rearrange("p e h -> p (e h)")).then_inc(running_stored, 16)

        @block.gpsimd
        def _(pool):
            pool.memset(before[:, :], -1).then_inc(pool_own, 1)
            pool.memset(ones[:, :], 1.0).then_inc(pool_own, 1)
            pool.memset(ones_nt[:, :], 1.0).then_inc(pool_own, 1)
            pool.memset(carried[:, :], LOW).then_inc(pool_own, 1)
            pool.wait_ge(pool_own, 4)
            pool.affine_select(out=upto[:, :], in_=ones[:, :], compare_op=ALU.is_ge, fill=0.0, base=0,
                               pattern=[[1, P]], channel_multiplier=-1).then_inc(pool_own, 1)
            pool.wait_ge(edges_in, 32)

            def gather(half, t, first):
                if not first:
                    pool.wait_ge(copied[half], (t - half) * 8)
                pool.tensor_copy(picked[:, half, :], src[:, ds(t * CH, CH)]).then_inc(picked_ready, 1)
                pool.wait_ge(picked_ready, t + 1)
                pool.sem_inc(gathers_begun, 1)
                for c in range(CH):
                    pool.indirect_dma_start(got[:, half, c, :], None, a.logit_dram.ap(),
                                            bass.IndirectOffsetOnAxis(picked[:, half, c:c + 1].bitcast(U32), 0)
                                            ).then_inc(got_in[half], 16)

            gather(0, 0, True)
            gather(1, 1, True)
            with pool.Fori(2, NCH, 2) as t:
                gather(0, t, False)
                gather(1, t + 1, False)
            pool.wait_ge(last_ready, 1)
            pool.wait_ge(running_stored, 16)
            for t in range(NT):
                pool.indirect_dma_start(a.best[:, t, :], None, a.running_dram.ap(),
                                        bass.IndirectOffsetOnAxis(last_edge_id[:, t:t + 1].bitcast(U32), 0)
                                        ).then_inc(best_in, 16)

        @block.scalar
        def _(act):
            def copy_turned(i, par):
                act.wait_ge(hot_turned, i + 1)
                after(act, rows_ready, i - 1)
                act.activation(row_hot_turned[:, par, :, :], ps_hot[par][:, :, :].bitcast(F32), ACT.Copy
                               ).then_inc(hot_copied, 1)

            in_pairs(act, 0, 3, NQ - 2, NQ, copy_turned)

        @block.tensor
        def _(pe):
            pe.wait_ge(pool_own, 5)
            pe.matmul(ps_count[0][:, :], upto[:, :], a.degree[:, :], start=True, stop=True).then_inc(counts_ready, 1)
            pe.matmul(ps_count[1][:, :], ones[:, :], a.degree[:, :], start=True, stop=True).then_inc(counts_ready, 1)
            def quad(i, par):
                if not isinstance(i, int) or i > 0:
                    pe.wait_ge(hot_copied, i)
                    after(pe, rows_masked, i - 2)
                    for q in range(QUAD):
                        out = ps_rows[1 - par][q // 2][:, (q % 2) * NT * H:(q % 2 + 1) * NT * H]
                        mm = pe.matmul(out, row_hot_turned[:, 1 - par, q, :],
                                       table[:, :, :].rearrange("p a h -> p (a h)"), start=True, stop=True)
                    mm.then_inc(rows_ready, 1)
                if not isinstance(i, int) or i < NQ:
                    pe.wait_ge(hot_ready, i + 1)
                    after(pe, hot_copied, i - 1)
                    for q in range(QUAD):
                        mm = pe.transpose(ps_hot[par][:, q, :], row_hot[:, par, q, :], ident[:, :])
                    mm.then_inc(hot_turned, 1)

            pe.wait_ge(counts_used, 1)
            pe.wait_ge(table_ready, 6)
            in_pairs(pe, 0, 5, NQ - 2, NQ + 1, quad)
            pe.wait_ge(tails_ready, 1)
            for i in range(2):
                mm = pe.transpose(ps_tail[i][:, :], tail[:, i, :], a.ident[:, :])
            mm.then_inc(tail_turned, 1)
            pe.wait_ge(carried_ready, 1)
            pe.transpose(ps_carry[:, :], carried[:, 0:P], a.ident[0:H, 0:H]).then_inc(carry_turned, 1)

        @block.vector
        def _(dve):
            o = Order(dve, own)
            dve.wait_ge(counts_ready, 2)
            o.link(dve.tensor_copy(last_edge[:, :], ps_count[1][:, :]))
            dve.wait_ge(pool_own, 5)
            o.link(dve.tensor_tensor_scan(before_tile[:, :], ones_nt[:, :], last_edge[:, :], 0.0, ALU.mult, ALU.add))
            o.link(dve.tensor_tensor(before_tile[:, :], before_tile[:, :], last_edge[:, :], ALU.subtract))
            o.link(dve.tensor_tensor(last_edge[:, :], before_tile[:, :], ps_count[0][:, :], ALU.add))
            dve.sem_inc(counts_used, 1)
            o.link(dve.tensor_scalar(last_edge[:, :], last_edge[:, :], -1.0, 0.0, ALU.add, ALU.max))
            dve.tensor_copy(last_edge_id[:, :], last_edge[:, :]).then_inc(last_ready, 1)
            o.mark(dve.tensor_scalar(edgeless[:, :], a.degree[:, :], 0.0, LOW, ALU.is_equal, ALU.mult))

            dve.wait_ge(edges_in, 32)
            dve.tensor_copy(table[:, :, :], a.sums[:, 0:NT, D:W1H]).then_inc(table_ready, 1)
            dve.tensor_copy(ident[:, :], a.ident[:, :]).then_inc(table_ready, 1)
            dve.tensor_scalar(node_row_int[:, :], src[:, 0:EC], P - 1, None, ALU.bitwise_and).then_inc(table_ready, 1)
            dve.tensor_scalar(node_column_int[:, :], src[:, 0:EC], 7, None, ALU.arith_shift_right
                              ).then_inc(table_ready, 1)
            dve.wait_ge(table_ready, 4)
            dve.tensor_copy(node_row[:, 0:EC], node_row_int[:, :]).then_inc(table_ready, 1)
            dve.tensor_copy(node_column[:, 0:EC], node_column_int[:, :]).then_inc(table_ready, 1)
            dve.wait_ge(table_ready, 6)

            def quad(i, par):
                if not isinstance(i, int) or i >= 2:
                    k = i - 2
                    dve.wait_ge(rows_ready, k + 1)
                    dve.wait_ge(column_ready, k + 1)
                    after(dve, looked_up, k - 1)
                    for h in range(2):
                        ins = dve.tensor_tensor(
                            masked[:, par, 2 * h:2 * h + 2, :, :],
                            ps_rows[par][h][:, 0:2 * NT * H].rearrange("p (q a h) -> p q a h", q=2, a=NT),
                            column_hot[:, par, 2 * h:2 * h + 2, :, None].to_broadcast([P, 2, NT, H]), ALU.mult)
                    ins.then_inc(rows_masked, 1)
                if not isinstance(i, int) or i < NQ:
                    edges = lambda x: x[:, ds(i * QUAD + GATHERED, QUAD)]
                    after(dve, hot_turned, i - 1)
                    dve.tensor_tensor(row_hot[:, par, :, :], a.columns[:, None, :].to_broadcast([P, QUAD, P]),
                                      edges(node_row)[:, :, None].to_broadcast([P, QUAD, P]), ALU.is_equal
                                      ).then_inc(hot_ready, 1)
                    after(dve, rows_masked, i - 1)
                    dve.tensor_tensor(column_hot[:, par, :, :], a.columns[:, None, 0:NT].to_broadcast([P, QUAD, NT]),
                                      edges(node_column)[:, :, None].to_broadcast([P, QUAD, NT]), ALU.is_equal
                                      ).then_inc(column_ready, 1)
                if not isinstance(i, int) or i >= 2:
                    dve.wait_ge(rows_masked, k + 1)
                    dve.tensor_reduce(logit[:, ds(k * QUAD + GATHERED, QUAD), :],
                                      masked[:, par, :, :, :].rearrange("p q a h -> p q h a"), AX, ALU.add
                                      ).then_inc(looked_up, 1)

            in_pairs(dve, 0, 5, NQ - 2, NQ + 2, quad)
            dve.wait_ge(looked_up, NQ)
            dve.wait_ge(before_in, 16)
            o.mark(dve.tensor_copy(dest[:, :], dst[:, :]))
            o.link(dve.tensor_copy(dest_before[:, :], before[:, :]))
            o.mark(dve.memset(reset[:, 0:1], LOW))
            o.mark(dve.tensor_tensor(reset[:, 1:EC], dest[:, 1:EC], dest[:, 0:EC - 1], ALU.not_equal))
            o.mark(dve.tensor_scalar(in_first[:, :], dest[:, :], dest[:, 0:1], LOW, ALU.not_equal, ALU.mult))
            o.mark(dve.tensor_tensor(flags[:, 0:1], dest[:, 0:1], dest_before[:, :], ALU.not_equal))
            o.link(dve.tensor_tensor(flags[:, 1:2], dest[:, 0:1], dest[:, EC - 1:EC], ALU.not_equal))
            o.mark(dve.tensor_scalar(reset[:, 1:EC], reset[:, 1:EC], LOW, None, ALU.mult))
            o.mark(dve.tensor_scalar(flags[:, 2:3], flags[:, 0:1], LOW, None, ALU.mult))
            o.link(dve.tensor_tensor(flags[:, 3:4], flags[:, 0:1], flags[:, 1:2], ALU.max))
            o.link(dve.tensor_scalar(tail[:, 1, :], flags[:, 3:4].to_broadcast([P, H]), LOW, None, ALU.mult))

            for half in range(2):
                dve.wait_ge(copied[half], NCH * 8)
            for h in range(H):
                o.mark(dve.tensor_tensor_scan(running[:, :, h], reset[:, :], logit[:, 0:EC, h], LOW, ALU.add, ALU.max))
            o.wait()
            dve.tensor_copy(tail[:, 0, :], running[:, EC - 1, :]).then_inc(tails_ready, 1)
            dve.wait_ge(tail_turned, 1)
            for i in range(2):
                o.link(dve.tensor_copy(tail_rows[:, i, :], ps_tail[i][:, :]))
            dve.tensor_tensor_scan(carried[:, 1:P + 1], tail_rows[:, 1, :], tail_rows[:, 0, :], LOW, ALU.add, ALU.max
                                   ).then_inc(carried_ready, 1)
            dve.wait_ge(carry_turned, 1)
            o.link(dve.tensor_scalar(carry[:, :], ps_carry[:, :], flags[:, 2:3], None, ALU.add))
            for h in range(H):
                dve.scalar_tensor_tensor(out=running[:, :, h], in0=in_first[:, :], scalar=carry[:, h:h + 1],
                                         in1=running[:, :, h], op0=ALU.add, op1=ALU.max).then_inc(running_ready, 1)
            dve.wait_ge(best_in, 16 * NT)
            o.link(dve.tensor_tensor(a.best[:, :, :], a.best[:, :, :],
                                     edgeless[:, :, None].to_broadcast([P, NT, H]), ALU.add))


def start_softmax(nc, a):
    with Stage(nc, "start") as st:
        z = st.sbuf("z", [P, NT, H])
        own = st.sem("own")
        z_ready, p_ready = st.sem("z_ready"), st.sem("p_ready")
        block = st.stack.enter_context(nc.Block())

        @block.scalar
        def _(act):
            act.wait_ge(z_ready, 1)
            act.activation(a.sums[:, 0:NT, D:W1H], z[:, :, :], ACT.Exp).then_inc(p_ready, 1)

        @block.vector
        def _(dve):
            o = Order(dve, own)
            source = a.sums[:, 0:NT, D:W1H]
            ad, top = a.attention[:, 0:NT, 0:H], a.attention[:, 0:NT, H:2 * H]
            o.link(dve.tensor_tensor(top, a.best[:, :, :], source, ALU.max))
            o.mark(dve.tensor_tensor(top, top, ad, ALU.add))
            o.link(dve.tensor_tensor(z[:, :, :], source, ad, ALU.add))
            o.mark(dve.scalar_tensor_tensor(out=top, in0=top, scalar=SLOPE, in1=top, op0=ALU.mult, op1=ALU.max))
            o.link(dve.scalar_tensor_tensor(out=z[:, :, :], in0=z[:, :, :], scalar=SLOPE, in1=z[:, :, :],
                                            op0=ALU.mult, op1=ALU.max))
            dve.tensor_tensor(z[:, :, :], z[:, :, :], top, ALU.subtract).then_inc(z_ready, 1)
            dve.wait_ge(p_ready, 1)
            for h in range(H):
                x = a.sums[:, 0:NT, h * C:(h + 1) * C]
                o.mark(dve.tensor_tensor(x, x, a.sums[:, 0:NT, D + h:D + h + 1].to_broadcast([P, NT, C]), ALU.mult))
            o.wait()


def attend(nc, a):
    with Stage(nc, "att") as st:
        tables = WalkTables(st, a, weights=False)
        rows = st.sbuf("rows", [P, RING, GE, W1H])
        picked = st.sbuf("picked", [P, 4, U * GE], I32)
        hot = st.sbuf("hot", [P, RING, GE, P], mybir.dt.float32r)
        ident = st.sbuf("ident", [P, P], mybir.dt.float32r)
        hot_turned = st.sbuf("hot_turned", [P, 2, GE, P], mybir.dt.float32r)
        table = st.sbuf("table", [P, NT + 1, 2, 2 * H], mybir.dt.float32r)
        node_logits = st.sbuf("node_logits", [P, 2, GE, 2 * H])
        z = st.sbuf("z", [P, 2, GE, H])
        ps_hot = [st.psum(f"ps_hot{i}", [P, GE, P], mybir.dt.float32r) for i in range(2)]
        ps_logit = [st.psum(f"ps_logit{i}", [P, GE, 2, 2 * H]) for i in range(2)]
        part = [st.psum(f"part{i}", [P, W1H]) for i in range(2)]
        rows_in = [st.sem(f"rows_in{i}") for i in range(RING)]
        picked_ready, gathers_begun, table_ready, hot_ready, turned, turned_copied, logit_ready, parts_summed, \
            source_added, bent, z_ready, p_ready, weighted, \
            product_ready, added = (st.sem(n) for n in (
                "picked_ready", "gathers_begun", "table_ready", "hot_ready", "turned", "turned_copied", "logit_ready", "parts_summed",
                "source_added", "bent",
                "z_ready", "p_ready", "weighted", "product_ready", "added"))
        block = st.stack.enter_context(nc.Block())

        def steps(eng, lags, stages):
            end = max(lags)

            def run(t, u):
                i = t * RING + u
                for lag, stage in zip(lags, stages):
                    if isinstance(i, int) and not 0 <= i - lag < STEPS:
                        continue
                    stage(i - lag, (u - lag) % RING, t - (lag > u))

            for u in range(RING):
                run(0, u)
            with eng.Fori(1, STEPS // RING) as t:
                for u in range(RING):
                    run(t, u)
            for u in range(end):
                run(STEPS // RING, u)

        def landed(eng, u, turn_of_ring):
            eng.wait_ge(rows_in[u], turn_of_ring * (16 * GE) + 16 * GE)

        @block.sync
        def _(sp):
            tables.load(sp)

        @block.gpsimd
        def _(pool):
            gather_rows(pool, tables, a.projected_dram.ap(), rows, rows_in, picked, picked_ready, gathers_begun,
                        product_ready)

        @block.scalar
        def _(act):
            def copy_turned(s, u, ring):
                act.wait_ge(turned, s + 1)
                after(act, logit_ready, s - 1)
                act.activation(hot_turned[:, u % 2, :, :], ps_hot[u % 2][:, :, :], ACT.Copy).then_inc(turned_copied, 1)

            def exponent(s, u, ring):
                act.wait_ge(z_ready, s + 1)
                act.activation(rows[:, u, :, D:W1H], z[:, u % 2, :, :], ACT.Exp).then_inc(p_ready, 1)

            steps(act, (1, 3), (copy_turned, exponent))

        @block.vector
        def _(dve):
            def one_hot(s, u, ring):
                after(dve, product_ready, s + 1 - RING)
                d = tables.dst[:, ds(s, 1), :].rearrange("p o g -> p (o g)")
                dve.tensor_tensor(hot[:, u, :, :], a.columns[:, None, :].to_broadcast([P, GE, P]),
                                  d[:, :, None].to_broadcast([P, GE, P]), ALU.is_equal).then_inc(hot_ready, 1)

            def sum_parts(s, u, ring):
                dve.wait_ge(logit_ready, s + 1)
                dve.tensor_reduce(node_logits[:, u % 2, :, :], ps_logit[u % 2][:, :, :, :].rearrange("p g k d -> p g d k"),
                                  AX, ALU.add).then_inc(parts_summed, 1)

            def add_source(s, u, ring):
                dve.wait_ge(parts_summed, s + 1)
                landed(dve, u, ring)
                dve.tensor_tensor(z[:, u % 2, :, :], rows[:, u, :, D:W1H], node_logits[:, u % 2, :, 0:H], ALU.add
                                  ).then_inc(source_added, 1)

            def bend(s, u, ring):
                dve.wait_ge(source_added, s + 1)
                zz = z[:, u % 2, :, :]
                dve.scalar_tensor_tensor(out=zz, in0=zz, scalar=SLOPE, in1=zz, op0=ALU.mult, op1=ALU.max
                                         ).then_inc(bent, 1)

            def subtract_maximum(s, u, ring):
                dve.wait_ge(bent, s + 1)
                zz = z[:, u % 2, :, :]
                dve.tensor_tensor(zz, zz, node_logits[:, u % 2, :, H:2 * H], ALU.subtract).then_inc(z_ready, 1)

            def weigh(s, u, ring):
                dve.wait_ge(p_ready, s + 1)
                x = rows[:, u, :, 0:D].rearrange("p g (h c) -> p g h c", c=C)
                p = rows[:, u, :, D:W1H]
                dve.tensor_tensor(x, x, p[:, :, :, None].to_broadcast([P, GE, H, C]), ALU.mult).then_inc(weighted, 1)

            place = {}

            def find_tile(s, u, ring):
                place[u] = dve.value_load(tables.tile[0:1, ds(s, 1)], min_val=0, max_val=SPARE)

            def add(s, u, ring):
                j = place.pop(u)
                dve.wait_ge(product_ready, s + 1)
                after(dve, added, s)
                total = a.sums[:, ds(j, 1), :].rearrange("p o d -> p (o d)")
                dve.tensor_tensor(total, total, part[u % 2][:, :], ALU.add).then_inc(added, 1)

            dve.tensor_copy(ident[:, :], a.ident[:, :]).then_inc(table_ready, 1)
            dve.tensor_copy(table[:, :, 0, :], a.attention[:, :, :]).then_inc(table_ready, 1)
            dve.wait_ge(table_ready, 2)
            dve.tensor_tensor(table[:, :, 1, :], a.attention[:, :, :], table[:, :, 0, :].bitcast(F32), ALU.subtract
                              ).then_inc(table_ready, 1)
            dve.wait_ge(tables.loaded, tables.count)
            steps(dve, (3, 0, 6, 3, 6, 3, 4, 3),
                  (sum_parts, one_hot, find_tile, add_source, add, bend, weigh, subtract_maximum))

        @block.tensor
        def _(pe):
            def spread(s, u, ring):
                j = pe.value_load(tables.tile[0:1, ds(s, 1)], min_val=0, max_val=SPARE)
                pe.wait_ge(turned_copied, s + 1)
                after(pe, z_ready, s - 1)
                for g in range(GE):
                    mm = pe.matmul(ps_logit[u % 2][:, g, :, :].rearrange("p k d -> p (k d)"),
                                   hot_turned[:, u % 2, g, :],
                                   table[:, ds(j, 1), :, :].rearrange("p o k d -> p (o k d)"), start=True, stop=True)
                mm.then_inc(logit_ready, 1)

            def turn(s, u, ring):
                pe.wait_ge(hot_ready, s + 1)
                after(pe, turned_copied, s - 1)
                for g in range(GE):
                    mm = pe.transpose(ps_hot[u % 2][:, g, :], hot[:, u, g, :], ident[:, :])
                mm.then_inc(turned, 1)

            def product(s, u, ring):
                pe.wait_ge(weighted, s + 1)
                after(pe, added, s - 1)
                for g in range(GE):
                    mm = pe.matmul(part[u % 2][:, :], hot[:, u, g, :].bitcast(F32), rows[:, u, g, :],
                                   start=(g == 0), stop=(g == GE - 1))
                mm.then_inc(product_ready, 1)

            pe.wait_ge(table_ready, 3)
            pe.wait_ge(tables.loaded, tables.count)
            steps(pe, (2, 1, 5), (spread, turn, product))


def finish_attention(nc, a, w):
    with Stage(nc, "fin") as st:
        bias = st.sbuf("bias", [P, D])
        share = st.sbuf("share", [P, NT, H])
        own, bias_in = st.sem("own"), st.sem("bias_in")
        block = st.stack.enter_context(nc.Block())

        @block.sync
        def _(sp):
            sp.dma_start(bias[:, :], w["L1_gnn_bias"].to_broadcast([P, D])).then_inc(bias_in, 16)

        @block.vector
        def _(dve):
            o = Order(dve, own)
            o.link(dve.tensor_scalar(share[:, :, :], a.sums[:, 0:NT, D:W1H], 1e-16, None, ALU.add))
            o.link(dve.reciprocal(share[:, :, :], share[:, :, :]))
            dve.wait_ge(bias_in, 16)
            for h in range(H):
                x = a.sums[:, 0:NT, h * C:(h + 1) * C]
                o.mark(dve.tensor_tensor(x, x, share[:, :, h:h + 1].to_broadcast([P, NT, C]), ALU.mult))
            o.wait()
            x = a.sums[:, 0:NT, 0:D]
            o.link(dve.tensor_tensor(x, x, bias[:, None, :].to_broadcast([P, NT, D]), ALU.add))
            o.link(dve.scalar_tensor_tensor(out=a.nodes[:, :, :], in0=x, scalar=0.0, in1=a.nodes[:, :, :],
                                            op0=ALU.max, op1=ALU.add))


def first_mixture(w):
    n = "L0_ffn_"
    return Mixture(E0, 2, ACT.Relu, True, False, [w[n + "expert_w1"], w[n + "expert_w2"], w[n + "expert_w3"]],
                   [w[n + "expert_b1"], w[n + "expert_b2"]], w[n + "expert_b3"],
                   [w[n + "router_w1"], w[n + "router_b1"], w[n + "router_w2"], w[n + "router_b2"]])


def second_mixture(w):
    n = "L1_ffn_"
    return Mixture(E1, 1, ACT.Gelu, False, True, [w[n + "w1"], w[n + "w2"]], [w[n + "b1"]], w[n + "b2"],
                   [w[n + "router_w"]])




def program(nc, aps):
    with ExitStack() as stack:
        a = Arena(nc, stack)
        make_constants(nc, a)
        with a.edge_sums("sums"):
            plan_walk(nc, a, aps["src"], aps["dst"], aps["edge_weight"], aps["x"])
            aggregate_messages(nc, a)
            convolve(nc, a, aps["x"], aps)
        mix(nc, a, "mix0", first_mixture(aps), aps)
        with a.edge_sums("attention_sums"), a.attention_tables():
            project(nc, a, aps)
            find_maxima(nc, a, aps["src_of_edge"], aps["dst_of_edge"])
            start_softmax(nc, a)
            attend(nc, a)
            finish_attention(nc, a, aps)
        mix(nc, a, "mix1", second_mixture(aps), aps, out=aps["out"])


def lay_out(inputs):
    import numpy as np

    more_edges, more_nodes = EP - E, NP - N
    edges = {
        "src": np.pad(inputs["src"], (0, more_edges)),
        "dst": np.pad(inputs["dst"], (0, more_edges), constant_values=PAD_DST),
        "edge_weight": np.pad(inputs["edge_weight"], (0, more_edges)),
    }
    out = {name: x.reshape(NG, GE * P) for name, x in edges.items()}
    out["src_of_edge"] = edges["src"].reshape(P, EC)
    out["dst_of_edge"] = edges["dst"].reshape(P, EC)
    out["x"] = np.pad(inputs["x"], ((0, more_nodes), (0, 0)))
    for name in ("L0_gnn_W_rel", "L0_gnn_W_root"):
        out[name] = inputs[name].transpose(2, 0, 1).reshape(D, LAYERS * D)
    for name in ("L0_gnn_W1", "L0_gnn_W2", "L1_ffn_router_w"):
        out[name] = inputs[name].T
    for name in ("L0_gnn_b_rel", "L0_gnn_ln_g", "L0_gnn_ln_b", "L0_gnn_b1", "L0_gnn_mg1", "L0_gnn_mb1", "L0_gnn_b2",
                 "L0_gnn_mg2", "L0_gnn_mb2", "L0_ffn_router_b2", "L1_gnn_att_src", "L1_gnn_att_dst", "L1_gnn_bias"):
        out[name] = inputs[name].reshape(1, -1)
    out["L0_ffn_router_b1"] = inputs["L0_ffn_router_b1"].reshape(-1, 1)
    for name in ("L0_ffn_expert_b1", "L0_ffn_expert_b2", "L1_ffn_b1"):
        out[name] = inputs[name].reshape(-1, KD, P).transpose(2, 0, 1)
    for name in ("L0_ffn_router_w1", "L0_ffn_router_w2", "L0_ffn_expert_w1", "L0_ffn_expert_w2", "L0_ffn_expert_w3",
                 "L0_ffn_expert_b3", "L1_gnn_W", "L1_ffn_w1", "L1_ffn_w2", "L1_ffn_b2"):
        out[name] = inputs[name]
    return {name: np.ascontiguousarray(x) for name, x in out.items()}


def kernel(**inputs):
    import concourse.bacc as bacc
    import numpy as np
    from concourse.bass_utils import run_bass_kernel_spmd

    nc = bacc.Bacc("TRN2", target_bir_lowering=False, num_devices=1)
    arrays = lay_out({name: np.asarray(x) for name, x in inputs.items()})
    aps = {name: nc.dram_tensor(name, x.shape, mybir.dt.from_np(x.dtype), kind="ExternalInput").ap()
           for name, x in arrays.items()}
    aps["out"] = nc.dram_tensor("out", (NP, D), F32, kind="ExternalOutput").ap()
    program(nc, aps)
    result = run_bass_kernel_spmd(nc, [arrays], core_ids=[0])
    return result.results[0]["out"][:N]
```
